# Optimizing a Trainium2 kernel written in Bass

```python
import numpy as np
import jax
import jax.numpy as jnp

def _softmax(x, axis=-1):
    return jax.nn.softmax(x, axis=axis)

def _gelu(x):
    return jax.nn.gelu(x, approximate=True)

def _silu(x):
    return jax.nn.silu(x)

def _sigmoid(x):
    return jax.nn.sigmoid(x)

def _layernorm(x, axis=-1, eps=1e-05):
    m = jnp.mean(x, axis=axis, keepdims=True)
    v = jnp.var(x, axis=axis, keepdims=True)
    return (x - m) / jnp.sqrt(v + eps)

def _scatter_add(tgt, idx, src, axis=0):
    return tgt.at[idx].add(src)

def _segment_sum(src, seg, n):
    return jax.ops.segment_sum(src, seg, n)
kernel_name = 'mk_xattn_ffn_d1_seqx_r4_8bca31'

def setup_inputs(seed: int=0):
    np.random.seed(seed)
    _w = jnp.asarray

    def _rec_inputs():
        import jax
        import jax.numpy as jnp
        _rk = jax.random.key(seed)
        x = 7.22e-05 + 1 * jax.random.normal(jax.random.fold_in(_rk, 1), (8, 512, 256), jnp.float32)
        _lenS = 512 - jax.random.randint(jax.random.fold_in(_rk, 7), (8,), 0, max(1, 512 // 4) + 1, jnp.int32)
        _lenS2 = 1024 - jax.random.randint(jax.random.fold_in(_rk, 8), (8,), 0, max(1, 1024 // 4) + 1, jnp.int32)
        _ctx_1024P = jax.random.normal(jax.random.fold_in(_rk, 11), (8, 16, 256), jnp.float32)
        _ctx_1024c = jax.random.dirichlet(jax.random.fold_in(_rk, 511), 0.3 * jnp.ones((16,), jnp.float32), (8, 1024))
        _ctx_1024t = jnp.einsum('bsk,bkd->bsd', _ctx_1024c, _ctx_1024P)
        _ctx_1024t = _ctx_1024t * jax.lax.rsqrt(jnp.mean(jnp.square(_ctx_1024t)) + 1e-12) * 0.953939
        ctx_1024 = -5.15168e-05 + 0.999825 * (_ctx_1024t + 0.3 * jax.random.normal(jax.random.fold_in(_rk, 611), (8, 1024, 256), jnp.float32))
        return (x, ctx_1024)
    x, ctx_1024 = _rec_inputs()

    def _L0_xattn_setup():
        import jax, jax.numpy as jnp
        import numpy as np
        HEAD_DIM = 64
        D_MODEL = 256
        key = jax.random.key(seed)
        ks = jax.random.split(key, 6)
        B, S_NEW, S_CACHE, D = (4, 512, 1536, D_MODEL)
        w_scale = 1.0 / np.sqrt(D)
        return {'hidden_states': jax.random.normal(ks[0], (B, S_NEW, D), dtype=jnp.float32), 'cached_key': jax.random.normal(ks[1], (B, S_CACHE, D), dtype=jnp.float32), 'cached_value': jax.random.normal(ks[2], (B, S_CACHE, D), dtype=jnp.float32), 'Wq': jax.random.normal(ks[3], (D, D), dtype=jnp.float32) * w_scale, 'bq': jnp.zeros((D,), dtype=jnp.float32), 'Wk': jax.random.normal(ks[4], (D, D), dtype=jnp.float32) * w_scale, 'bk': jnp.zeros((D,), dtype=jnp.float32), 'Wv': jax.random.normal(ks[5], (D, D), dtype=jnp.float32) * w_scale, 'bv': jnp.zeros((D,), dtype=jnp.float32)}
    _L0_xattn_all = _L0_xattn_setup()
    _L0_xattn_in = {k: v for k, v in _L0_xattn_all.items() if k in ('Wq', 'bq', 'Wk', 'bk', 'Wv', 'bv')}
    del _L0_xattn_all

    def _L0_ffn_setup():
        import jax, jax.numpy as jnp
        import numpy as np
        E, D, F = (8, 256, 1024)
        LN_EPS = 1e-05
        key = jax.random.key(seed)
        k = jax.random.split(key, 8)
        x = jax.random.normal(k[0], (4, 512, D), jnp.float32)
        centroids = jax.random.normal(k[1], (E, D), jnp.float32) * 0.1
        ln_g = jnp.ones((E, D), jnp.float32)
        ln_b = jnp.zeros((E, D), jnp.float32)
        w1 = jax.random.normal(k[2], (E, F, D), jnp.float32) * (1.0 / np.sqrt(D))
        b1 = jnp.zeros((E, F), jnp.float32)
        w2 = jax.random.normal(k[3], (E, D, F), jnp.float32) * (1.0 / np.sqrt(F))
        b2 = jnp.zeros((E, D), jnp.float32)
        return {'input_features': x, 'centroids': centroids, 'ln_g': ln_g, 'ln_b': ln_b, 'w1': w1, 'b1': b1, 'w2': w2, 'b2': b2}
    _L0_ffn_all = _L0_ffn_setup()
    _L0_ffn_in = {k: v for k, v in _L0_ffn_all.items() if k in ('centroids', 'ln_g', 'ln_b', 'w1', 'b1', 'w2', 'b2')}
    del _L0_ffn_all
    return {'x': x, 'ctx_1024': ctx_1024, 'L0_xattn_Wq': _L0_xattn_in['Wq'], 'L0_xattn_bq': _L0_xattn_in['bq'], 'L0_xattn_Wk': _L0_xattn_in['Wk'], 'L0_xattn_bk': _L0_xattn_in['bk'], 'L0_xattn_Wv': _L0_xattn_in['Wv'], 'L0_xattn_bv': _L0_xattn_in['bv'], 'L0_ffn_centroids': _L0_ffn_in['centroids'], 'L0_ffn_ln_g': _L0_ffn_in['ln_g'], 'L0_ffn_ln_b': _L0_ffn_in['ln_b'], 'L0_ffn_w1': _L0_ffn_in['w1'], 'L0_ffn_b1': _L0_ffn_in['b1'], 'L0_ffn_w2': _L0_ffn_in['w2'], 'L0_ffn_b2': _L0_ffn_in['b2']}

def reference(x, ctx_1024, L0_xattn_Wq, L0_xattn_bq, L0_xattn_Wk, L0_xattn_bk, L0_xattn_Wv, L0_xattn_bv, L0_ffn_centroids, L0_ffn_ln_g, L0_ffn_ln_b, L0_ffn_w1, L0_ffn_b1, L0_ffn_w2, L0_ffn_b2):
    import jax
    import jax.numpy as jnp

    def _L0_xattn_ref(hidden_states, cached_key, cached_value, Wq, bq, Wk, bk, Wv, bv):
        import jax, jax.numpy as jnp
        import numpy as np
        HEAD_DIM = 64
        D_MODEL = 256
        q = jnp.einsum('bsd,ed->bse', hidden_states, Wq) + bq
        new_k = jnp.einsum('bsd,ed->bse', hidden_states, Wk) + bk
        new_v = jnp.einsum('bsd,ed->bse', hidden_states, Wv) + bv
        k = jnp.concatenate([cached_key, new_k], axis=1)
        v = jnp.concatenate([cached_value, new_v], axis=1)
        scale = 1.0 / jnp.sqrt(jnp.asarray(HEAD_DIM, dtype=q.dtype))
        scores = jnp.einsum('bqd,bkd->bqk', q, k) * scale
        probs = jax.nn.softmax(scores, axis=-1)
        out = jnp.einsum('bqk,bkd->bqd', probs, v)
        return out

    def _L0_ffn_ref(input_features, centroids, ln_g, ln_b, w1, b1, w2, b2):
        import jax, jax.numpy as jnp
        import numpy as np
        E, D, F = (8, 256, 1024)
        LN_EPS = 1e-05
        x = input_features.reshape(-1, D)
        aff = jax.lax.stop_gradient(x) @ centroids.T
        assign = jnp.argmax(aff, axis=1)
        onehot = jax.nn.one_hot(assign, E, dtype=x.dtype)
        mu = jnp.mean(x, axis=-1, keepdims=True)
        var = jnp.mean((x - mu) ** 2, axis=-1, keepdims=True)
        xhat = (x - mu) * jax.lax.rsqrt(var + LN_EPS)
        xn = xhat[None, :, :] * ln_g[:, None, :] + ln_b[:, None, :]
        h = jax.nn.relu(jnp.einsum('etd,efd->etf', xn, w1) + b1[:, None, :])
        y = x[None, :, :] + jnp.einsum('etf,edf->etd', h, w2) + b2[:, None, :]
        alpha = jax.nn.sigmoid(x @ centroids.T)
        a = alpha.T[:, :, None]
        gated = a * y + (1.0 - a) * x[None, :, :]
        out = jnp.einsum('te,etd->td', onehot, gated)
        return out.reshape(input_features.shape)
    x = x + _L0_xattn_ref(_layernorm(x, axis=-1), ctx_1024, ctx_1024, L0_xattn_Wq, L0_xattn_bq, L0_xattn_Wk, L0_xattn_bk, L0_xattn_Wv, L0_xattn_bv)
    x = x + _L0_ffn_ref(_layernorm(x, axis=-1), L0_ffn_centroids, L0_ffn_ln_g, L0_ffn_ln_b, L0_ffn_w1, L0_ffn_b1, L0_ffn_w2, L0_ffn_b2)
    return x

_drawn_inputs = setup_inputs


def setup_inputs(seed=0):
    import zlib

    import numpy as np

    out = dict(_drawn_inputs(seed))
    spreads = {'L0_xattn_bq': (0.0, 0.1),
     'L0_xattn_bk': (0.0, 0.1),
     'L0_xattn_bv': (0.0, 0.1),
     'L0_ffn_ln_g': (1.0, 0.2),
     'L0_ffn_ln_b': (0.0, 0.285),
     'L0_ffn_b1': (0.0, 0.281),
     'L0_ffn_b2': (0.0, 0.1)}
    factors = {}
    for name, (base, spread) in spreads.items():
        noise = np.random.default_rng([zlib.crc32(name.encode()), seed]).standard_normal(out[name].shape)
        drawn = base * np.exp(spread * noise) if base else spread * noise
        out[name] = jnp.asarray(drawn.astype(out[name].dtype))
    for name, factor in factors.items():
        out[name] = (out[name] * factor).astype(out[name].dtype)
    return out
```

```python
from contextlib import ExitStack

import concourse.bass as bass
from concourse import mybir

P = 128
B, S, D = 8, 512, 256
K_CTX = 1024
KEYS = K_CTX + S
DC = D // P
QT = S // P
KC = KEYS // P
CC = K_CTX // P
BANK = 512
KB = KEYS // BANK
GPB = BANK // P
TOKENS = B * S
E, F = 8, 1024
FC = F // P
TILE = 256
HALVES = TILE // P
TILES = TOKENS // TILE + E - 1
RANKS = TOKENS // P
MAXT = TOKENS // TILE
META = TILES + 2
ROW = 2 * D + 4
NO_TOKEN = 2 * TOKENS
LN_EPS = 1e-5
SCALE = 64 ** -0.5

ALU = mybir.AluOpType
ACT = mybir.ActivationFunctionType
AX = mybir.AxisListType
F32 = mybir.dt.float32
F32R = mybir.dt.float32r
BF16 = mybir.dt.bfloat16
I32 = mybir.dt.int32
U32 = mybir.dt.uint32

QKV_ORDER = ("q0", "q1", "k0", "k1", "v0", "v1")
NPROJ = len(QKV_ORDER)
NPIECE = 4


class Steps:

    def __init__(self, sem, per):
        self.sem, self.per = sem, per

    def begin(self, b):
        self.b, self.n = b, 0

    def __call__(self, eng, ins):
        self.n += 1
        assert self.n <= self.per
        ins.then_inc(self.sem, 1)
        eng.wait_ge(self.sem, self.b * self.per + self.n)

    def done(self, b):
        return (b + 1) * self.per


def wait(eng, sem, value):
    if not isinstance(value, int) or value > 0:
        eng.wait_ge(sem, value)


def settle(eng, sem):
    eng.sem_inc(sem, 1)


def xattn_experts(nc, x, keys_src, vals_src, wq, wk, wv, b_cols, bv, cent, vecs, b2, out):
    rows = nc.dram_tensor("rows", [TOKENS, ROW], F32, kind="Internal").ap()

    ctx = ExitStack()
    with ctx:
        def sb(name, shape, dt=F32):
            return ctx.enter_context(nc.sbuf_tensor(name, shape, dt))

        def sem(name):
            return ctx.enter_context(nc.semaphore(name))

        ps_s = ctx.enter_context(nc.psum_tensor("ps_s", [P, KB, BANK], F32))
        ps_a, ps_b, ps_pv, ps_ma, ps_mb = [
            ctx.enter_context(nc.psum_tensor(n, [P, BANK], F32))
            for n in ("ps_a", "ps_b", "ps_pv", "ps_ma", "ps_mb")]

        ident = sb("ident", [P, P])
        ident_in = sb("ident_in", [P, P])
        tri = sb("tri", [P, P], BF16)
        ones = sb("ones", [P, P], BF16)
        iota_f = sb("iota_f", [P, P])
        iota_e = sb("iota_e", [P, QT, E])
        iota_r = sb("iota_r", [P, QT, RANKS])
        part1 = sb("part1", [P, 1])
        tile_no = sb("tile_no", [P, QT, E])
        thr = sb("thr", [P, E, MAXT])
        upto = sb("upto", [P, E, E])
        upto_in = sb("upto_in", [P, E, E])
        tile_j = sb("tile_j", [P, META, E - 1])
        w_hi = sb("w_hi", [P, 3, DC, D], F32R)
        w_lo = sb("w_lo", [P, 3, DC, D], F32R)
        bqk = sb("bqk", [P, 2, DC])
        bv_all = sb("bv_all", [P, D])
        cent_sb = sb("cent_sb", [P, DC, E])
        eps = sb("eps", [P, 1])

        k_raw = sb("k_raw", [P, DC, K_CTX])
        v_raw = sb("v_raw", [P, CC, D])
        k_hi = [sb(f"k_hi{i}", [P, DC, K_CTX], F32R) for i in range(2)]
        k_lo = [sb(f"k_lo{i}", [P, DC, K_CTX], F32R) for i in range(2)]
        v_hi = [sb(f"v_hi{i}", [P, CC, D], F32R) for i in range(2)]
        v_lo = [sb(f"v_lo{i}", [P, CC, D], F32R) for i in range(2)]
        kn_hi = sb("kn_hi", [P, DC, S], F32R)
        kn_lo = sb("kn_lo", [P, DC, S], F32R)
        vn_hi = [sb(f"vn_hi{i}", [P, QT, D], F32R) for i in range(2)]
        vn_lo = [sb(f"vn_lo{i}", [P, QT, D], F32R) for i in range(2)]
        vn_f = sb("vn_f", [P, 2, D])
        q_hi = sb("q_hi", [P, DC, S], F32R)
        q_lo = sb("q_lo", [P, DC, S], F32R)
        x_both = sb("x_both", [P, 2 * QT, D])
        x_sb = [x_both[:, i * QT:(i + 1) * QT] for i in range(2)]
        xn = sb("xn", [P, QT, D])
        xt_hi = sb("xt_hi", [P, DC, S], F32R)
        xt_lo = sb("xt_lo", [P, DC, S], F32R)
        probs = sb("probs", [P, KEYS])
        w_raw = probs[:].rearrange("p (a c d) -> p a c d", a=3, c=DC)
        pt_hi = sb("pt_hi", [P, KC, P], F32R)
        pt_lo = sb("pt_lo", [P, KC, P], F32R)
        x1 = [sb(f"x1_{i}", [P, QT, D]) for i in range(2)]
        mx3 = sb("mx3", [P, KB])
        mx1 = sb("mx1", [P, 1])
        neg_max = sb("neg_max", [P, 1])
        sums = sb("sums", [P, 2, QT])
        rsum = sb("rsum", [P, 1])

        st = [sb(f"st{i}", [P, QT, 6]) for i in range(3)]
        mv = [sb(f"mv{i}", [P, QT, 2]) for i in range(3)]
        ve = [sb(f"ve{i}", [P, QT]) for i in range(3)]
        lnv = [sb(f"lnv{i}", [P, QT]) for i in range(3)]
        y0 = [sb(f"y0{i}", [P, QT]) for i in range(3)]
        ysq = [sb(f"ysq{i}", [P, QT]) for i in range(3)]
        rstd = [sb(f"rstd{i}", [P, QT]) for i in range(3)]
        h_sb = sb("h_sb", [P, QT, D])
        ht = sb("ht", [P, DC, S])
        row_sb = sb("row_sb", [P, QT, ROW])
        aff = sb("aff", [P, QT, E])
        top = sb("top", [P, QT, 8])
        top_i = sb("top_i", [P, QT, 8], U32)
        top_f = sb("top_f", [P, QT])
        ea = sb("ea", [P, QT])
        ea1 = sb("ea1", [P, QT])
        hot = sb("hot", [P, QT, E], BF16)
        hot_sum = sb("hot_sum", [P, E])
        acc = sb("acc", [P, E], BF16)
        rank_e = sb("rank_e", [P, QT, E])
        rank_f = sb("rank_f", [P, QT])
        rank_i = sb("rank_i", [P, QT], I32)
        lohi_i = sb("lohi_i", [P, 2, QT], I32)
        lohi = sb("lohi", [P, 2, QT])
        lo_hot = sb("lo_hot", [P, QT, P], BF16)
        hi_hot = sb("hi_hot", [P, QT, RANKS], BF16)
        hot_id = sb("hot_id", [P, QT, 2, E], BF16)
        put = sb("put", [P, QT, 2, E, RANKS], BF16)
        table = sb("table", [P, 2, E * RANKS])
        ids_f, empty = ht[:, 0, 0:E * RANKS], ht[:, 0, E * RANKS:2 * E * RANKS]
        ids = sb("ids", [P, E * RANKS], I32)
        cnt = sb("cnt", [P, E])
        over = sb("over", [P, E, MAXT])
        tl = sb("tl", [P, E])
        tl1 = sb("tl1", [P, E])
        tlu = sb("tlu", [P, E, E])
        ends = sb("ends", [P, E])
        past = sb("past", [P, META, E - 1])
        past_t = sb("past_t", [P, META, E - 1])
        eid_f = sb("eid_f", [P, META])
        start_f = sb("start_f", [P, META])
        meta_f = sb("meta_f", [P, 2, META])
        meta = sb("meta", [P, 2, META], I32)

        w1_raw, w2_raw = k_raw, v_raw
        w1_hi, w1_lo, w2_hi, w2_lo = k_hi[0], k_lo[0], v_hi[0], v_lo[0]
        h1_hi, h1_lo = v_hi[1], v_lo[1]
        tok_out = sb("tok_out", [P, HALVES], I32)
        tok = [sb(f"tok{i}", [P, HALVES], I32) for i in range(2)]
        g = [row_sb[:, i * HALVES:(i + 1) * HALVES] for i in range(2)]
        vec = [sb(f"vec{i}", [P, 2 * DC + FC]) for i in range(2)]
        b2_all = [ht[:, 1, i * D:(i + 1) * D] for i in range(2)]
        xe, y_b = xn[:, 0:DC], xn[:, DC:DC + HALVES]
        xe_hi, xe_lo = xt_hi[:, :, 0:TILE], xt_lo[:, :, 0:TILE]
        h1 = x_both
        o_sb = h_sb[:, 0:HALVES]

        const_in, x_in, k_in, v_in, rows_out = map(sem, ("const_in", "x_in", "k_in", "v_in", "rows_out"))
        made, made2, w_hi_ok, w_lo_ok = map(sem, ("made", "made2", "w_hi_ok", "w_lo_ok"))
        scored, p_turned, pv_done, x_turned, projected = map(
            sem, ("scored", "p_turned", "pv_done", "x_turned", "projected"))
        h_turned, aff_ps, rank_ps, table_ps, cnt_ps = map(
            sem, ("h_turned", "aff_ps", "rank_ps", "table_ps", "cnt_ps"))
        exp_done, pt_hi_ok, xt_hi_ok, proj_hi_ok, ctx_hi_ok, ht_ok, gate_exp = map(
            sem, ("exp_done", "pt_hi_ok", "xt_hi_ok", "proj_hi_ok", "ctx_hi_ok", "ht_ok", "gate_exp"))
        ln_act = [sem(f"ln_act{i}") for i in range(3)]
        max_ok, pt_lo_ok, x1_ok, xt_lo_ok, proj_lo_ok, v_sum_ok = map(
            sem, ("max_ok", "pt_lo_ok", "x1_ok", "xt_lo_ok", "proj_lo_ok", "v_sum_ok"))
        var_ok = [sem(f"var_ok{i}") for i in range(3)]
        max_step = Steps(sem("max_step"), QT)
        ln_step = [Steps(sem(f"ln_step{i}"), 2) for i in range(3)]
        rstd_step = [Steps(sem(f"rstd_step{i}"), 4) for i in range(3)]
        top_step = Steps(sem("top_step"), 5)
        rank_step = Steps(sem("rank_step"), 6)
        hot_ok, gate_ok, id_ok, lo_hot_ok, table_ok, sum_step, rsum_ok = map(
            sem, ("hot_ok", "gate_ok", "id_ok", "lo_hot_ok", "table_ok", "sum_step", "rsum_ok"))
        meta_ok, ids_ok, meta_step, max_a, gate_step, settled = map(sem, ("meta_ok", "ids_ok", "meta_step", "max_a", "gate_step", "settled"))
        norm_ok, tok_out_ok = sem("norm_ok"), sem("tok_out_ok")
        ctx_lo_ok, xn_ok, h_ok, row_ok, put_ok = map(sem, ("ctx_lo_ok", "xn_ok", "h_ok", "row_ok", "put_ok"))
        w1_in, w2_in, tok_ok, stored0, fed, mm1_ok, mm2_ok, xe_turned = map(
            sem, ("w1_in", "w2_in", "tok_ok", "stored0", "fed", "mm1_ok", "mm2_ok", "xe_turned"))
        gathered = [[sem(f"gathered{i}{k}") for k in range(HALVES)] for i in range(2)]
        vec_in = [sem(f"vec_in{i}") for i in range(2)]
        stored = [sem(f"stored{k}_") for k in range(HALVES)]
        xe_ok, xe_hi_ok, xe_lo_ok, h1_ok, h1_hi_ok, h1_lo_ok = map(
            sem, ("xe_ok", "xe_hi_ok", "xe_lo_ok", "h1_ok", "h1_hi_ok", "h1_lo_ok"))
        w1_hi_ok, w2_hi_ok, w1_lo_v, w2_lo_v, w1_lo_p, w2_lo_p, y_read, o_ok = map(
            sem, ("w1_hi_ok", "w2_hi_ok", "w1_lo_v", "w2_lo_v", "w1_lo_p", "w2_lo_p", "y_read", "o_ok"))

        def batches(eng, body):
            body(0, 0)
            with eng.Fori(0, (B - 2) // 2) as i:
                body(2 * i + 1, 1)
                body(2 * i + 2, 0)
            body(B - 1, (B - 1) % 2)

        def tiles(eng, body):
            body(0, 0)
            with eng.Fori(0, (TILES - 1) // 2) as i:
                body(2 * i + 1, 1)
                body(2 * i + 2, 0)

        def h_bank(n):
            return ps_s[:, n] if n < KB else ps_a[:]

        def vec_value(j, par):
            return (j - par) * 16 + 32

        def is_last(b):
            return isinstance(b, int) and b == B - 1

        block = ctx.enter_context(nc.Block())

        @block.sync
        def _(sp):
            def load_ctx(n):
                wait(sp, ctx_hi_ok, NPIECE * n)
                wait(sp, ctx_lo_ok, NPIECE * n)
                sp.dma_start(k_raw[:], keys_src[bass.ds(n, 1)].rearrange("o (c p) k -> p (o c) k", p=P)).then_inc(k_in, 16)
                sp.dma_start(v_raw[:], vals_src[bass.ds(n, 1)].rearrange("o (c p) d -> p (o c) d", p=P)).then_inc(v_in, 16)

            def load_x(n, par):
                wait(sp, x1_ok, QT * (n - 1))
                wait(sp, var_ok[0], n - 1)
                sp.dma_start(x_sb[par], x[bass.ds(n, 1)].rearrange("o (t p) d -> p (o t) d", p=P)).then_inc(x_in, 16)

            sp.dma_start(x_sb[0], x[0:1].rearrange("o (t p) d -> p (o t) d", p=P)).then_inc(x_in, 16)
            for n, w in enumerate((wq, wk, wv)):
                sp.dma_start(w_raw[:, n], w.rearrange("(c p) d -> p c d", p=P)).then_inc(const_in, 16)
            sp.dma_start(bqk[:], b_cols).then_inc(const_in, 16)
            sp.dma_start(bv_all[:], bv.rearrange("(o d) -> o d", o=1).broadcast_to([P, D])).then_inc(const_in, 16)
            sp.dma_start(cent_sb[:], cent.rearrange("(c p) e -> p c e", p=P)).then_inc(const_in, 16)
            load_ctx(0)
            load_ctx(1)

            def store_rows(b):
                wait(sp, row_ok, b + 1)
                wait(sp, norm_ok, b + 1)
                wait(sp, gate_ok, b + 1)
                sp.dma_start(rows[bass.ds(b * S, S)].rearrange("(t p) w -> p t w", p=P), row_sb[:]).then_inc(rows_out, 16)

            def body(b, par):
                if not is_last(b):
                    load_x(b + 1, 1 - par)
                if not isinstance(b, int) or b > 0:
                    store_rows(b - 1)
                if not is_last(b):
                    load_ctx(b + 2)

            batches(sp, body)
            store_rows(B - 1)

            def expert(j):
                settle(sp, settled)
                return sp.value_load(meta[0:1, 0, bass.ds(j, 1)], min_val=0, max_val=E - 1)

            def load_w1(j):
                wait(sp, w1_hi_ok, 2 * (j - 1))
                wait(sp, w1_lo_v, j - 1)
                wait(sp, w1_lo_p, j - 1)
                sp.dma_start(w1_raw[:], keys_src[bass.ds(expert(j) + B, 1)].rearrange("o (c p) k -> p (o c) k", p=P)).then_inc(w1_in, 16)

            def load_w2(j):
                wait(sp, w2_hi_ok, 2 * (j - 1))
                wait(sp, w2_lo_v, j - 1)
                wait(sp, w2_lo_p, j - 1)
                sp.dma_start(w2_raw[:], vals_src[bass.ds(expert(j) + B, 1)].rearrange("o (c p) k -> p (o c) k", p=P)).then_inc(w2_in, 16)

            def load_vec(j, par):
                wait(sp, o_ok, 2 * (j - 1))
                e = expert(j)
                sp.dma_start(vec[par][:], vecs[bass.ds(e, 1)].rearrange("o p n -> (o p) n")).then_inc(vec_in[par], 16)
                sp.dma_start(b2_all[par], b2[bass.ds(e, 1)].broadcast_to([P, D])).then_inc(vec_in[par], 16)

            sp.wait_ge(meta_ok, 1)
            sp.wait_ge(ctx_hi_ok, NPIECE * (B + 1))
            sp.wait_ge(ctx_lo_ok, NPIECE * (B + 1))
            load_vec(0, 0)
            load_w1(1)
            load_w2(1)

            def tile_body(j, par):
                load_vec(j + 1, 1 - par)
                if not isinstance(j, int) or j > 0:
                    load_w2(j + 1)
                load_w1(j + 2)

            tiles(sp, tile_body)
            sp.wait_ge(rows_out, 16 * B)
            for k in range(HALVES):
                sp.wait_ge(stored[k], 16 * TILES)
            sp.wait_ge(w1_in, 16 * (TILES + 1))
            sp.wait_ge(w2_in, 16 * TILES)

        @block.gpsimd
        def _(pool):
            pool.memset(ident_in[:], 0.0).then_inc(made, 1)
            pool.memset(upto_in[:], 1.0).then_inc(made, 1)
            pool.memset(ones[:], 1.0).then_inc(made, 1)
            pool.memset(eps[:], LN_EPS).then_inc(made, 1)
            pool.memset(acc[:], 0.0).then_inc(made, 1)
            pool.memset(table[:], 0.0).then_inc(made, 1)
            pool.memset(row_sb[:], 0.0).then_inc(made, 1)
            kw = dict(allow_small_or_imprecise_dtypes=True)
            pool.iota(iota_f[:], pattern=[[1, P]], base=0, channel_multiplier=0, **kw).then_inc(made, 1)
            pool.iota(iota_e[:], pattern=[[0, QT], [1, E]], base=0, channel_multiplier=0, **kw).then_inc(made, 1)
            pool.iota(iota_r[:], pattern=[[0, QT], [1, RANKS]], base=0, channel_multiplier=0, **kw).then_inc(made, 1)
            pool.iota(part1[:], pattern=[[1, 1]], base=1, channel_multiplier=1, **kw).then_inc(made, 1)
            pool.iota(tile_no[:], pattern=[[1, QT], [0, E]], base=0, channel_multiplier=0, **kw).then_inc(made, 1)
            pool.iota(thr[:], pattern=[[0, E], [TILE, MAXT]], base=0, channel_multiplier=0, **kw).then_inc(made, 1)
            pool.iota(tile_j[:], pattern=[[1, META], [0, E - 1]], base=0, channel_multiplier=0, **kw).then_inc(made, 1)
            pool.wait_ge(made, 14)
            pool.affine_select(out=ident[:], in_=ident_in[:], compare_op=ALU.not_equal, fill=1.0,
                               base=0, pattern=[[-1, P]], channel_multiplier=1).then_inc(made2, 1)
            pool.affine_select(out=tri[:], in_=ones[:], compare_op=ALU.is_gt, fill=0.0,
                               base=0, pattern=[[1, P]], channel_multiplier=-1).then_inc(made2, 1)
            pool.affine_select(out=upto[:], in_=upto_in[:], compare_op=ALU.is_ge, fill=0.0,
                               base=0, pattern=[[1, E], [-1, E]], channel_multiplier=0).then_inc(made2, 1)

            def ctx_lo(n, par, piece):
                wait(pool, ctx_hi_ok, NPIECE * n + piece + 1)
                if piece < 2:
                    args = k_lo[par][:, piece], k_raw[:, piece], k_hi[par][:, piece].bitcast(F32)
                else:
                    c = slice((piece - 2) * 4, (piece - 2) * 4 + 4)
                    args = v_lo[par][:, c], v_raw[:, c], v_hi[par][:, c].bitcast(F32)
                pool.tensor_tensor(*args, ALU.subtract).then_inc(ctx_lo_ok, 1)

            for piece in range(NPIECE):
                ctx_lo(0, 0, piece)

            def body(b, par):
                later = not isinstance(b, int) or b > 0
                ctx_lo(b + 1, 1 - par, 0)
                if later:
                    residual(b - 1, 1 - par)
                ctx_lo(b + 1, 1 - par, 1)
                ctx_lo(b + 1, 1 - par, 2)
                if later:
                    put_ids(b - 1)
                ctx_lo(b + 1, 1 - par, 3)

            def residual(b, par):
                wait(pool, h_ok, b + 1)
                wait(pool, rows_out, 16 * b)
                pool.tensor_tensor(row_sb[:, :, D:2 * D], x1[par][:], h_sb[:], ALU.add).then_inc(row_ok, 1)

            def put_ids(b):
                wait(pool, id_ok, b + 1)
                wait(pool, table_ps, b)
                for t in range(QT):
                    ins = pool.tensor_tensor(
                        put[:, t], hot_id[:, t, :, :, None].broadcast_to([P, 2, E, RANKS]),
                        hi_hot[:, t, None, None, :].broadcast_to([P, 2, E, RANKS]), ALU.mult)
                ins.then_inc(put_ok, 1)

            batches(pool, body)
            residual(B - 1, (B - 1) % 2)
            put_ids(B - 1)

            pool.wait_ge(ids_ok, 1)
            pool.wait_ge(meta_ok, 1)
            pool.wait_ge(rows_out, 16 * B)

            def gather(j, par):
                col = pool.value_load(meta[0:1, 1, bass.ds(j, 1)], min_val=0, max_val=E * RANKS - HALVES)
                wait(pool, o_ok, 2 * (j - 1))
                settle(pool, settled)
                if not isinstance(j, int) or j > 1:
                    for k in range(HALVES):
                        wait(pool, gathered[par][k], 8 * (j - par))
                pool.tensor_copy(tok[par][:], ids[:, bass.ds(col, HALVES)]).then_inc(tok_ok, 1)
                pool.wait_ge(tok_ok, j + 1)
                settle(pool, settled)
                for k in range(HALVES):
                    pool.indirect_dma_start(
                        out=g[par][:, k, :], out_offset=None, in_=rows[:, :],
                        in_offset=bass.IndirectOffsetOnAxis(ap=tok[par][:, k:k + 1], axis=0),
                        bounds_check=TOKENS - 1, oob_is_err=False).then_inc(gathered[par][k], 16)

            def scatter(j):
                col = pool.value_load(meta[0:1, 1, bass.ds(j, 1)], min_val=0, max_val=E * RANKS - HALVES)
                for k in range(HALVES):
                    wait(pool, stored[k], 16 * j)
                pool.tensor_copy(tok_out[:], ids[:, bass.ds(col, HALVES)]).then_inc(tok_out_ok, 1)
                wait(pool, tok_out_ok, j + 1)
                wait(pool, o_ok, 2 * (j + 1))
                settle(pool, settled)
                for k in range(HALVES):
                    pool.indirect_dma_start(
                        out=out[:, :], out_offset=bass.IndirectOffsetOnAxis(ap=tok_out[:, k:k + 1], axis=0),
                        in_=o_sb[:, k, :], in_offset=None,
                        bounds_check=TOKENS - 1, oob_is_err=False).then_inc(stored[k], 16)

            gather(0, 0)

            def tile_body(j, par):
                gather(j + 1, 1 - par)
                if not isinstance(j, int) or j > 0:
                    wait(pool, w2_hi_ok, 2 * j)
                    pool.tensor_tensor(w2_lo[:, FC // 2:], w2_raw[:, FC // 2:], w2_hi[:, FC // 2:].bitcast(F32),
                                       ALU.subtract).then_inc(w2_lo_p, 1)
                    scatter(j - 1)
                wait(pool, w1_hi_ok, 2 * (j + 1))
                pool.tensor_tensor(w1_lo[:, 1], w1_raw[:, 1], w1_hi[:, 1].bitcast(F32),
                                   ALU.subtract).then_inc(w1_lo_p, 1)

            tiles(pool, tile_body)
            scatter(TILES - 1)
            for k in range(HALVES):
                pool.wait_ge(gathered[TILES % 2][k], 16 * ((TILES + 1 + (1 - TILES % 2)) // 2))

        @block.scalar
        def _(act):
            act.preload_act_table_set("natural_log_exp_and_others")
            act.wait_ge(const_in, 16 * 6)
            act.activation(w_hi[:], w_raw, ACT.Copy).then_inc(w_hi_ok, 1)

            def ln(kind, b):
                wait(act, var_ok[kind], b + 1)
                act.activation(lnv[kind][:], ve[kind][:], ACT.Ln).then_inc(ln_act[kind], 1)
                act.wait_ge(ln_act[kind], 2 * b + 1)
                act.activation(y0[kind][:], lnv[kind][:], ACT.Exp, scale=-0.5).then_inc(ln_act[kind], 1)

            def ctx_hi(n, par, piece):
                if piece == 0:
                    wait(act, k_in, 16 * (n + 1))
                    wait(act, scored, KB * QT * (n - 1))
                if piece == 2:
                    wait(act, v_in, 16 * (n + 1))
                    wait(act, pv_done, QT * (n - 1))
                if piece < 2:
                    args = k_hi[par][:, piece], k_raw[:, piece]
                else:
                    c = slice((piece - 2) * 4, (piece - 2) * 4 + 4)
                    args = v_hi[par][:, c], v_raw[:, c]
                act.activation(*args, ACT.Copy).then_inc(ctx_hi_ok, 1)

            def turned_x(n, c):
                wait(act, x_turned, DC * n + c + 1)
                wait(act, projected, NPROJ * n)
                act.activation(xt_hi[:, c], ps_mb[:], ACT.Copy).then_inc(xt_hi_ok, 1)

            def proj_hi(n, par, m):
                name, c = QKV_ORDER[m][0], int(QKV_ORDER[m][1])
                if name == "v":
                    wait(act, v_sum_ok, 2 * n + c + 1)
                    if c == 0:
                        wait(act, pv_done, QT * (n - 1))
                    act.activation(vn_hi[par][:, 2 * c:2 * c + 2], vn_f[:], ACT.Copy).then_inc(proj_hi_ok, 1)
                    return
                wait(act, projected, NPROJ * n + m + 1)
                if m == 0:
                    wait(act, scored, KB * QT * n)
                bank = {"q0": ps_mb, "q1": ps_ma, "k0": ps_a, "k1": ps_b}[QKV_ORDER[m]]
                dst, bias = (q_hi, 0) if name == "q" else (kn_hi, 1)
                act.activation(dst[:, c], bank[:], ACT.Identity, bias=bqk[:, bias, c:c + 1]).then_inc(proj_hi_ok, 1)

            def exps(b, par, t):
                wait(act, max_ok, QT * b + t + 1)
                wait(act, p_turned, KB * (QT * b + t))
                act.activation(probs[:], ps_s[:].rearrange("p a n -> p (a n)"), ACT.Exp, bias=neg_max[:, 0:1],
                               scale=SCALE, accum_out=sums[:, par, t:t + 1]).then_inc(exp_done, 1)

            def p_hi(b, t, n, bank):
                wait(act, p_turned, KB * (QT * b + t) + n + 1)
                if n == 0:
                    wait(act, pv_done, QT * b + t)
                act.activation(pt_hi[:, GPB * n:GPB * n + GPB], bank[:].rearrange("p (g q) -> p g q", g=GPB),
                               ACT.Copy).then_inc(pt_hi_ok, 1)

            ln(0, 0)
            for piece in range(NPIECE):
                ctx_hi(0, 0, piece)
            turned_x(0, 0)
            turned_x(0, 1)
            for m in range(NPROJ):
                proj_hi(0, 0, m)
            exps(0, 0, 0)

            def turned_h(b, c):
                wait(act, h_turned, DC * b + c + 1)
                wait(act, aff_ps, b)
                act.activation(ht[:, c], (ps_ma, ps_mb)[c][:], ACT.Copy).then_inc(ht_ok, 1)

            def gate(b):
                wait(act, top_step.sem, top_step.per * b + 2)
                act.activation(ea[:], top[:, :, 0], ACT.Exp, scale=-1.0).then_inc(gate_exp, 1)

            def body(b, par):
                later = not isinstance(b, int) or b > 0
                for t in range(1, QT):
                    for n in range(KB):
                        p_hi(b, t - 1, n, (ps_a, ps_b, ps_a)[n])
                    ctx_hi(b + 1, 1 - par, t - 1)
                    if later and t == 1:
                        ln(1, b - 1)
                    if later and t == 2:
                        ln(2, b - 1)
                    if not is_last(b) and t == 2:
                        ln(0, b + 1)
                    if later and t == 3:
                        gate(b - 1)
                    if not is_last(b) and t == 3:
                        turned_x(b + 1, 0)
                    exps(b, par, t)
                    if later and t == 1:
                        turned_h(b - 1, 0)
                        turned_h(b - 1, 1)
                if not is_last(b):
                    turned_x(b + 1, 1)
                    for m in range(4):
                        proj_hi(b + 1, 1 - par, m)
                    ctx_hi(b + 1, 1 - par, 3)
                    proj_hi(b + 1, 1 - par, 4)
                    p_hi(b, 3, 0, ps_a)
                    p_hi(b, 3, 1, ps_b)
                    proj_hi(b + 1, 1 - par, 5)
                    p_hi(b, 3, 2, ps_a)
                    exps(b + 1, 1 - par, 0)
                else:
                    p_hi(b, 3, 0, ps_a)
                    p_hi(b, 3, 1, ps_b)
                    p_hi(b, 3, 2, ps_a)
                    ctx_hi(b + 1, 1 - par, 3)

            batches(act, body)
            ln(1, B - 1)
            turned_h(B - 1, 0)
            turned_h(B - 1, 1)
            gate(B - 1)
            ln(2, B - 1)

            def expert_x(j, par):
                wait(act, xe_turned, j + 1)
                wait(act, vec_in[par], vec_value(j, par))
                wait(act, xe_hi_ok, j)
                wait(act, xe_lo_ok, j)
                for c in range(DC):
                    act.activation(xe[:, c], ps_mb[:, c * TILE:(c + 1) * TILE], ACT.Identity,
                                   bias=vec[par][:, DC + c:DC + c + 1], scale=vec[par][:, c:c + 1]).then_inc(xe_ok, 1)

            expert_x(0, 0)

            def w2_part(j, n):
                wait(act, w2_in, 16 * j)
                if n == 0:
                    wait(act, mm2_ok, HALVES * j)
                c = slice(n * FC // 2, (n + 1) * FC // 2)
                act.activation(w2_hi[:, c], w2_raw[:, c], ACT.Copy).then_inc(w2_hi_ok, 1)

            def relu(j, par, f):
                if f % 2 == 0:
                    wait(act, mm1_ok, FC // 2 * j + f // 2 + 1)
                    wait(act, h1_lo_ok, FC // 2 * (j - 1) + f // 2 + 1)
                bank = h_bank(f // 2)
                act.activation(h1[:, f], bank[:, (f % 2) * TILE:(f % 2 + 1) * TILE], ACT.Relu,
                               bias=vec[par][:, 2 * DC + f:2 * DC + f + 1]).then_inc(h1_ok, 1)

            def w1_part(j, n):
                wait(act, w1_in, 16 * j)
                if n == 0:
                    wait(act, mm1_ok, FC // 2 * j)
                act.activation(w1_hi[:, n], w1_raw[:, n], ACT.Copy).then_inc(w1_hi_ok, 1)

            def tile_body(j, par):
                if not isinstance(j, int) or j > 0:
                    w2_part(j, 0)
                    w2_part(j, 1)
                for f in range(FC):
                    relu(j, par, f)
                w1_part(j + 1, 0)
                expert_x(j + 1, 1 - par)
                w1_part(j + 1, 1)

            tiles(act, tile_body)

        @block.vector
        def _(dve):
            def stats(kind, b, t, src):
                return dve.bn_stats(st[kind][:, t], src)

            def variance(kind, b, par, src):
                ln_step[kind].begin(b)
                for t in range(QT):
                    ins = dve.bn_stats(st[kind][:, t], src(t))
                ln_step[kind](dve, ins)
                settle(dve, settled)
                for t in range(QT):
                    ins = dve.bn_aggr(mv[kind][:, t], st[kind][:, t])
                ln_step[kind](dve, ins)
                dve.tensor_scalar(ve[kind][:], mv[kind][:, :, 1], LN_EPS, None, ALU.add).then_inc(var_ok[kind], 1)

            def refine(kind, b):
                s = rstd_step[kind]
                s.begin(b)
                wait(dve, ln_act[kind], 2 * b + 2)
                s(dve, dve.tensor_tensor(ysq[kind][:], y0[kind][:], y0[kind][:], ALU.mult))
                s(dve, dve.tensor_tensor(ysq[kind][:], ysq[kind][:], ve[kind][:], ALU.mult))
                s(dve, dve.tensor_scalar(ysq[kind][:], ysq[kind][:], -0.5, 1.5, ALU.mult, ALU.add))
                s(dve, dve.tensor_tensor(rstd[kind][:], y0[kind][:], ysq[kind][:], ALU.mult))

            def norm(kind, src, dst, done):
                for t in range(QT):
                    ins = dve.tensor_scalar(dst(t), src(t), mv[kind][:, t, 0:1], rstd[kind][:, t:t + 1],
                                            ALU.subtract, ALU.mult)
                ins.then_inc(done, 1)

            def ln1(n, par):
                refine(0, n)
                wait(dve, x_turned, DC * n)
                norm(0, lambda t: x_sb[par][:, t], lambda t: xn[:, t], xn_ok)

            def ln2(b, par):
                refine(1, b)
                wait(dve, h_turned, DC * b)
                wait(dve, row_ok, b)
                norm(1, lambda t: x1[par][:, t], lambda t: h_sb[:, t], h_ok)

            def ln3(b):
                refine(2, b)
                wait(dve, rows_out, 16 * b)
                norm(2, lambda t: h_sb[:, t], lambda t: row_sb[:, t, 0:D], norm_ok)

            def turned_x(n, c):
                wait(dve, xt_hi_ok, DC * n + c + 1)
                dve.tensor_tensor(xt_lo[:, c], ps_mb[:], xt_hi[:, c].bitcast(F32), ALU.subtract).then_inc(xt_lo_ok, 1)

            def proj_sum(n, c):
                wait(dve, projected, NPROJ * n + 4 + c + 1)
                wait(dve, proj_lo_ok, NPROJ * n + 4 + c)
                bank = (ps_mb, ps_ma)[c]
                dve.tensor_tensor(vn_f[:], bank[:].rearrange("p (t d) -> p t d", t=2),
                                  bv_all[:, None, :].broadcast_to([P, 2, D]),
                                  ALU.add).then_inc(v_sum_ok, 1)

            def proj_lo(n, par, m):
                name, c = QKV_ORDER[m][0], int(QKV_ORDER[m][1])
                wait(dve, proj_hi_ok, NPROJ * n + m + 1)
                if name == "v":
                    dve.tensor_tensor(vn_lo[par][:, 2 * c:2 * c + 2], vn_f[:],
                                      vn_hi[par][:, 2 * c:2 * c + 2].bitcast(F32), ALU.subtract).then_inc(proj_lo_ok, 1)
                    return
                bank = {"q0": ps_mb, "q1": ps_ma, "k0": ps_a, "k1": ps_b}[QKV_ORDER[m]]
                hi, lo, bias = (q_hi, q_lo, 0) if name == "q" else (kn_hi, kn_lo, 1)
                dve.scalar_tensor_tensor(out=lo[:, c], in0=bank[:], scalar=bqk[:, bias, c:c + 1],
                                         in1=hi[:, c].bitcast(F32), op0=ALU.add, op1=ALU.subtract).then_inc(proj_lo_ok, 1)

            def max_of(b, t, n):
                wait(dve, scored, KB * (QT * b + t) + n + 1)
                ins = dve.tensor_reduce(mx3[:, n:n + 1], ps_s[:, n], AX.X, ALU.max)
                if n < KB - 1:
                    return
                max_steps(b, t, ins)

            def max_steps(b, t, ins):
                ins.then_inc(max_a, 1)
                wait(dve, max_a, QT * b + t + 1)
                dve.tensor_reduce(mx1[:], mx3[:], AX.X, ALU.max).then_inc(max_step.sem, 1)
                wait(dve, max_step.sem, QT * b + t + 1)
                wait(dve, exp_done, QT * b + t)
                dve.tensor_scalar(neg_max[:], mx1[:], -SCALE, None, ALU.mult).then_inc(max_ok, 1)

            def p_lo(b, t, n, bank):
                wait(dve, pt_hi_ok, KB * (QT * b + t) + n + 1)
                c = slice(GPB * n, GPB * n + GPB)
                dve.tensor_tensor(pt_lo[:, c], bank[:].rearrange("p (g q) -> p g q", g=GPB), pt_hi[:, c].bitcast(F32),
                                  ALU.subtract).then_inc(pt_lo_ok, 1)

            def add_x(b, par, t):
                wait(dve, pv_done, QT * b + t + 1)
                dve.reciprocal(rsum[:], sums[:, par, t:t + 1]).then_inc(rsum_ok, 1)
                wait(dve, rsum_ok, QT * b + t + 1)
                if t == 0:
                    wait(dve, row_ok, b - 1)
                dve.scalar_tensor_tensor(out=x1[par][:, t], in0=ps_pv[:, 0:D], scalar=rsum[:, 0:1], in1=x_sb[par][:, t],
                                         op0=ALU.mult, op1=ALU.add).then_inc(x1_ok, 1)

            def top_expert(b):
                s = top_step
                s.begin(b)
                wait(dve, aff_ps, b + 1)
                s(dve, dve.tensor_copy(aff[:].rearrange("p t e -> p (t e)"), ps_ma[:, 0:QT * E]))
                settle(dve, settled)
                for t in range(QT):
                    ins = dve.max(top[:, t], aff[:, t])
                s(dve, ins)
                settle(dve, settled)
                for t in range(QT):
                    ins = dve.max_index(top_i[:, t], top[:, t], aff[:, t])
                s(dve, ins)
                s(dve, dve.tensor_copy(top_f[:], top_i[:, :, 0]))
                s(dve, dve.tensor_tensor(hot[:], iota_e[:], top_f[:, :, None].broadcast_to([P, QT, E]), ALU.is_equal))

            def gates(b):
                wait(dve, gate_exp, b + 1)
                dve.tensor_scalar(ea1[:], ea[:], 1.0, None, ALU.add).then_inc(gate_step, 1)
                wait(dve, gate_step, b + 1)
                wait(dve, rows_out, 16 * b)
                dve.reciprocal(row_sb[:, :, 2 * D], ea1[:]).then_inc(gate_ok, 1)

            def ranks(b):
                s = rank_step
                s.begin(b)
                wait(dve, rank_ps, b + 1)
                s(dve, dve.tensor_tensor(rank_e[:], ps_ma[:, 0:QT * E].rearrange("p (t e) -> p t e", t=QT), hot[:], ALU.mult))
                s(dve, dve.tensor_reduce(rank_f[:], rank_e[:], AX.X, ALU.add))
                s(dve, dve.tensor_copy(rank_i[:], rank_f[:]))
                dve.tensor_scalar(lohi_i[:, 0], rank_i[:], P - 1, None, ALU.bitwise_and).then_inc(s.sem, 1)
                s.n += 1
                s(dve, dve.tensor_scalar(lohi_i[:, 1], rank_i[:], 7, None, ALU.logical_shift_right))
                s(dve, dve.tensor_copy(lohi[:], lohi_i[:]))
                wait(dve, table_ps, b)
                for t in range(QT):
                    ins = dve.tensor_scalar(lo_hot[:, t], iota_f[:], lohi[:, 0, t:t + 1], None, ALU.is_equal)
                ins.then_inc(lo_hot_ok, 1)
                wait(dve, put_ok, b)
                dve.tensor_tensor(hi_hot[:], iota_r[:], lohi[:, 1, :, None].broadcast_to([P, QT, RANKS]), ALU.is_equal)
                dve.tensor_scalar(hot_id[:, :, 0], hot[:], part1[:, 0:1], None, ALU.mult)
                dve.tensor_tensor(hot_id[:, :, 1], hot[:], tile_no[:], ALU.mult).then_inc(id_ok, 1)
                dve.tensor_reduce(hot_sum[:], hot[:].rearrange("p t e -> p e t"), AX.X, ALU.add).then_inc(sum_step, 1)
                wait(dve, id_ok, b + 1)
                dve.tensor_scalar(tile_no[:], tile_no[:], float(QT), None, ALU.add)
                wait(dve, sum_step, 2 * b + 1)
                dve.tensor_tensor(acc[:], acc[:], hot_sum[:], ALU.add).then_inc(sum_step, 1)

            def add_table(b):
                wait(dve, table_ps, b + 1)
                wait(dve, table_ok, b)
                dve.tensor_tensor(table[:].rearrange("p a n -> p (a n)"), table[:].rearrange("p a n -> p (a n)"), ps_ma[:],
                                  ALU.add).then_inc(table_ok, 1)

            dve.wait_ge(x_in, 16)
            variance(0, 0, 0, lambda t: x_sb[0][:, t])
            dve.wait_ge(w_hi_ok, 1)
            dve.tensor_tensor(w_lo[:], w_raw, w_hi[:].bitcast(F32), ALU.subtract).then_inc(w_lo_ok, 1)
            ln1(0, 0)
            turned_x(0, 0)
            turned_x(0, 1)
            for m in range(4):
                proj_lo(0, 0, m)
            for c in range(2):
                proj_sum(0, c)
                proj_lo(0, 0, 4 + c)
            dve.wait_ge(made, 14)
            dve.wait_ge(made2, 3)
            for n in range(KB):
                max_of(0, 0, n)

            def body(b, par):
                later = not isinstance(b, int) or b > 0
                for t in range(1, QT):
                    if t > 1:
                        add_x(b, par, t - 2)
                    elif later:
                        add_x(b - 1, 1 - par, QT - 1)
                        wait(dve, x1_ok, QT * b)
                        variance(1, b - 1, 1 - par, lambda u: x1[1 - par][:, u])
                    p_lo(b, t - 1, 0, ps_a)
                    p_lo(b, t - 1, 1, ps_b)
                    max_of(b, t, 0)
                    p_lo(b, t - 1, 2, ps_a)
                    max_of(b, t, 1)
                    if later and t == 1:
                        ln2(b - 1, 1 - par)
                    if later and t == 2:
                        ln3(b - 1)
                    if later and t == 3:
                        ranks(b - 1)
                    if not is_last(b) and t == 3:
                        turned_x(b + 1, 0)
                    max_of(b, t, 2)
                    if later and t == 1:
                        wait(dve, h_ok, b)
                        variance(2, b - 1, 1 - par, lambda u: h_sb[:, u])
                    if not is_last(b) and t == 1:
                        wait(dve, x_in, 16 * (b + 2))
                        variance(0, b + 1, 1 - par, lambda u: x_sb[1 - par][:, u])
                    if not is_last(b) and t == 2:
                        ln1(b + 1, 1 - par)
                    if later and t == 2:
                        top_expert(b - 1)
                    if later and t == 3:
                        gates(b - 1)
                add_x(b, par, 2)
                if not is_last(b):
                    turned_x(b + 1, 1)
                    if later:
                        add_table(b - 1)
                    for m in range(4):
                        proj_lo(b + 1, 1 - par, m)
                    proj_sum(b + 1, 0)
                    proj_lo(b + 1, 1 - par, 4)
                    p_lo(b, 3, 0, ps_a)
                    p_lo(b, 3, 1, ps_b)
                    proj_sum(b + 1, 1)
                    proj_lo(b + 1, 1 - par, 5)
                    p_lo(b, 3, 2, ps_a)
                    for n in range(KB):
                        max_of(b + 1, 0, n)
                else:
                    p_lo(b, 3, 0, ps_a)
                    p_lo(b, 3, 1, ps_b)
                    p_lo(b, 3, 2, ps_a)
                    add_table(b - 1)

            batches(dve, body)
            par = (B - 1) % 2
            add_x(B - 1, par, QT - 1)
            wait(dve, x1_ok, QT * B)
            variance(1, B - 1, par, lambda u: x1[par][:, u])
            ln2(B - 1, par)
            wait(dve, h_ok, B)
            variance(2, B - 1, par, lambda u: h_sb[:, u])
            top_expert(B - 1)
            ln3(B - 1)
            gates(B - 1)
            ranks(B - 1)

            step = [0]

            def link(ins):
                step[0] += 1
                ins.then_inc(meta_step, 1)
                dve.wait_ge(meta_step, step[0])

            dve.wait_ge(cnt_ps, 1)
            link(dve.tensor_copy(cnt[:], ps_mb[:, 0:E]))
            link(dve.tensor_tensor(over[:], cnt[:, :, None].broadcast_to([P, E, MAXT]), thr[:], ALU.is_gt))
            link(dve.tensor_reduce(tl[:], over[:], AX.X, ALU.add))
            link(dve.tensor_scalar(tl1[:], tl[:], 1.0, None, ALU.max))
            link(dve.tensor_tensor(tlu[:], upto[:], tl1[:, None, :].broadcast_to([P, E, E]), ALU.mult))
            link(dve.tensor_reduce(ends[:], tlu[:], AX.X, ALU.add))
            link(dve.tensor_tensor(past[:], tile_j[:], ends[:, None, 0:E - 1].broadcast_to([P, META, E - 1]), ALU.is_ge))
            link(dve.tensor_tensor(past_t[:], past[:], tl1[:, None, 0:E - 1].broadcast_to([P, META, E - 1]), ALU.mult))
            dve.tensor_reduce(meta_f[:, 0], past[:], AX.X, ALU.add)
            link(dve.tensor_reduce(start_f[:], past_t[:], AX.X, ALU.add))
            link(dve.tensor_tensor(start_f[:], tile_j[:, :, 0], start_f[:], ALU.subtract))
            link(dve.tensor_scalar(start_f[:], start_f[:], float(HALVES), None, ALU.mult))
            link(dve.scalar_tensor_tensor(out=meta_f[:, 1], in0=meta_f[:, 0], scalar=float(RANKS), in1=start_f[:],
                                          op0=ALU.mult, op1=ALU.add))
            link(dve.tensor_scalar(meta_f[:, 1], meta_f[:, 1], float(E * RANKS - HALVES), None, ALU.min))
            dve.tensor_copy(meta[:], meta_f[:]).then_inc(meta_ok, 1)
            add_table(B - 1)
            dve.wait_ge(table_ok, B)
            link(dve.scalar_tensor_tensor(out=ids_f, in0=table[:, 1], scalar=float(P), in1=table[:, 0],
                                          op0=ALU.mult, op1=ALU.add))
            link(dve.tensor_scalar(empty, ids_f, 0.0, float(NO_TOKEN), ALU.is_equal, ALU.mult))
            dve.scalar_tensor_tensor(out=ids[:], in0=ids_f, scalar=-1.0, in1=empty,
                                     op0=ALU.add, op1=ALU.add).then_inc(ids_ok, 1)

            def expert_x(j):
                wait(dve, xe_ok, DC * (j + 1))
                wait(dve, mm1_ok, FC // 2 * j)
                dve.tensor_copy(xe_hi, xe).then_inc(xe_hi_ok, 1)
                wait(dve, xe_hi_ok, j + 1)
                dve.tensor_tensor(xe_lo, xe, xe_hi.bitcast(F32), ALU.subtract).then_inc(xe_lo_ok, 1)

            expert_x(0)

            def store_tile(j, par):
                wait(dve, mm2_ok, HALVES * (j + 1))
                wait(dve, vec_in[par], vec_value(j, par))
                dve.tensor_tensor(y_b, ps_pv[:].rearrange("p (k d) -> p k d", k=HALVES),
                                  b2_all[par][:, None, :].broadcast_to([P, HALVES, D]), ALU.add).then_inc(y_read, 1)
                wait(dve, y_read, j + 1)
                for k in range(HALVES):
                    wait(dve, stored[k], 16 * j)
                    wait(dve, gathered[par][k], 8 * (j - par) + 16)
                    dve.scalar_tensor_tensor(out=o_sb[:, k], in0=y_b[:, k], scalar=g[par][:, k, 2 * D:2 * D + 1],
                                             in1=g[par][:, k, D:2 * D], op0=ALU.mult, op1=ALU.add).then_inc(o_ok, 1)

            def tile_body(j, par):
                if not isinstance(j, int) or j > 0:
                    store_tile(j - 1, 1 - par)
                    wait(dve, w2_hi_ok, 2 * j)
                    dve.tensor_tensor(w2_lo[:, 0:FC // 2], w2_raw[:, 0:FC // 2], w2_hi[:, 0:FC // 2].bitcast(F32),
                                      ALU.subtract).then_inc(w2_lo_v, 1)
                for n in range(FC // 2):
                    c = slice(2 * n, 2 * n + 2)
                    wait(dve, h1_ok, FC * j + 2 * n + 2)
                    if n == 0:
                        wait(dve, mm2_ok, HALVES * j)
                    dve.tensor_copy(h1_hi[:, c], h1[:, c]).then_inc(h1_hi_ok, 1)
                    wait(dve, h1_hi_ok, FC // 2 * j + n + 1)
                    dve.tensor_tensor(h1_lo[:, c], h1[:, c], h1_hi[:, c].bitcast(F32), ALU.subtract).then_inc(h1_lo_ok, 1)
                wait(dve, w1_hi_ok, 2 * j + 1)
                dve.tensor_tensor(w1_lo[:, 0], w1_raw[:, 0], w1_hi[:, 0].bitcast(F32),
                                  ALU.subtract).then_inc(w1_lo_v, 1)
                expert_x(j + 1)

            tiles(dve, tile_body)
            store_tile(TILES - 1, (TILES - 1) % 2)

        @block.tensor
        def _(pe):
            pe.wait_ge(made2, 3)

            def three(out_ap, ahi, alo, bhi, blo, first, last):
                pe.matmul(out_ap, ahi, bhi, start=first, stop=False)
                pe.matmul(out_ap, ahi, blo, start=False, stop=False)
                return pe.matmul(out_ap, alo, bhi, start=False, stop=last)

            def turn_x(n, c):
                if c == 0:
                    wait(pe, xn_ok, n + 1)
                    wait(pe, ht_ok, DC * (n - 1))
                else:
                    wait(pe, xt_lo_ok, DC * n + 1)
                for t in range(QT):
                    ins = pe.transpose(ps_mb[:, t * P:(t + 1) * P], xn[:, t, c * P:(c + 1) * P], ident[:])
                ins.then_inc(x_turned, 1)

            def project(n, m):
                name, c = QKV_ORDER[m][0], int(QKV_ORDER[m][1])
                bank = {"q0": ps_mb, "q1": ps_ma, "k0": ps_a, "k1": ps_b, "v0": ps_mb, "v1": ps_ma}[QKV_ORDER[m]]
                if m == 0:
                    wait(pe, xt_lo_ok, DC * (n + 1))
                if m == 1:
                    wait(pe, table_ok, n - 1)
                if m == 2:
                    wait(pe, pt_lo_ok, KB * (QT * n - 1))
                if m >= 4:
                    wait(pe, proj_lo_ok, NPROJ * n + m - 3)
                if name == "v":
                    for u in range(2):
                        t = 2 * c + u
                        for k in range(DC):
                            ins = three(bank[:, u * D:(u + 1) * D], xt_hi[:, k, t * P:(t + 1) * P], xt_lo[:, k, t * P:(t + 1) * P],
                                        w_hi[:, 2, k], w_lo[:, 2, k], k == 0, k == DC - 1)
                else:
                    w = "qk".index(name)
                    for k in range(DC):
                        e = slice(c * P, (c + 1) * P)
                        ins = three(bank[:], w_hi[:, w, k, e], w_lo[:, w, k, e], xt_hi[:, k], xt_lo[:, k], k == 0, k == DC - 1)
                ins.then_inc(projected, 1)

            def score(b, par, t, n):
                if n == 0:
                    wait(pe, exp_done, QT * b + t)
                    if t == 0:
                        wait(pe, proj_lo_ok, NPROJ * b + 2)
                        wait(pe, ctx_lo_ok, NPIECE * b + 2)
                if n == KB - 1 and t == 0:
                    wait(pe, proj_lo_ok, NPROJ * b + 4)
                for k in range(DC):
                    q = q_hi[:, k, t * P:(t + 1) * P], q_lo[:, k, t * P:(t + 1) * P]
                    if n < KB - 1:
                        kk = k_hi[par][:, k, n * BANK:(n + 1) * BANK], k_lo[par][:, k, n * BANK:(n + 1) * BANK]
                    else:
                        kk = kn_hi[:, k], kn_lo[:, k]
                    ins = three(ps_s[:, n], *q, *kk, k == 0, k == DC - 1)
                ins.then_inc(scored, 1)

            def turn_p(b, t, n, bank):
                if n == 0:
                    wait(pe, exp_done, QT * b + t + 1)
                    wait(pe, pt_lo_ok, KB * (QT * b + t))
                if n == KB - 1:
                    wait(pe, pt_lo_ok, KB * (QT * b + t) + 1)
                for u in range(GPB):
                    c = GPB * n + u
                    ins = pe.transpose(bank[:, u * P:(u + 1) * P], probs[:, c * P:(c + 1) * P], ident[:])
                ins.then_inc(p_turned, 1)

            def attend(b, par, t):
                wait(pe, x1_ok, QT * b + t)
                for c in range(KC):
                    if c % GPB == 0:
                        wait(pe, pt_lo_ok, KB * (QT * b + t) + c // GPB + 1)
                    if t == 0 and c == 0:
                        wait(pe, ctx_lo_ok, NPIECE * (b + 1))
                        wait(pe, proj_lo_ok, NPROJ * (b + 1))
                    v = (v_hi[par][:, c], v_lo[par][:, c]) if c < CC else (vn_hi[par][:, c - CC], vn_lo[par][:, c - CC])
                    ins = three(ps_pv[:, 0:D], pt_hi[:, c], pt_lo[:, c], *v, c == 0, c == KC - 1)
                ins.then_inc(pv_done, 1)

            def turn_h(b, c):
                bank = (ps_ma, ps_mb)[c]
                if c == 0:
                    wait(pe, h_ok, b + 1)
                    wait(pe, proj_lo_ok, NPROJ * min_b(b + 2))
                    wait(pe, table_ok, b)
                for t in range(QT):
                    ins = pe.transpose(bank[:, t * P:(t + 1) * P], h_sb[:, t, c * P:(c + 1) * P], ident[:])
                ins.then_inc(h_turned, 1)

            def min_b(n):
                return min(n, B) if isinstance(n, int) else n

            def affinities(b):
                wait(pe, ht_ok, DC * (b + 1))
                for t in range(QT):
                    for k in range(DC):
                        ins = pe.matmul(ps_ma[:, t * E:(t + 1) * E], ht[:, k, t * P:(t + 1) * P], cent_sb[:, k],
                                        start=(k == 0), stop=(k == DC - 1))
                ins.then_inc(aff_ps, 1)

            def rank(b):
                wait(pe, top_step.sem, top_step.done(b))
                wait(pe, sum_step, 2 * b)
                pe.matmul(ps_ma[:, 0:QT * E], tri[:], hot[:].rearrange("p t e -> p (t e)"), start=True, stop=False)
                for t in range(QT - 1):
                    n = QT - 1 - t
                    pe.matmul(ps_ma[:, (t + 1) * E:QT * E].rearrange("p (n e) -> p n e", n=n), ones[:],
                              hot[:, t, None, :].broadcast_to([P, n, E]), start=False, stop=False)
                pe.matmul(ps_ma[:, 0:QT * E].rearrange("p (n e) -> p n e", n=QT), ones[:],
                          acc[:, None, :].broadcast_to([P, QT, E]), start=False, stop=True).then_inc(rank_ps, 1)

            def fill_table(b):
                wait(pe, lo_hot_ok, b + 1)
                wait(pe, put_ok, b + 1)
                wait(pe, id_ok, b + 1)
                for t in range(QT):
                    ins = pe.matmul(ps_ma[:], lo_hot[:, t], put[:, t].rearrange("p a e r -> p (a e r)"),
                                    start=(t == 0), stop=(t == QT - 1))
                ins.then_inc(table_ps, 1)

            turn_x(0, 0)
            turn_x(0, 1)
            pe.wait_ge(w_lo_ok, 1)
            for m in range(NPROJ):
                project(0, m)
            for n in range(KB):
                score(0, 0, 0, n)

            def body(b, par):
                later = not isinstance(b, int) or b > 0
                for t in range(1, QT):
                    turn_p(b, t - 1, 0, ps_a)
                    turn_p(b, t - 1, 1, ps_b)
                    if later and t == 3:
                        rank(b - 1)
                    score(b, par, t, 0)
                    turn_p(b, t - 1, 2, ps_a)
                    if not is_last(b) and t == 3:
                        turn_x(b + 1, 0)
                    score(b, par, t, 1)
                    score(b, par, t, 2)
                    if later and t == 1:
                        turn_h(b - 1, 0)
                        turn_h(b - 1, 1)
                    if later and t == 2:
                        affinities(b - 1)
                    if not is_last(b) and t == 3:
                        turn_x(b + 1, 1)
                    attend(b, par, t - 1)
                if later:
                    fill_table(b - 1)
                if not is_last(b):
                    for m in range(5):
                        project(b + 1, m)
                    wait(pe, proj_lo_ok, NPROJ * (b + 1) + 4)
                    turn_p(b, 3, 0, ps_a)
                    turn_p(b, 3, 1, ps_b)
                    project(b + 1, 5)
                    turn_p(b, 3, 2, ps_a)
                    for n in range(KB):
                        score(b + 1, 1 - par, 0, n)
                else:
                    for n, bank in enumerate((ps_a, ps_b, ps_a)):
                        turn_p(b, 3, n, bank)
                attend(b, par, 3)

            batches(pe, body)
            turn_h(B - 1, 0)
            turn_h(B - 1, 1)
            affinities(B - 1)
            rank(B - 1)
            pe.wait_ge(sum_step, 2 * B)
            pe.matmul(ps_mb[:, 0:E], ones[:], acc[:], start=True, stop=True).then_inc(cnt_ps, 1)
            fill_table(B - 1)

            def turn_rows(j, par):
                for k in range(HALVES):
                    wait(pe, gathered[par][k], 8 * (j - par) + 16)
                wait(pe, xe_ok, DC * j)
                if isinstance(j, int) and j == 0:
                    pe.wait_ge(meta_step, 1)
                for c in range(DC):
                    for k in range(HALVES):
                        ins = pe.transpose(ps_mb[:, c * TILE + k * P:c * TILE + (k + 1) * P],
                                           g[par][:, k, c * P:(c + 1) * P], ident[:])
                ins.then_inc(xe_turned, 1)

            turn_rows(0, 0)

            def tile_body(j, par):
                wait(pe, xe_lo_ok, j + 1)
                wait(pe, xe_hi_ok, j + 1)
                wait(pe, w1_hi_ok, 2 * j)
                wait(pe, w1_lo_v, j)
                wait(pe, w1_lo_p, j)
                if isinstance(j, int) and j == 0:
                    pe.wait_ge(ctx_lo_ok, NPIECE * (B + 1))
                for f in range(FC):
                    if f % 2 == 0:
                        wait(pe, h1_ok, FC * (j - 1) + f + 2)
                    fs = slice(f * P, (f + 1) * P)
                    for k in range(DC):
                        ins = three(h_bank(f // 2)[:, (f % 2) * TILE:(f % 2 + 1) * TILE],
                                    w1_hi[:, k, fs], w1_lo[:, k, fs], xe_hi[:, k], xe_lo[:, k], k == 0, k == DC - 1)
                    if f % 2:
                        ins.then_inc(mm1_ok, 1)
                wait(pe, y_read, j)
                wait(pe, w2_hi_ok, 2 * j)
                wait(pe, w2_lo_v, j)
                for k in range(HALVES):
                    ks = slice(k * P, (k + 1) * P)
                    for f in range(FC):
                        if k == 0 and f % 2 == 0:
                            wait(pe, h1_lo_ok, FC // 2 * j + f // 2 + 1)
                            wait(pe, h1_hi_ok, FC // 2 * j + f // 2 + 1)
                        if k == 0 and f == FC // 2:
                            wait(pe, w2_lo_p, j)
                        ins = three(ps_pv[:, k * D:(k + 1) * D], h1_hi[:, f, ks], h1_lo[:, f, ks],
                                    w2_hi[:, f], w2_lo[:, f], f == 0, f == FC - 1)
                    ins.then_inc(mm2_ok, 1)
                    if k == 0:
                        turn_rows(j + 1, 1 - par)

            tiles(pe, tile_body)


def kernel(x, ctx_1024, L0_xattn_Wq, L0_xattn_bq, L0_xattn_Wk, L0_xattn_bk, L0_xattn_Wv, L0_xattn_bv,
           L0_ffn_centroids, L0_ffn_ln_g, L0_ffn_ln_b, L0_ffn_w1, L0_ffn_b1, L0_ffn_w2, L0_ffn_b2):
    import numpy as np
    import concourse.bacc as bacc
    from concourse import mybir as mb
    from concourse.bass_utils import run_bass_kernel_spmd

    def a(v):
        return np.asarray(v)

    def columns(v):
        return a(v).reshape(E, -1, P).transpose(0, 2, 1)

    data = {
        "x": a(x),
        "keys_src": np.concatenate([a(ctx_1024).transpose(0, 2, 1), a(L0_ffn_w1).transpose(0, 2, 1)]),
        "vals_src": np.concatenate([a(ctx_1024), a(L0_ffn_w2).transpose(0, 2, 1)]),
        "wq": a(L0_xattn_Wq).T, "wk": a(L0_xattn_Wk).T, "wv": a(L0_xattn_Wv).T,
        "b_cols": np.stack([a(v).reshape(DC, P).T for v in (L0_xattn_bq, L0_xattn_bk)], axis=1), "bv": a(L0_xattn_bv),
        "cent": a(L0_ffn_centroids).T,
        "vecs": np.concatenate([columns(L0_ffn_ln_g), columns(L0_ffn_ln_b), columns(L0_ffn_b1)], axis=2),
        "b2": a(L0_ffn_b2),
    }
    nc = bacc.Bacc("TRN2", target_bir_lowering=False, num_devices=1)
    arrays, args = {}, []
    for name, v in data.items():
        v = np.ascontiguousarray(v)
        arrays[f"in_{name}"] = v
        args.append(nc.dram_tensor(f"in_{name}", v.shape, mb.dt.from_np(v.dtype), kind="ExternalInput").ap())
    args.append(nc.dram_tensor("out_0", (TOKENS, D), mb.dt.float32, kind="ExternalOutput").ap())
    xattn_experts(nc, *args)
    r = run_bass_kernel_spmd(nc, [arrays], core_ids=[0])
    return r.results[0]["out_0"].reshape(B, S, D)
```

```python
from contextlib import ExitStack

import concourse.bass as bass
from concourse import mybir

P = 128
B, S, D = 8, 512, 256
K_CTX = 1024
KEYS = K_CTX + S
DC = D // P
QT = S // P
KC = KEYS // P
CC = K_CTX // P
BANK = 512
KB = KEYS // BANK
GPB = BANK // P
TOKENS = B * S
E, F = 8, 1024
FC = F // P
TILE = 256
HALVES = TILE // P
TILES = TOKENS // TILE + E - 1
RANKS = TOKENS // P
MAXT = TOKENS // TILE
META = TILES + 2
ROW = 2 * D + 4
NO_TOKEN = 2 * TOKENS
LN_EPS = 1e-5
SCALE = 64 ** -0.5

ALU = mybir.AluOpType
ACT = mybir.ActivationFunctionType
AX = mybir.AxisListType
F32 = mybir.dt.float32
F32R = mybir.dt.float32r
BF16 = mybir.dt.bfloat16
I32 = mybir.dt.int32
U32 = mybir.dt.uint32

QKV_ORDER = ("v0", "v1", "q0", "q1", "k0", "k1")
NPROJ = len(QKV_ORDER)
NPIECE = 4


class Steps:

    def __init__(self, sem, per):
        self.sem, self.per = sem, per

    def begin(self, b):
        self.b, self.n = b, 0

    def __call__(self, eng, ins):
        self.n += 1
        assert self.n <= self.per
        ins.then_inc(self.sem, 1)
        eng.wait_ge(self.sem, self.b * self.per + self.n)

    def count(self, ins):
        self.n += 1
        ins.then_inc(self.sem, 1)

    def done(self, b):
        return (b + 1) * self.per


def some(count):
    return not isinstance(count, int) or count > 0


def settle(eng, sem):
    eng.sem_inc(sem, 1)


def xattn_experts(nc, x, keys_src, vals_src, wq, wk, wv, b_cols, bv, cent, vecs, b2, out):
    rows = nc.dram_tensor("rows", [TOKENS, ROW], F32, kind="Internal").ap()

    ctx = ExitStack()
    with ctx:
        def sb(name, shape, dt=F32):
            return ctx.enter_context(nc.sbuf_tensor(name, shape, dt))

        def sem(name):
            return ctx.enter_context(nc.semaphore(name))

        ps_s = ctx.enter_context(nc.psum_tensor("ps_s", [P, KB, BANK], F32))
        ps_a, ps_b, ps_pv, ps_ma, ps_mb = [
            ctx.enter_context(nc.psum_tensor(n, [P, BANK], F32))
            for n in ("ps_a", "ps_b", "ps_pv", "ps_ma", "ps_mb")]

        ident = sb("ident", [P, P])
        ident_in = sb("ident_in", [P, P])
        tri = sb("tri", [P, P], BF16)
        ones = sb("ones", [P, P], BF16)
        iota_f = sb("iota_f", [P, P])
        iota_e = sb("iota_e", [P, QT, E])
        iota_r = sb("iota_r", [P, QT, RANKS])
        part1 = sb("part1", [P, 1])
        tile_no = sb("tile_no", [P, QT, E])
        thr = sb("thr", [P, E, MAXT])
        upto = sb("upto", [P, E, E])
        upto_in = sb("upto_in", [P, E, E])
        tile_j = sb("tile_j", [P, META, E - 1])
        w_hi = sb("w_hi", [P, 3, DC, D], F32R)
        w_lo = sb("w_lo", [P, 3, DC, D], F32R)
        bqk = sb("bqk", [P, 2, DC])
        bv_all = sb("bv_all", [P, D])
        cent_sb = sb("cent_sb", [P, DC, E])
        eps = sb("eps", [P, 1])

        k_raw = sb("k_raw", [P, DC, K_CTX])
        v_raw = sb("v_raw", [P, CC, D])
        k_hi = [sb(f"k_hi{i}", [P, DC, K_CTX], F32R) for i in range(2)]
        k_lo = [sb(f"k_lo{i}", [P, DC, K_CTX], F32R) for i in range(2)]
        v_hi = [sb(f"v_hi{i}", [P, CC, D], F32R) for i in range(2)]
        v_lo = [sb(f"v_lo{i}", [P, CC, D], F32R) for i in range(2)]
        kn_hi = sb("kn_hi", [P, DC, S], F32R)
        kn_lo = sb("kn_lo", [P, DC, S], F32R)
        vn_hi = [sb(f"vn_hi{i}", [P, QT, D], F32R) for i in range(2)]
        vn_lo = [sb(f"vn_lo{i}", [P, QT, D], F32R) for i in range(2)]
        vn_f = sb("vn_f", [P, 2, D])
        q_hi = sb("q_hi", [P, DC, S], F32R)
        q_lo = sb("q_lo", [P, DC, S], F32R)
        x_both = sb("x_both", [P, 2 * QT, D])
        x_sb = [x_both[:, i * QT:(i + 1) * QT] for i in range(2)]
        xn = sb("xn", [P, QT, D])
        xt_hi = sb("xt_hi", [P, DC, S], F32R)
        xt_lo = sb("xt_lo", [P, DC, S], F32R)
        probs = sb("probs", [P, KEYS])
        w_raw = probs[:].rearrange("p (a c d) -> p a c d", a=3, c=DC)
        pt_hi = sb("pt_hi", [P, KC, P], F32R)
        pt_lo = sb("pt_lo", [P, KC, P], F32R)
        x1 = [sb(f"x1_{i}", [P, QT, D]) for i in range(2)]
        mx3 = sb("mx3", [P, KB])
        mx1 = sb("mx1", [P, 1])
        neg_max = sb("neg_max", [P, 1])
        sums = sb("sums", [P, 2, QT])
        rsum = sb("rsum", [P, 1])

        st = [sb(f"st{i}", [P, QT, 6]) for i in range(3)]
        mv = [sb(f"mv{i}", [P, QT, 2]) for i in range(3)]
        ve = [sb(f"ve{i}", [P, QT]) for i in range(3)]
        lnv = [sb(f"lnv{i}", [P, QT]) for i in range(3)]
        y0 = [sb(f"y0{i}", [P, QT]) for i in range(3)]
        ysq = [sb(f"ysq{i}", [P, QT]) for i in range(3)]
        rstd = [sb(f"rstd{i}", [P, QT]) for i in range(3)]
        h_sb = sb("h_sb", [P, QT, D])
        ht = sb("ht", [P, DC, S])
        row_sb = sb("row_sb", [P, QT, ROW])
        aff = sb("aff", [P, QT, E])
        top = sb("top", [P, QT, 8])
        top_i = sb("top_i", [P, QT, 8], U32)
        top_f = sb("top_f", [P, QT])
        ea = sb("ea", [P, QT])
        ea1 = sb("ea1", [P, QT])
        hot = sb("hot", [P, QT, E], BF16)
        hot_sum = sb("hot_sum", [P, E])
        acc = sb("acc", [P, E], BF16)
        rank_e = sb("rank_e", [P, QT, E])
        rank_f = sb("rank_f", [P, QT])
        rank_i = sb("rank_i", [P, QT], I32)
        lohi_i = sb("lohi_i", [P, 2, QT], I32)
        lohi = sb("lohi", [P, 2, QT])
        lo_hot = sb("lo_hot", [P, QT, P], BF16)
        hi_hot = sb("hi_hot", [P, QT, RANKS], BF16)
        hot_id = sb("hot_id", [P, QT, 2, E], BF16)
        put = sb("put", [P, QT, 2, E, RANKS], BF16)
        table = sb("table", [P, 2, E * RANKS])
        ids_f, empty = ht[:, 0, 0:E * RANKS], ht[:, 0, E * RANKS:2 * E * RANKS]
        ids = sb("ids", [P, E * RANKS], I32)
        cnt = sb("cnt", [P, E])
        over = sb("over", [P, E, MAXT])
        tl = sb("tl", [P, E])
        tl1 = sb("tl1", [P, E])
        tlu = sb("tlu", [P, E, E])
        ends = sb("ends", [P, E])
        past = sb("past", [P, META, E - 1])
        past_t = sb("past_t", [P, META, E - 1])
        eid_f = sb("eid_f", [P, META])
        start_f = sb("start_f", [P, META])
        meta_f = sb("meta_f", [P, 2, META])
        meta = sb("meta", [P, 2, META], I32)

        def in_parts(buf):
            return [buf[:, n * FC // 2:(n + 1) * FC // 2] for n in range(2)]

        w1_raw = [[k_raw[:, n] for n in range(DC)], [x1[n][:].rearrange("p t d -> p (t d)") for n in range(DC)]]
        w2_raw = [in_parts(v_raw), [h_sb[:], probs[:, 0:FC // 2 * D].rearrange("p (c d) -> p c d", d=D)]]
        w1_hi, w1_lo = k_hi, k_lo
        w2_hi, w2_lo = [in_parts(v_hi[0]), [v[:] for v in vn_hi]], [in_parts(v_lo[0]), [v[:] for v in vn_lo]]
        h1_hi, h1_lo = v_hi[1], v_lo[1]
        tok_out = sb("tok_out", [P, HALVES], I32)
        tok = [sb(f"tok{i}", [P, HALVES], I32) for i in range(2)]
        g = [row_sb[:, i * HALVES:(i + 1) * HALVES] for i in range(2)]
        vec = [sb(f"vec{i}", [P, 2 * DC + FC]) for i in range(2)]
        b2_all = [ht[:, 1, i * D:(i + 1) * D] for i in range(2)]
        xe, y_b = xn[:, 0:DC], xn[:, DC:DC + HALVES]
        xe_hi, xe_lo = [[xt[:, :, i * TILE:(i + 1) * TILE] for i in range(2)] for xt in (xt_hi, xt_lo)]
        y_banks = ps_pv, ps_ma
        h1 = x_both
        o_sb = vn_f

        ps_aff, ps_rank, ps_cnt = ps_ma[:, 0:QT * E], ps_ma[:, 0:QT * E], ps_mb[:, 0:E]

        const_in, x_in, k_in, v_in, rows_out = map(sem, ("const_in", "x_in", "k_in", "v_in", "rows_out"))
        made, made2, w_hi_ok, w_lo_ok = map(sem, ("made", "made2", "w_hi_ok", "w_lo_ok"))
        scored, p_turned, pv_done, x_turned, projected = map(
            sem, ("scored", "p_turned", "pv_done", "x_turned", "projected"))
        h_turned, aff_ps, rank_ps, table_ps, cnt_ps = map(
            sem, ("h_turned", "aff_ps", "rank_ps", "table_ps", "cnt_ps"))
        exp_done, pt_hi_ok, xt_hi_ok, proj_hi_ok, ctx_hi_ok, ht_ok, gate_exp = map(
            sem, ("exp_done", "pt_hi_ok", "xt_hi_ok", "proj_hi_ok", "ctx_hi_ok", "ht_ok", "gate_exp"))
        ln_act = [sem(f"ln_act{i}") for i in range(3)]
        max_ok, pt_lo_ok, x1_ok, xt_lo_ok, proj_lo_ok, v_sum_ok = map(
            sem, ("max_ok", "pt_lo_ok", "x1_ok", "xt_lo_ok", "proj_lo_ok", "v_sum_ok"))
        var_ok = [sem(f"var_ok{i}") for i in range(3)]
        max_step = Steps(sem("max_step"), QT)
        stat_ok = [sem(f"stat_ok{i}") for i in range(3)]
        aggr_ok = [sem(f"aggr_ok{i}") for i in range(3)]
        rstd_step = [Steps(sem(f"rstd_step{i}"), 4) for i in range(3)]
        top_step = Steps(sem("top_step"), 5)
        rank_step = Steps(sem("rank_step"), 6)
        hot_ok, gate_ok, id_ok, lo_hot_ok, table_ok, sum_step, rsum_ok = map(
            sem, ("hot_ok", "gate_ok", "id_ok", "lo_hot_ok", "table_ok", "sum_step", "rsum_ok"))
        meta_ok, ids_ok, meta_step, max_a, gate_step, settled = map(sem, ("meta_ok", "ids_ok", "meta_step", "max_a", "gate_step", "settled"))
        norm_ok, tok_out_ok = sem("norm_ok"), sem("tok_out_ok")
        ctx_lo_ok, xn_ok, h_ok, row_ok, put_ok = map(sem, ("ctx_lo_ok", "xn_ok", "h_ok", "row_ok", "put_ok"))
        tok_ok, mm1_ok, mm2_ok, xe_turned = map(sem, ("tok_ok", "mm1_ok", "mm2_ok", "xe_turned"))
        w1_in, w2_in = [[sem(f"{n}_in{i}") for i in range(2)] for n in ("w1", "w2")]
        gathered = [[sem(f"gathered{i}{k}") for k in range(HALVES)] for i in range(2)]
        vec_in = [sem(f"vec_in{i}") for i in range(2)]
        stored = [sem(f"stored{k}_") for k in range(HALVES)]
        xe_ok, xe_hi_ok, xe_lo_ok, h1_ok, h1_hi_ok, h1_lo_ok = map(
            sem, ("xe_ok", "xe_hi_ok", "xe_lo_ok", "h1_ok", "h1_hi_ok", "h1_lo_ok"))
        w1_hi_ok, w2_hi_ok, w1_lo_v, w2_lo_v, w1_lo_p, w2_lo_p, y_read, o_ok = map(
            sem, ("w1_hi_ok", "w2_hi_ok", "w1_lo_v", "w2_lo_v", "w1_lo_p", "w2_lo_p", "y_read", "o_ok"))

        def batches(eng, body):
            body(0, 0)
            with eng.Fori(0, (B - 2) // 2) as i:
                body(2 * i + 1, 1)
                body(2 * i + 2, 0)
            body(B - 1, (B - 1) % 2)

        def tiles(eng, body):
            body(0, 0)
            with eng.Fori(0, (TILES - 1) // 2) as i:
                body(2 * i + 1, 1)
                body(2 * i + 2, 0)

        proj_bank = ps_mb, ps_ma, ps_a, ps_b, ps_mb, ps_ma

        def h_bank(n):
            return ps_s[:, n] if n < KB else ps_a[:]

        def vec_value(j, par):
            return (j - par) * 16 + 32

        def w_value(j, par):
            return (j + par) * 16

        def is_last(b):
            return isinstance(b, int) and b == B - 1

        block = ctx.enter_context(nc.Block())

        @block.sync
        def _(sp):
            def load_k(n):
                if some(NPIECE * n - 2):
                    sp.wait_ge(ctx_hi_ok, NPIECE * n - 2)
                if some(NPIECE * n - 2):
                    sp.wait_ge(ctx_lo_ok, NPIECE * n - 2)
                sp.dma_start(k_raw[:], keys_src[bass.ds(n, 1)].rearrange("o (c p) k -> p (o c) k", p=P)).then_inc(k_in, 16)

            def load_v(n):
                if some(NPIECE * n):
                    sp.wait_ge(ctx_hi_ok, NPIECE * n)
                if some(NPIECE * n):
                    sp.wait_ge(ctx_lo_ok, NPIECE * n)
                sp.dma_start(v_raw[:], vals_src[bass.ds(n, 1)].rearrange("o (c p) d -> p (o c) d", p=P)).then_inc(v_in, 16)

            def load_x(n, par):
                if some(QT * (n - 1)):
                    sp.wait_ge(x1_ok, QT * (n - 1))
                if some(n - 1):
                    sp.wait_ge(var_ok[0], n - 1)
                sp.dma_start(x_sb[par], x[bass.ds(n, 1)].rearrange("o (t p) d -> p (o t) d", p=P)).then_inc(x_in, 16)

            sp.dma_start(x_sb[0], x[0:1].rearrange("o (t p) d -> p (o t) d", p=P)).then_inc(x_in, 16)
            for n, w in enumerate((wq, wk, wv)):
                sp.dma_start(w_raw[:, n], w.rearrange("(c p) d -> p c d", p=P)).then_inc(const_in, 16)
            sp.dma_start(bqk[:], b_cols).then_inc(const_in, 16)
            sp.dma_start(bv_all[:], bv.rearrange("(o d) -> o d", o=1).broadcast_to([P, D])).then_inc(const_in, 16)
            sp.dma_start(cent_sb[:], cent.rearrange("(c p) e -> p c e", p=P)).then_inc(const_in, 16)
            load_k(0)
            load_v(0)
            load_k(1)
            load_v(1)

            def store_rows(b):
                sp.wait_ge(row_ok, b + 1)
                sp.wait_ge(norm_ok, QT * (b + 1))
                sp.wait_ge(gate_ok, b + 1)
                sp.dma_start(rows[bass.ds(b * S, S)].rearrange("(t p) w -> p t w", p=P), row_sb[:]).then_inc(rows_out, 16)

            def body(b, par):
                if not is_last(b):
                    load_x(b + 1, 1 - par)
                if not is_last(b):
                    load_k(b + 2)
                    load_v(b + 2)
                if not isinstance(b, int) or b > 0:
                    store_rows(b - 1)

            batches(sp, body)
            store_rows(B - 1)

            def expert(j):
                settle(sp, settled)
                return sp.value_load(meta[0:1, 0, bass.ds(j, 1)], min_val=0, max_val=E - 1)

            def load_w(j, par):
                e = expert(j) + B
                for n in range(2):
                    if some(2 * (j - 2)):
                        sp.wait_ge(w1_hi_ok, 2 * (j - 2))
                    if some(j - 2):
                        sp.wait_ge(w1_lo_v, j - 2)
                    if some(j - 2):
                        sp.wait_ge(w1_lo_p, j - 2)
                    sp.dma_start(w1_raw[par][n], keys_src[bass.ds(e, 1), n * P:(n + 1) * P].rearrange("o p k -> p (o k)")
                                 ).then_inc(w1_in[par], 16)
                for n in range(2):
                    if some(2 * (j - 2)):
                        sp.wait_ge(w2_hi_ok, 2 * (j - 2))
                    if some(j - 2):
                        sp.wait_ge(w2_lo_v, j - 2)
                    if some(j - 2):
                        sp.wait_ge(w2_lo_p, j - 2)
                    sp.dma_start(w2_raw[par][n], vals_src[bass.ds(e, 1), n * F // 2:(n + 1) * F // 2].rearrange(
                        "o (c p) d -> p (o c) d", p=P)).then_inc(w2_in[par], 16)

            def load_vec(j, par):
                if some(2 * (j - 1)):
                    sp.wait_ge(o_ok, 2 * (j - 1))
                e = expert(j) if not isinstance(j, int) or j > 0 else 0
                sp.dma_start(vec[par][:], vecs[bass.ds(e, 1)].rearrange("o p n -> (o p) n")).then_inc(vec_in[par], 16)
                sp.dma_start(b2_all[par], b2[bass.ds(e, 1)].broadcast_to([P, D])).then_inc(vec_in[par], 16)

            sp.wait_ge(aff_ps, B)
            load_vec(0, 0)
            for k in range(HALVES):
                sp.wait_ge(gathered[0][k], 16)
            sp.wait_ge(meta_ok, 1)
            sp.wait_ge(row_ok, B)
            sp.wait_ge(norm_ok, QT * B)
            load_w(1, 1)
            sp.wait_ge(ctx_hi_ok, NPIECE * (B + 1))
            sp.wait_ge(ctx_lo_ok, NPIECE * (B + 1))
            load_w(2, 0)

            def tile_body(j, par):
                load_vec(j + 1, 1 - par)
                if not isinstance(j, int) or j > 0:
                    load_w(j + 2, par)

            tiles(sp, tile_body)
            sp.wait_ge(rows_out, 16 * B)
            for k in range(HALVES):
                sp.wait_ge(stored[k], 16 * TILES)
            for loaded in (w1_in, w2_in):
                for par in range(2):
                    last = TILES + 1 - (TILES + 1 - par) % 2
                    sp.wait_ge(loaded[par], w_value(last, par))

        @block.gpsimd
        def _(pool):
            pool.memset(ident_in[:], 0.0).then_inc(made, 1)
            pool.memset(upto_in[:], 1.0).then_inc(made, 1)
            pool.memset(ones[:], 1.0).then_inc(made, 1)
            pool.memset(eps[:], LN_EPS).then_inc(made, 1)
            pool.memset(acc[:], 0.0).then_inc(made, 1)
            pool.memset(table[:], 0.0).then_inc(made, 1)
            pool.memset(row_sb[:], 0.0).then_inc(made, 1)
            kw = dict(allow_small_or_imprecise_dtypes=True)
            pool.iota(iota_f[:], pattern=[[1, P]], base=0, channel_multiplier=0, **kw).then_inc(made, 1)
            pool.iota(iota_e[:], pattern=[[0, QT], [1, E]], base=0, channel_multiplier=0, **kw).then_inc(made, 1)
            pool.iota(iota_r[:], pattern=[[0, QT], [1, RANKS]], base=0, channel_multiplier=0, **kw).then_inc(made, 1)
            pool.iota(part1[:], pattern=[[1, 1]], base=1, channel_multiplier=1, **kw).then_inc(made, 1)
            pool.iota(tile_no[:], pattern=[[1, QT], [0, E]], base=0, channel_multiplier=0, **kw).then_inc(made, 1)
            pool.iota(thr[:], pattern=[[0, E], [TILE, MAXT]], base=0, channel_multiplier=0, **kw).then_inc(made, 1)
            pool.iota(tile_j[:], pattern=[[1, META], [0, E - 1]], base=0, channel_multiplier=0, **kw).then_inc(made, 1)
            pool.wait_ge(made, 14)
            pool.affine_select(out=ident[:], in_=ident_in[:], compare_op=ALU.not_equal, fill=1.0,
                               base=0, pattern=[[-1, P]], channel_multiplier=1).then_inc(made2, 1)
            pool.affine_select(out=tri[:], in_=ones[:], compare_op=ALU.is_gt, fill=0.0,
                               base=0, pattern=[[1, P]], channel_multiplier=-1).then_inc(made2, 1)
            pool.affine_select(out=upto[:], in_=upto_in[:], compare_op=ALU.is_ge, fill=0.0,
                               base=0, pattern=[[1, E], [-1, E]], channel_multiplier=0).then_inc(made2, 1)

            def ctx_lo(n, par, piece):
                pool.wait_ge(ctx_hi_ok, NPIECE * n + piece + 1)
                if piece < 2:
                    args = k_lo[par][:, piece], k_raw[:, piece], k_hi[par][:, piece].bitcast(F32)
                else:
                    c = slice((piece - 2) * 4, (piece - 2) * 4 + 4)
                    args = v_lo[par][:, c], v_raw[:, c], v_hi[par][:, c].bitcast(F32)
                pool.tensor_tensor(*args, ALU.subtract).then_inc(ctx_lo_ok, 1)

            for piece in range(NPIECE):
                ctx_lo(0, 0, piece)

            def body(b, par):
                later = not isinstance(b, int) or b > 0
                ctx_lo(b + 1, 1 - par, 0)
                if later:
                    residual(b - 1, 1 - par)
                ctx_lo(b + 1, 1 - par, 1)
                ctx_lo(b + 1, 1 - par, 2)
                if later:
                    put_ids(b - 1)
                ctx_lo(b + 1, 1 - par, 3)

            def residual(b, par):
                pool.wait_ge(h_ok, QT * (b + 1))
                pool.wait_ge(rows_out, 16 * b)
                pool.tensor_tensor(row_sb[:, :, D:2 * D], x1[par][:], h_sb[:], ALU.add).then_inc(row_ok, 1)

            def put_ids(b):
                pool.wait_ge(id_ok, b + 1)
                pool.wait_ge(table_ps, b)
                for t in range(QT):
                    pool.tensor_tensor(
                        put[:, t], hot_id[:, t, :, :, None].broadcast_to([P, 2, E, RANKS]),
                        hi_hot[:, t, None, None, :].broadcast_to([P, 2, E, RANKS]), ALU.mult).then_inc(put_ok, 1)

            batches(pool, body)
            residual(B - 1, (B - 1) % 2)

            pool.wait_ge(ids_ok, 1)
            pool.wait_ge(rows_out, 16 * B)

            def gather_value(j, par):
                return 8 * (j - par) + 16

            def first_ids(j, par):
                if isinstance(j, int) and j == 0:
                    col = 0
                else:
                    col = pool.value_load(meta[0:1, 1, bass.ds(j, 1)], min_val=0, max_val=E * RANKS - HALVES)
                settle(pool, settled)
                if not isinstance(j, int) or j > 1:
                    for k in range(HALVES):
                        pool.wait_ge(gathered[par][k], gather_value(j, par) - 16)
                pool.tensor_copy(tok[par][:], ids[:, bass.ds(col, HALVES)]).then_inc(tok_ok, 1)

            def gather(j, par, k):
                if some(2 * (j - 2) + k + 1):
                    pool.wait_ge(o_ok, 2 * (j - 2) + k + 1)
                pool.wait_ge(tok_ok, j + 1)
                settle(pool, settled)
                pool.indirect_dma_start(
                    out=g[par][:, k, :], out_offset=None, in_=rows[:, :],
                    in_offset=bass.IndirectOffsetOnAxis(ap=tok[par][:, k:k + 1], axis=0),
                    bounds_check=TOKENS - 1, oob_is_err=False).then_inc(gathered[par][k], 16)

            def out_ids(j):
                col = pool.value_load(meta[0:1, 1, bass.ds(j, 1)], min_val=0, max_val=E * RANKS - HALVES)
                for k in range(HALVES):
                    if some(16 * j):
                        pool.wait_ge(stored[k], 16 * j)
                pool.tensor_copy(tok_out[:], ids[:, bass.ds(col, HALVES)]).then_inc(tok_out_ok, 1)

            def scatter(j, k):
                pool.wait_ge(tok_out_ok, j + 1)
                pool.wait_ge(o_ok, 2 * j + k + 1)
                settle(pool, settled)
                pool.indirect_dma_start(
                    out=out[:, :], out_offset=bass.IndirectOffsetOnAxis(ap=tok_out[:, k:k + 1], axis=0),
                    in_=o_sb[:, k, :], in_offset=None,
                    bounds_check=TOKENS - 1, oob_is_err=False).then_inc(stored[k], 16)

            first_ids(0, 0)
            gather(0, 0, 0)
            gather(0, 0, 1)
            pool.wait_ge(meta_ok, 1)
            first_ids(1, 1)
            gather(1, 1, 0)

            def tile_body(j, par):
                gather(j + 1, 1 - par, 1)
                if not isinstance(j, int) or j > 0:
                    scatter(j - 1, 0)
                    pool.wait_ge(w2_hi_ok, 2 * j - 1)
                    pool.tensor_tensor(w2_lo[par][1], w2_raw[par][1], w2_hi[par][1].bitcast(F32),
                                       ALU.subtract).then_inc(w2_lo_p, 1)
                    scatter(j - 1, 1)
                pool.wait_ge(w1_hi_ok, 2 * j + 1)
                pool.tensor_tensor(w1_lo[1 - par][:, 1], w1_raw[1 - par][1], w1_hi[1 - par][:, 1].bitcast(F32),
                                   ALU.subtract).then_inc(w1_lo_p, 1)
                out_ids(j)
                first_ids(j + 2, par)
                gather(j + 2, par, 0)

            tiles(pool, tile_body)
            scatter(TILES - 1, 0)
            scatter(TILES - 1, 1)
            for k in range(HALVES):
                for par in range(2):
                    last = TILES + 1 - k
                    last -= (last - par) % 2
                    pool.wait_ge(gathered[par][k], gather_value(last, par))

        @block.scalar
        def _(act):
            act.preload_act_table_set("natural_log_exp_and_others")
            def ln(kind, b):
                act.wait_ge(var_ok[kind], b + 1)
                act.activation(lnv[kind][:], ve[kind][:], ACT.Ln).then_inc(ln_act[kind], 1)
                act.wait_ge(ln_act[kind], 2 * b + 1)
                act.activation(y0[kind][:], lnv[kind][:], ACT.Exp, scale=-0.5).then_inc(ln_act[kind], 1)

            def ctx_hi(n, par, piece):
                if piece == 0:
                    act.wait_ge(k_in, 16 * (n + 1))
                    if some(KB * QT * (n - 1)):
                        act.wait_ge(scored, KB * QT * (n - 1))
                if piece == 2:
                    act.wait_ge(v_in, 16 * (n + 1))
                    if some(QT * (n - 1)):
                        act.wait_ge(pv_done, QT * (n - 1))
                if piece < 2:
                    args = k_hi[par][:, piece], k_raw[:, piece]
                else:
                    c = slice((piece - 2) * 4, (piece - 2) * 4 + 4)
                    args = v_hi[par][:, c], v_raw[:, c]
                act.activation(*args, ACT.Copy).then_inc(ctx_hi_ok, 1)

            def turned_x(n, c):
                act.wait_ge(x_turned, DC * n + c + 1)
                if some(NPROJ * n):
                    act.wait_ge(projected, NPROJ * n)
                act.activation(xt_hi[:, c], (ps_mb, ps_ma)[c][:], ACT.Copy).then_inc(xt_hi_ok, 1)

            def proj_hi(n, par, m):
                name, c = QKV_ORDER[m][0], int(QKV_ORDER[m][1])
                if name == "v":
                    act.wait_ge(v_sum_ok, 2 * n + c + 1)
                    if c == 0:
                        if some(QT * (n - 1)):
                            act.wait_ge(pv_done, QT * (n - 1))
                    act.activation(vn_hi[par][:, 2 * c:2 * c + 2], vn_f[:], ACT.Copy).then_inc(proj_hi_ok, 1)
                    return
                act.wait_ge(projected, NPROJ * n + m + 1)
                if m == 2:
                    if some(KB * QT * n):
                        act.wait_ge(scored, KB * QT * n)
                bank = proj_bank[m]
                dst, bias = (q_hi, 0) if name == "q" else (kn_hi, 1)
                act.activation(dst[:, c], bank[:], ACT.Identity, bias=bqk[:, bias, c:c + 1]).then_inc(proj_hi_ok, 1)

            def exps(b, par, t):
                act.wait_ge(max_ok, QT * b + t + 1)
                if some(KB * (QT * b + t)):
                    act.wait_ge(p_turned, KB * (QT * b + t))
                act.activation(probs[:], ps_s[:].rearrange("p a n -> p (a n)"), ACT.Exp, bias=neg_max[:, 0:1],
                               scale=SCALE, accum_out=sums[:, par, t:t + 1]).then_inc(exp_done, 1)

            def p_hi(b, t, n, bank):
                act.wait_ge(p_turned, KB * (QT * b + t) + n + 1)
                if n == 0:
                    if some(QT * b + t):
                        act.wait_ge(pv_done, QT * b + t)
                act.activation(pt_hi[:, GPB * n:GPB * n + GPB], bank[:].rearrange("p (g q) -> p g q", g=GPB),
                               ACT.Copy).then_inc(pt_hi_ok, 1)

            ln(0, 0)
            act.wait_ge(const_in, 16 * 6)
            act.activation(w_hi[:], w_raw, ACT.Copy).then_inc(w_hi_ok, 1)
            turned_x(0, 0)
            turned_x(0, 1)
            ctx_hi(0, 0, 0)
            ctx_hi(0, 0, 1)
            for m in range(NPROJ):
                proj_hi(0, 0, m)
                if m == 1:
                    ctx_hi(0, 0, 2)
                if m == 3:
                    ctx_hi(0, 0, 3)
            exps(0, 0, 0)

            def turned_h(b, c):
                act.wait_ge(h_turned, DC * b + c + 1)
                act.wait_ge(aff_ps, b)
                act.activation(ht[:, c], (ps_ma, ps_mb)[c][:], ACT.Copy).then_inc(ht_ok, 1)

            def gate(b):
                act.wait_ge(top_step.sem, top_step.per * b + 2)
                act.activation(ea[:], top[:, :, 0], ACT.Exp, scale=-1.0).then_inc(gate_exp, 1)

            def body(b, par):
                later = not isinstance(b, int) or b > 0
                for t in range(1, QT):
                    p_hi(b, t - 1, 0, ps_a)
                    p_hi(b, t - 1, 1, ps_b)
                    if not is_last(b) and t == 2:
                        ln(0, b + 1)
                    ctx_hi(b + 1, 1 - par, t - 1)
                    if later and t == 1:
                        ln(1, b - 1)
                    if later and t == 2:
                        turned_h(b - 1, 0)
                        turned_h(b - 1, 1)
                    if later and t == 3:
                        gate(b - 1)
                    p_hi(b, t - 1, 2, ps_a)
                    exps(b, par, t)
                if not is_last(b):
                    turned_x(b + 1, 0)
                    turned_x(b + 1, 1)
                    for m in range(NPROJ):
                        proj_hi(b + 1, 1 - par, m)
                p_hi(b, 3, 0, ps_a)
                p_hi(b, 3, 1, ps_b)
                if later:
                    ln(2, b - 1)
                if not is_last(b):
                    ctx_hi(b + 1, 1 - par, 3)
                p_hi(b, 3, 2, ps_a)
                if not is_last(b):
                    exps(b + 1, 1 - par, 0)
                else:
                    ctx_hi(b + 1, 1 - par, 3)

            batches(act, body)
            ln(1, B - 1)
            turned_h(B - 1, 0)
            turned_h(B - 1, 1)
            ln(2, B - 1)
            gate(B - 1)

            def expert_x(j, par):
                act.wait_ge(xe_turned, j + 1)
                act.wait_ge(vec_in[par], vec_value(j, par))
                if some(j):
                    act.wait_ge(xe_hi_ok, j)
                if some(j):
                    act.wait_ge(xe_lo_ok, j)
                for c in range(DC):
                    act.activation(xe[:, c], ps_mb[:, c * TILE:(c + 1) * TILE], ACT.Identity,
                                   bias=vec[par][:, DC + c:DC + c + 1], scale=vec[par][:, c:c + 1]).then_inc(xe_ok, 1)

            expert_x(0, 0)

            def w1_part(j, par, n):
                act.wait_ge(w1_in[par], w_value(j, par))
                if n == 1:
                    if some(FC // 2 * (j - 1)):
                        act.wait_ge(mm1_ok, FC // 2 * (j - 1))
                act.activation(w1_hi[par][:, n], w1_raw[par][n], ACT.Copy).then_inc(w1_hi_ok, 1)

            def w2_part(j, par, n):
                act.wait_ge(w2_in[par], w_value(j, par))
                if n == 1:
                    if some(HALVES * (j - 1)):
                        act.wait_ge(mm2_ok, HALVES * (j - 1))
                act.activation(w2_hi[par][n], w2_raw[par][n], ACT.Copy).then_inc(w2_hi_ok, 1)

            def hidden(j, par, n):
                act.wait_ge(mm1_ok, FC // 2 * j + n + 1)
                if some(FC // 2 * (j - 1) + n + 1):
                    act.wait_ge(h1_lo_ok, FC // 2 * (j - 1) + n + 1)
                for f in (2 * n, 2 * n + 1):
                    act.activation(h1[:, f], h_bank(n)[:, (f % 2) * TILE:(f % 2 + 1) * TILE], ACT.Relu,
                                   bias=vec[par][:, 2 * DC + f:2 * DC + f + 1]).then_inc(h1_ok, 1)

            def tile_body(j, par):
                hidden(j, par, 0)
                w1_part(j + 1, 1 - par, 1)
                hidden(j, par, 1)
                hidden(j, par, 2)
                w1_part(j + 1, 1 - par, 0)
                hidden(j, par, 3)
                expert_x(j + 1, 1 - par)
                w2_part(j + 1, 1 - par, 1)
                w2_part(j + 1, 1 - par, 0)

            tiles(act, tile_body)

        @block.vector
        def _(dve):
            def stats(kind, b, t, src):
                dve.bn_stats(st[kind][:, t], src).then_inc(stat_ok[kind], 1)

            def variance(kind, b):
                dve.wait_ge(stat_ok[kind], QT * (b + 1))
                settle(dve, settled)
                for t in range(QT):
                    ins = dve.bn_aggr(mv[kind][:, t], st[kind][:, t])
                ins.then_inc(aggr_ok[kind], 1)
                dve.wait_ge(aggr_ok[kind], b + 1)
                dve.tensor_scalar(ve[kind][:], mv[kind][:, :, 1], LN_EPS, None, ALU.add).then_inc(var_ok[kind], 1)

            def x_stats(n, par):
                dve.wait_ge(x_in, 16 * (n + 1))
                for t in range(QT):
                    stats(0, n, t, x_sb[par][:, t])
                variance(0, n)

            def x1_stats(b, par, t):
                dve.wait_ge(x1_ok, QT * b + t + 1)
                stats(1, b, t, x1[par][:, t])

            def h_stats(b, t):
                dve.wait_ge(h_ok, QT * b + t + 1)
                stats(2, b, t, h_sb[:, t])

            def refine(kind, b):
                s = rstd_step[kind]
                s.begin(b)
                dve.wait_ge(ln_act[kind], 2 * b + 2)
                s(dve, dve.tensor_tensor(ysq[kind][:], y0[kind][:], y0[kind][:], ALU.mult))
                s(dve, dve.tensor_tensor(ysq[kind][:], ysq[kind][:], ve[kind][:], ALU.mult))
                s(dve, dve.tensor_scalar(ysq[kind][:], ysq[kind][:], -0.5, 1.5, ALU.mult, ALU.add))
                s(dve, dve.tensor_tensor(rstd[kind][:], y0[kind][:], ysq[kind][:], ALU.mult))

            def norm(kind, src, dst, done):
                for t in range(QT):
                    dve.tensor_scalar(dst(t), src(t), mv[kind][:, t, 0:1], rstd[kind][:, t:t + 1],
                                      ALU.subtract, ALU.mult).then_inc(done, 1)

            def ln1(n, par):
                refine(0, n)
                if some(DC * n):
                    dve.wait_ge(x_turned, DC * n)
                norm(0, lambda t: x_sb[par][:, t], lambda t: xn[:, t], xn_ok)

            def ln2(b, par):
                refine(1, b)
                dve.wait_ge(h_turned, DC * b)
                dve.wait_ge(row_ok, b)
                norm(1, lambda t: x1[par][:, t], lambda t: h_sb[:, t], h_ok)

            def ln3(b):
                refine(2, b)
                dve.wait_ge(rows_out, 16 * b)
                norm(2, lambda t: h_sb[:, t], lambda t: row_sb[:, t, 0:D], norm_ok)

            def turned_x(n, c):
                dve.wait_ge(xt_hi_ok, DC * n + c + 1)
                dve.tensor_tensor(xt_lo[:, c], (ps_mb, ps_ma)[c][:], xt_hi[:, c].bitcast(F32), ALU.subtract).then_inc(xt_lo_ok, 1)

            def proj_sum(n, c):
                dve.wait_ge(projected, NPROJ * n + c + 1)
                if some(NPROJ * n + c):
                    dve.wait_ge(proj_lo_ok, NPROJ * n + c)
                dve.tensor_tensor(vn_f[:], proj_bank[c][:].rearrange("p (t d) -> p t d", t=2),
                                  bv_all[:, None, :].broadcast_to([P, 2, D]),
                                  ALU.add).then_inc(v_sum_ok, 1)

            def proj_lo(n, par, m):
                name, c = QKV_ORDER[m][0], int(QKV_ORDER[m][1])
                dve.wait_ge(proj_hi_ok, NPROJ * n + m + 1)
                if name == "v":
                    dve.tensor_tensor(vn_lo[par][:, 2 * c:2 * c + 2], vn_f[:],
                                      vn_hi[par][:, 2 * c:2 * c + 2].bitcast(F32), ALU.subtract).then_inc(proj_lo_ok, 1)
                    return
                bank = proj_bank[m]
                hi, lo, bias = (q_hi, q_lo, 0) if name == "q" else (kn_hi, kn_lo, 1)
                dve.scalar_tensor_tensor(out=lo[:, c], in0=bank[:], scalar=bqk[:, bias, c:c + 1],
                                         in1=hi[:, c].bitcast(F32), op0=ALU.add, op1=ALU.subtract).then_inc(proj_lo_ok, 1)

            def max_of(b, t, n):
                dve.wait_ge(scored, KB * (QT * b + t) + n + 1)
                ins = dve.tensor_reduce(mx3[:, n:n + 1], ps_s[:, n], AX.X, ALU.max)
                if n < KB - 1:
                    return
                max_steps(b, t, ins)

            def max_steps(b, t, ins):
                ins.then_inc(max_a, 1)
                dve.wait_ge(max_a, QT * b + t + 1)
                dve.tensor_reduce(mx1[:], mx3[:], AX.X, ALU.max).then_inc(max_step.sem, 1)
                dve.wait_ge(max_step.sem, QT * b + t + 1)
                if some(QT * b + t):
                    dve.wait_ge(exp_done, QT * b + t)
                dve.tensor_scalar(neg_max[:], mx1[:], -SCALE, None, ALU.mult).then_inc(max_ok, 1)

            def p_lo(b, t, n, bank):
                dve.wait_ge(pt_hi_ok, KB * (QT * b + t) + n + 1)
                c = slice(GPB * n, GPB * n + GPB)
                dve.tensor_tensor(pt_lo[:, c], bank[:].rearrange("p (g q) -> p g q", g=GPB), pt_hi[:, c].bitcast(F32),
                                  ALU.subtract).then_inc(pt_lo_ok, 1)

            def add_x(b, par, t):
                dve.wait_ge(pv_done, QT * b + t + 1)
                dve.reciprocal(rsum[:], sums[:, par, t:t + 1]).then_inc(rsum_ok, 1)
                dve.wait_ge(rsum_ok, QT * b + t + 1)
                if t == 0:
                    if some(b - 1):
                        dve.wait_ge(row_ok, b - 1)
                dve.scalar_tensor_tensor(out=x1[par][:, t], in0=ps_pv[:, 0:D], scalar=rsum[:, 0:1], in1=x_sb[par][:, t],
                                         op0=ALU.mult, op1=ALU.add).then_inc(x1_ok, 1)

            def top_expert(b):
                s = top_step
                s.begin(b)
                dve.wait_ge(aff_ps, b + 1)
                s(dve, dve.tensor_copy(aff[:].rearrange("p t e -> p (t e)"), ps_aff))
                settle(dve, settled)
                for t in range(QT):
                    ins = dve.max(top[:, t], aff[:, t])
                s(dve, ins)
                settle(dve, settled)
                for t in range(QT):
                    ins = dve.max_index(top_i[:, t], top[:, t], aff[:, t])
                s(dve, ins)
                s(dve, dve.tensor_copy(top_f[:], top_i[:, :, 0]))
                s(dve, dve.tensor_tensor(hot[:], iota_e[:], top_f[:, :, None].broadcast_to([P, QT, E]), ALU.is_equal))

            def gates(b):
                dve.wait_ge(gate_exp, b + 1)
                dve.tensor_scalar(ea1[:], ea[:], 1.0, None, ALU.add).then_inc(gate_step, 1)
                dve.wait_ge(gate_step, b + 1)
                dve.wait_ge(rows_out, 16 * b)
                dve.reciprocal(row_sb[:, :, 2 * D], ea1[:]).then_inc(gate_ok, 1)

            def read_ranks(b):
                s = rank_step
                s.begin(b)
                dve.wait_ge(rank_ps, b + 1)
                s.count(dve.tensor_tensor(rank_e[:], ps_rank.rearrange("p (t e) -> p t e", t=QT), hot[:], ALU.mult))

            def ranks(b):
                s = rank_step
                dve.wait_ge(s.sem, s.per * b + 1)
                s(dve, dve.tensor_reduce(rank_f[:], rank_e[:], AX.X, ALU.add))
                s(dve, dve.tensor_copy(rank_i[:], rank_f[:]))
                s.count(dve.tensor_scalar(lohi_i[:, 0], rank_i[:], P - 1, None, ALU.bitwise_and))
                s(dve, dve.tensor_scalar(lohi_i[:, 1], rank_i[:], 7, None, ALU.logical_shift_right))
                s(dve, dve.tensor_copy(lohi[:], lohi_i[:]))
                dve.wait_ge(table_ps, b)
                for t in range(QT):
                    ins = dve.tensor_scalar(lo_hot[:, t], iota_f[:], lohi[:, 0, t:t + 1], None, ALU.is_equal)
                ins.then_inc(lo_hot_ok, 1)
                dve.wait_ge(put_ok, QT * b)
                dve.tensor_tensor(hi_hot[:], iota_r[:], lohi[:, 1, :, None].broadcast_to([P, QT, RANKS]), ALU.is_equal)
                dve.tensor_scalar(hot_id[:, :, 0], hot[:], part1[:, 0:1], None, ALU.mult)
                dve.tensor_tensor(hot_id[:, :, 1], hot[:], tile_no[:], ALU.mult).then_inc(id_ok, 1)
                if is_last(b):
                    return
                dve.tensor_reduce(hot_sum[:], hot[:].rearrange("p t e -> p e t"), AX.X, ALU.add).then_inc(sum_step, 1)
                dve.wait_ge(id_ok, b + 1)
                dve.tensor_scalar(tile_no[:], tile_no[:], float(QT), None, ALU.add)
                dve.wait_ge(sum_step, 2 * b + 1)
                dve.tensor_tensor(acc[:], acc[:], hot_sum[:], ALU.add).then_inc(sum_step, 1)

            def put_ids(b):
                dve.wait_ge(id_ok, b + 1)
                dve.wait_ge(table_ps, b)
                for t in range(QT):
                    dve.tensor_tensor(
                        put[:, t], hot_id[:, t, :, :, None].broadcast_to([P, 2, E, RANKS]),
                        hi_hot[:, t, None, None, :].broadcast_to([P, 2, E, RANKS]), ALU.mult).then_inc(put_ok, 1)

            def add_table(b):
                dve.wait_ge(table_ps, b + 1)
                dve.wait_ge(table_ok, b)
                dve.tensor_tensor(table[:].rearrange("p a n -> p (a n)"), table[:].rearrange("p a n -> p (a n)"), ps_ma[:],
                                  ALU.add).then_inc(table_ok, 1)

            x_stats(0, 0)
            ln1(0, 0)
            dve.wait_ge(w_hi_ok, 1)
            dve.tensor_tensor(w_lo[:], w_raw, w_hi[:].bitcast(F32), ALU.subtract).then_inc(w_lo_ok, 1)
            turned_x(0, 0)
            turned_x(0, 1)
            for c in range(2):
                proj_sum(0, c)
                proj_lo(0, 0, c)
            for m in range(2, NPROJ):
                proj_lo(0, 0, m)
            dve.wait_ge(made, 14)
            dve.wait_ge(made2, 3)
            for n in range(KB):
                max_of(0, 0, n)

            def body(b, par):
                later = not isinstance(b, int) or b > 0
                for t in range(1, QT):
                    if t > 1:
                        add_x(b, par, t - 2)
                    elif later:
                        add_x(b - 1, 1 - par, QT - 1)
                    p_lo(b, t - 1, 0, ps_a)
                    if t > 1:
                        x1_stats(b, par, t - 2)
                    elif later:
                        x1_stats(b - 1, 1 - par, QT - 1)
                    p_lo(b, t - 1, 1, ps_b)
                    if later and t == 1:
                        variance(1, b - 1)
                    max_of(b, t, 0)
                    if later and t == 3:
                        read_ranks(b - 1)
                    max_of(b, t, 1)
                    p_lo(b, t - 1, 2, ps_a)
                    max_of(b, t, 2)
                    if later and t == 1:
                        ln2(b - 1, 1 - par)
                    if not is_last(b) and t == 1:
                        x_stats(b + 1, 1 - par)
                    if later and t == 2:
                        top_expert(b - 1)
                    if not is_last(b) and t == 2:
                        ln1(b + 1, 1 - par)
                if not is_last(b):
                    turned_x(b + 1, 0)
                    turned_x(b + 1, 1)
                if later:
                    ranks(b - 1)
                add_x(b, par, 2)
                if not is_last(b):
                    for c in range(2):
                        proj_sum(b + 1, c)
                        if c == 0:
                            x1_stats(b, par, 2)
                        proj_lo(b + 1, 1 - par, c)
                    for m in range(2, NPROJ):
                        proj_lo(b + 1, 1 - par, m)
                        if later:
                            h_stats(b - 1, m - 2)
                else:
                    x1_stats(b, par, 2)
                    for t in range(QT):
                        h_stats(b - 1, t)
                if later:
                    variance(2, b - 1)
                p_lo(b, 3, 0, ps_a)
                p_lo(b, 3, 1, ps_b)
                if not is_last(b):
                    max_of(b + 1, 0, 0)
                    max_of(b + 1, 0, 1)
                p_lo(b, 3, 2, ps_a)
                if not is_last(b):
                    max_of(b + 1, 0, 2)
                if later:
                    ln3(b - 1)
                    gates(b - 1)
                    add_table(b - 1)

            batches(dve, body)
            par = (B - 1) % 2
            add_x(B - 1, par, QT - 1)
            x1_stats(B - 1, par, QT - 1)
            variance(1, B - 1)
            ln2(B - 1, par)
            for t in range(QT):
                h_stats(B - 1, t)
            variance(2, B - 1)
            ln3(B - 1)
            top_expert(B - 1)
            read_ranks(B - 1)
            ranks(B - 1)
            put_ids(B - 1)
            gates(B - 1)

            step = [0]

            def link(ins):
                step[0] += 1
                ins.then_inc(meta_step, 1)
                dve.wait_ge(meta_step, step[0])

            dve.wait_ge(cnt_ps, 1)
            link(dve.tensor_copy(cnt[:], ps_cnt))
            link(dve.tensor_tensor(over[:], cnt[:, :, None].broadcast_to([P, E, MAXT]), thr[:], ALU.is_gt))
            link(dve.tensor_reduce(tl[:], over[:], AX.X, ALU.add))
            link(dve.tensor_scalar(tl1[:], tl[:], 1.0, None, ALU.max))
            link(dve.tensor_tensor(tlu[:], upto[:], tl1[:, None, :].broadcast_to([P, E, E]), ALU.mult))
            link(dve.tensor_reduce(ends[:], tlu[:], AX.X, ALU.add))
            add_table(B - 1)
            dve.wait_ge(table_ok, B)
            link(dve.scalar_tensor_tensor(out=ids_f, in0=table[:, 1], scalar=float(P), in1=table[:, 0],
                                          op0=ALU.mult, op1=ALU.add))
            link(dve.tensor_scalar(empty, ids_f, 0.0, float(NO_TOKEN), ALU.is_equal, ALU.mult))
            dve.scalar_tensor_tensor(out=ids[:], in0=ids_f, scalar=-1.0, in1=empty,
                                     op0=ALU.add, op1=ALU.add).then_inc(ids_ok, 1)
            link(dve.tensor_tensor(past[:], tile_j[:], ends[:, None, 0:E - 1].broadcast_to([P, META, E - 1]), ALU.is_ge))
            link(dve.tensor_tensor(past_t[:], past[:], tl1[:, None, 0:E - 1].broadcast_to([P, META, E - 1]), ALU.mult))
            dve.tensor_reduce(meta_f[:, 0], past[:], AX.X, ALU.add)
            link(dve.tensor_reduce(start_f[:], past_t[:], AX.X, ALU.add))
            link(dve.tensor_tensor(start_f[:], tile_j[:, :, 0], start_f[:], ALU.subtract))
            link(dve.tensor_scalar(start_f[:], start_f[:], float(HALVES), None, ALU.mult))
            link(dve.scalar_tensor_tensor(out=meta_f[:, 1], in0=meta_f[:, 0], scalar=float(RANKS), in1=start_f[:],
                                          op0=ALU.mult, op1=ALU.add))
            link(dve.tensor_scalar(meta_f[:, 1], meta_f[:, 1], float(E * RANKS - HALVES), None, ALU.min))
            dve.tensor_copy(meta[:], meta_f[:]).then_inc(meta_ok, 1)

            def expert_x(j, par):
                dve.wait_ge(xe_ok, DC * (j + 1))
                if some(FC // 2 * (j - 1)):
                    dve.wait_ge(mm1_ok, FC // 2 * (j - 1))
                dve.tensor_copy(xe_hi[par], xe).then_inc(xe_hi_ok, 1)
                dve.wait_ge(xe_hi_ok, j + 1)
                dve.tensor_tensor(xe_lo[par], xe, xe_hi[par].bitcast(F32), ALU.subtract).then_inc(xe_lo_ok, 1)

            expert_x(0, 0)

            def store_tile(j, par, k):
                dve.wait_ge(mm2_ok, HALVES * j + k + 1)
                dve.wait_ge(vec_in[par], vec_value(j, par))
                dve.tensor_tensor(y_b[:, k], y_banks[k][:, 0:D], b2_all[par], ALU.add).then_inc(y_read, 1)
                dve.wait_ge(y_read, HALVES * j + k + 1)
                if some(16 * j):
                    dve.wait_ge(stored[k], 16 * j)
                dve.wait_ge(gathered[par][k], 8 * (j - par) + 16)
                dve.scalar_tensor_tensor(out=o_sb[:, k], in0=y_b[:, k], scalar=g[par][:, k, 2 * D:2 * D + 1],
                                         in1=g[par][:, k, D:2 * D], op0=ALU.mult, op1=ALU.add).then_inc(o_ok, 1)

            def tile_body(j, par):
                if not isinstance(j, int) or j > 0:
                    store_tile(j - 1, 1 - par, 1)
                    dve.wait_ge(w2_hi_ok, 2 * j)
                    dve.tensor_tensor(w2_lo[par][0], w2_raw[par][0], w2_hi[par][0].bitcast(F32),
                                      ALU.subtract).then_inc(w2_lo_v, 1)
                for n in range(FC // 2):
                    c = slice(2 * n, 2 * n + 2)
                    dve.wait_ge(h1_ok, FC * j + 2 * n + 2)
                    if n == 0 and some(HALVES * j):
                        dve.wait_ge(mm2_ok, HALVES * j)
                    dve.tensor_copy(h1_hi[:, c], h1[:, c]).then_inc(h1_hi_ok, 1)
                    dve.wait_ge(h1_hi_ok, FC // 2 * j + n + 1)
                    dve.tensor_tensor(h1_lo[:, c], h1[:, c], h1_hi[:, c].bitcast(F32), ALU.subtract).then_inc(h1_lo_ok, 1)
                dve.wait_ge(w1_hi_ok, 2 * (j + 1))
                dve.tensor_tensor(w1_lo[1 - par][:, 0], w1_raw[1 - par][0], w1_hi[1 - par][:, 0].bitcast(F32),
                                  ALU.subtract).then_inc(w1_lo_v, 1)
                expert_x(j + 1, 1 - par)
                store_tile(j, par, 0)

            tiles(dve, tile_body)
            store_tile(TILES - 1, (TILES - 1) % 2, 1)

        @block.tensor
        def _(pe):
            pe.wait_ge(made2, 3)

            def three(out_ap, ahi, alo, bhi, blo, first, last):
                pe.matmul(out_ap, ahi, bhi, start=first, stop=False)
                pe.matmul(out_ap, ahi, blo, start=False, stop=False)
                return pe.matmul(out_ap, alo, bhi, start=False, stop=last)

            def turn_x(n, c):
                if c == 0:
                    if some(DC * (n - 1)):
                        pe.wait_ge(ht_ok, DC * (n - 1))
                elif not isinstance(n, int) or n > 1:
                    pe.wait_ge(rank_step.sem, rank_step.per * (n - 2) + 1)
                for t in range(QT):
                    pe.wait_ge(xn_ok, QT * n + t + 1)
                    ins = pe.transpose((ps_mb, ps_ma)[c][:, t * P:(t + 1) * P], xn[:, t, c * P:(c + 1) * P], ident[:])
                ins.then_inc(x_turned, 1)

            def project(n, m):
                name, c = QKV_ORDER[m][0], int(QKV_ORDER[m][1])
                bank = proj_bank[m]
                if m == 0:
                    pe.wait_ge(xt_lo_ok, DC * (n + 1))
                if m == 2:
                    if some(KB * (QT * n - 1)):
                        pe.wait_ge(pt_lo_ok, KB * (QT * n - 1))
                if m >= 4:
                    pe.wait_ge(v_sum_ok, 2 * n + m - 3)
                if name == "v":
                    for u in range(2):
                        t = 2 * c + u
                        for k in range(DC):
                            ins = three(bank[:, u * D:(u + 1) * D], xt_hi[:, k, t * P:(t + 1) * P], xt_lo[:, k, t * P:(t + 1) * P],
                                        w_hi[:, 2, k], w_lo[:, 2, k], k == 0, k == DC - 1)
                else:
                    w = "qk".index(name)
                    for k in range(DC):
                        e = slice(c * P, (c + 1) * P)
                        ins = three(bank[:], w_hi[:, w, k, e], w_lo[:, w, k, e], xt_hi[:, k], xt_lo[:, k], k == 0, k == DC - 1)
                ins.then_inc(projected, 1)

            def score(b, par, t, n):
                if n == 0:
                    if some(QT * b + t):
                        pe.wait_ge(exp_done, QT * b + t)
                    if t == 0:
                        pe.wait_ge(proj_lo_ok, NPROJ * b + 4)
                        pe.wait_ge(ctx_lo_ok, NPIECE * b + 2)
                if n == KB - 1 and t == 0:
                    pe.wait_ge(proj_lo_ok, NPROJ * (b + 1))
                for k in range(DC):
                    q = q_hi[:, k, t * P:(t + 1) * P], q_lo[:, k, t * P:(t + 1) * P]
                    if n < KB - 1:
                        kk = k_hi[par][:, k, n * BANK:(n + 1) * BANK], k_lo[par][:, k, n * BANK:(n + 1) * BANK]
                    else:
                        kk = kn_hi[:, k], kn_lo[:, k]
                    ins = three(ps_s[:, n], *q, *kk, k == 0, k == DC - 1)
                ins.then_inc(scored, 1)

            def turn_p(b, t, n, bank):
                if n == 0:
                    pe.wait_ge(exp_done, QT * b + t + 1)
                    if some(KB * (QT * b + t)):
                        pe.wait_ge(pt_lo_ok, KB * (QT * b + t))
                    if t == QT - 1 and not is_last(b):
                        pe.wait_ge(proj_lo_ok, NPROJ * (b + 1) + 4)
                if n == KB - 1:
                    pe.wait_ge(pt_lo_ok, KB * (QT * b + t) + 1)
                for u in range(GPB):
                    c = GPB * n + u
                    ins = pe.transpose(bank[:, u * P:(u + 1) * P], probs[:, c * P:(c + 1) * P], ident[:])
                ins.then_inc(p_turned, 1)

            def attend(b, par, t):
                if some(QT * b + t):
                    pe.wait_ge(x1_ok, QT * b + t)
                for c in range(KC):
                    if c % GPB == 0:
                        pe.wait_ge(pt_lo_ok, KB * (QT * b + t) + c // GPB + 1)
                    if t == 0 and c == 0:
                        pe.wait_ge(ctx_lo_ok, NPIECE * (b + 1))
                        pe.wait_ge(proj_lo_ok, NPROJ * (b + 1))
                    v = (v_hi[par][:, c], v_lo[par][:, c]) if c < CC else (vn_hi[par][:, c - CC], vn_lo[par][:, c - CC])
                    ins = three(ps_pv[:, 0:D], pt_hi[:, c], pt_lo[:, c], *v, c == 0, c == KC - 1)
                ins.then_inc(pv_done, 1)

            def turn_h(b, c):
                bank = (ps_ma, ps_mb)[c]
                if c == 0:
                    pe.wait_ge(proj_lo_ok, NPROJ * min_b(b + 2))
                    pe.wait_ge(table_ok, b)
                for t in range(QT):
                    pe.wait_ge(h_ok, QT * b + t + 1)
                    ins = pe.transpose(bank[:, t * P:(t + 1) * P], h_sb[:, t, c * P:(c + 1) * P], ident[:])
                ins.then_inc(h_turned, 1)

            def min_b(n):
                return min(n, B) if isinstance(n, int) else n

            def affinities(b):
                pe.wait_ge(ht_ok, DC * (b + 1))
                for t in range(QT):
                    for k in range(DC):
                        ins = pe.matmul(ps_aff[:, t * E:(t + 1) * E], ht[:, k, t * P:(t + 1) * P], cent_sb[:, k],
                                        start=(k == 0), stop=(k == DC - 1))
                ins.then_inc(aff_ps, 1)

            def rank(b):
                pe.wait_ge(top_step.sem, top_step.done(b))
                pe.wait_ge(sum_step, 2 * b)
                pe.matmul(ps_rank, tri[:], hot[:].rearrange("p t e -> p (t e)"), start=True, stop=False)
                for t in range(QT - 1):
                    n = QT - 1 - t
                    pe.matmul(ps_rank[:, (t + 1) * E:QT * E].rearrange("p (n e) -> p n e", n=n), ones[:],
                              hot[:, t, None, :].broadcast_to([P, n, E]), start=False, stop=False)
                pe.matmul(ps_rank.rearrange("p (n e) -> p n e", n=QT), ones[:],
                          acc[:, None, :].broadcast_to([P, QT, E]), start=False, stop=True).then_inc(rank_ps, 1)

            def fill_table(b):
                pe.wait_ge(proj_lo_ok, NPROJ * min_b(b + 2))
                pe.wait_ge(lo_hot_ok, b + 1)
                pe.wait_ge(id_ok, b + 1)
                for t in range(QT):
                    pe.wait_ge(put_ok, QT * b + t + 1)
                    ins = pe.matmul(ps_ma[:], lo_hot[:, t], put[:, t].rearrange("p a e r -> p (a e r)"),
                                    start=(t == 0), stop=(t == QT - 1))
                ins.then_inc(table_ps, 1)

            turn_x(0, 0)
            turn_x(0, 1)
            pe.wait_ge(w_lo_ok, 1)
            for m in range(NPROJ):
                project(0, m)
            for n in range(KB):
                score(0, 0, 0, n)

            def body(b, par):
                later = not isinstance(b, int) or b > 0
                for t in range(1, QT):
                    turn_p(b, t - 1, 0, ps_a)
                    turn_p(b, t - 1, 1, ps_b)
                    score(b, par, t, 0)
                    if later and t == 2:
                        turn_h(b - 1, 0)
                        turn_h(b - 1, 1)
                    if later and t == 3:
                        rank(b - 1)
                    score(b, par, t, 1)
                    turn_p(b, t - 1, 2, ps_a)
                    score(b, par, t, 2)
                    if later and t == 2:
                        affinities(b - 1)
                    if not is_last(b) and t == 3:
                        turn_x(b + 1, 0)
                        turn_x(b + 1, 1)
                    attend(b, par, t - 1)
                if not is_last(b):
                    for m in range(NPROJ):
                        project(b + 1, m)
                turn_p(b, 3, 0, ps_a)
                turn_p(b, 3, 1, ps_b)
                if not is_last(b):
                    score(b + 1, 1 - par, 0, 0)
                    score(b + 1, 1 - par, 0, 1)
                turn_p(b, 3, 2, ps_a)
                if not is_last(b):
                    score(b + 1, 1 - par, 0, 2)
                    if later:
                        fill_table(b - 1)
                    attend(b, par, 3)
                else:
                    attend(b, par, 3)
                    fill_table(b - 1)

            batches(pe, body)
            turn_h(B - 1, 0)
            turn_h(B - 1, 1)
            affinities(B - 1)
            rank(B - 1)
            for t in range(QT):
                pe.matmul(ps_cnt, ones[:], hot[:, t], start=(t == 0), stop=False)
            pe.matmul(ps_cnt, ones[:], acc[:], start=False, stop=True).then_inc(cnt_ps, 1)
            fill_table(B - 1)

            def turn_rows(j, par):
                for k in range(HALVES):
                    pe.wait_ge(gathered[par][k], 8 * (j - par) + 16)
                if some(DC * j):
                    pe.wait_ge(xe_ok, DC * j)
                for c in range(DC):
                    for k in range(HALVES):
                        ins = pe.transpose(ps_mb[:, c * TILE + k * P:c * TILE + (k + 1) * P],
                                           g[par][:, k, c * P:(c + 1) * P], ident[:])
                ins.then_inc(xe_turned, 1)

            turn_rows(0, 0)

            def tile_body(j, par):
                pe.wait_ge(xe_lo_ok, j + 1)
                pe.wait_ge(xe_hi_ok, j + 1)
                if some(2 * j):
                    pe.wait_ge(w1_hi_ok, 2 * j)
                if some(j):
                    pe.wait_ge(w1_lo_v, j)
                if some(j):
                    pe.wait_ge(w1_lo_p, j)
                if isinstance(j, int) and j == 0:
                    pe.wait_ge(ctx_lo_ok, NPIECE * (B + 1))
                for f in range(FC):
                    if f % 2 == 0:
                        if some(FC * (j - 1) + f + 2):
                            pe.wait_ge(h1_ok, FC * (j - 1) + f + 2)
                    fs = slice(f * P, (f + 1) * P)
                    for k in range(DC):
                        ins = three(h_bank(f // 2)[:, (f % 2) * TILE:(f % 2 + 1) * TILE], w1_hi[par][:, k, fs],
                                    w1_lo[par][:, k, fs], xe_hi[par][:, k], xe_lo[par][:, k], k == 0, k == DC - 1)
                    if f % 2:
                        ins.then_inc(mm1_ok, 1)
                turn_rows(j + 1, 1 - par)
                for k in range(HALVES):
                    ks = slice(k * P, (k + 1) * P)
                    if some(HALVES * (j - 1) + k + 1):
                        pe.wait_ge(y_read, HALVES * (j - 1) + k + 1)
                    if k == 0:
                        if some(2 * j):
                            pe.wait_ge(w2_hi_ok, 2 * j)
                        if some(j):
                            pe.wait_ge(w2_lo_v, j)
                    for f in range(FC):
                        if k == 0 and f % 2 == 0:
                            pe.wait_ge(h1_lo_ok, FC // 2 * j + f // 2 + 1)
                            pe.wait_ge(h1_hi_ok, FC // 2 * j + f // 2 + 1)
                        if k == 0 and f == FC // 2:
                            if some(j):
                                pe.wait_ge(w2_lo_p, j)
                        part, c = divmod(f, FC // 2)
                        ins = three(y_banks[k][:, 0:D], h1_hi[:, f, ks], h1_lo[:, f, ks],
                                    w2_hi[par][part][:, c], w2_lo[par][part][:, c], f == 0, f == FC - 1)
                    ins.then_inc(mm2_ok, 1)

            tiles(pe, tile_body)


def kernel(x, ctx_1024, L0_xattn_Wq, L0_xattn_bq, L0_xattn_Wk, L0_xattn_bk, L0_xattn_Wv, L0_xattn_bv,
           L0_ffn_centroids, L0_ffn_ln_g, L0_ffn_ln_b, L0_ffn_w1, L0_ffn_b1, L0_ffn_w2, L0_ffn_b2):
    import numpy as np
    import concourse.bacc as bacc
    from concourse import mybir as mb
    from concourse.bass_utils import run_bass_kernel_spmd

    def a(v):
        return np.asarray(v)

    def columns(v):
        return a(v).reshape(E, -1, P).transpose(0, 2, 1)

    data = {
        "x": a(x),
        "keys_src": np.concatenate([a(ctx_1024).transpose(0, 2, 1), a(L0_ffn_w1).transpose(0, 2, 1)]),
        "vals_src": np.concatenate([a(ctx_1024), a(L0_ffn_w2).transpose(0, 2, 1)]),
        "wq": a(L0_xattn_Wq).T, "wk": a(L0_xattn_Wk).T, "wv": a(L0_xattn_Wv).T,
        "b_cols": np.stack([a(v).reshape(DC, P).T for v in (L0_xattn_bq, L0_xattn_bk)], axis=1), "bv": a(L0_xattn_bv),
        "cent": a(L0_ffn_centroids).T,
        "vecs": np.concatenate([columns(L0_ffn_ln_g), columns(L0_ffn_ln_b), columns(L0_ffn_b1)], axis=2),
        "b2": a(L0_ffn_b2),
    }
    nc = bacc.Bacc("TRN2", target_bir_lowering=False, num_devices=1)
    arrays, args = {}, []
    for name, v in data.items():
        v = np.ascontiguousarray(v)
        arrays[f"in_{name}"] = v
        args.append(nc.dram_tensor(f"in_{name}", v.shape, mb.dt.from_np(v.dtype), kind="ExternalInput").ap())
    args.append(nc.dram_tensor("out_0", (TOKENS, D), mb.dt.float32, kind="ExternalOutput").ap())
    xattn_experts(nc, *args)
    r = run_bass_kernel_spmd(nc, [arrays], core_ids=[0])
    return r.results[0]["out_0"].reshape(B, S, D)
```

```python
from contextlib import ExitStack

import concourse.bass as bass
from concourse import mybir

P = 128
B, S, D = 8, 512, 256
K_CTX = 1024
KEYS = K_CTX + S
DC = D // P
QT = S // P
KC = KEYS // P
CC = K_CTX // P
BANK = 512
KB = KEYS // BANK
GPB = BANK // P
TOKENS = B * S
E, F = 8, 1024
FC = F // P
TILE = 256
HALVES = TILE // P
TILES = TOKENS // TILE + E - 1
RANKS = TOKENS // P
MAXT = TOKENS // TILE
META = TILES + 2
GATE, REST = D, D + 4
ROW = REST + D
NO_TOKEN = 2 * TOKENS
LN_EPS = 1e-5
SCALE = 64 ** -0.5

ALU = mybir.AluOpType
ACT = mybir.ActivationFunctionType
AX = mybir.AxisListType
F32 = mybir.dt.float32
F32R = mybir.dt.float32r
BF16 = mybir.dt.bfloat16
I32 = mybir.dt.int32
U32 = mybir.dt.uint32

QKV_ORDER = ("v0", "v1", "q0", "q1", "k0", "k1")
NPROJ = len(QKV_ORDER)
W_ORDER = (2, 0, 1)
NPIECE = 4


class Steps:

    def __init__(self, sem, per):
        self.sem, self.per = sem, per

    def begin(self, b):
        self.b, self.n = b, 0

    def __call__(self, eng, ins):
        self.n += 1
        assert self.n <= self.per
        ins.then_inc(self.sem, 1)
        eng.wait_ge(self.sem, self.b * self.per + self.n)

    def count(self, ins):
        self.n += 1
        ins.then_inc(self.sem, 1)

    def done(self, b):
        return (b + 1) * self.per


def some(count):
    return not isinstance(count, int) or count > 0


def settle(eng, sem):
    eng.sem_inc(sem, 1)


def xattn_experts(nc, x, keys_src, vals_src, wq, wk, wv, b_cols, bv, cent, vecs, b2, out):
    rows = nc.dram_tensor("rows", [TOKENS, ROW], F32, kind="Internal").ap()

    ctx = ExitStack()
    with ctx:
        def sb(name, shape, dt=F32):
            return ctx.enter_context(nc.sbuf_tensor(name, shape, dt))

        def sem(name):
            return ctx.enter_context(nc.semaphore(name))

        ps_s = ctx.enter_context(nc.psum_tensor("ps_s", [P, KB, BANK], F32))
        ps_a, ps_b, ps_pv, ps_ma, ps_mb = [
            ctx.enter_context(nc.psum_tensor(n, [P, BANK], F32))
            for n in ("ps_a", "ps_b", "ps_pv", "ps_ma", "ps_mb")]

        ident = sb("ident", [P, P])
        ident_in = sb("ident_in", [P, P])
        tri = sb("tri", [P, P], BF16)
        ones = sb("ones", [P, P], BF16)
        iota_f = sb("iota_f", [P, P])
        iota_e = sb("iota_e", [P, QT, E])
        iota_r = sb("iota_r", [P, QT, RANKS])
        tok_no = sb("tok_no", [P, QT])
        thr = sb("thr", [P, E, MAXT])
        upto = sb("upto", [P, E, E])
        upto_in = sb("upto_in", [P, E, E])
        tile_j = sb("tile_j", [P, META, E - 1])
        w_hi = sb("w_hi", [P, 3, DC, D], F32R)
        w_lo = sb("w_lo", [P, 3, DC, D], F32R)
        bqk = sb("bqk", [P, 2, DC])
        bv_all = sb("bv_all", [P, D])
        cent_sb = sb("cent_sb", [P, DC, E])

        k_raw = sb("k_raw", [P, DC, K_CTX])
        v_raw = sb("v_raw", [P, CC, D])
        k_hi = [sb(f"k_hi{i}", [P, DC, K_CTX], F32R) for i in range(2)]
        k_lo = [sb(f"k_lo{i}", [P, DC, K_CTX], F32R) for i in range(2)]
        v_hl = [sb(f"v_hl{i}", [P, CC, 2, D], F32R) for i in range(2)]
        v_hi, v_lo = [[v[:, :, n] for v in v_hl] for n in range(2)]
        kn_hi = sb("kn_hi", [P, DC, S], F32R)
        kn_lo = sb("kn_lo", [P, DC, S], F32R)
        vn_hl = [sb(f"vn_hl{i}", [P, QT, 2, D], F32R) for i in range(2)]
        vn_hi, vn_lo = [[v[:, :, n] for v in vn_hl] for n in range(2)]
        vn_f = sb("vn_f", [P, 2, D])
        q_hi = sb("q_hi", [P, DC, S], F32R)
        q_lo = sb("q_lo", [P, DC, S], F32R)
        x_both = sb("x_both", [P, 2 * QT, D])
        x_sb = [x_both[:, i * QT:(i + 1) * QT] for i in range(2)]
        xn = sb("xn", [P, QT, D])
        xt_hi = sb("xt_hi", [P, DC, S], F32R)
        xt_lo = sb("xt_lo", [P, DC, S], F32R)
        probs = sb("probs", [P, KEYS])
        w_raw = probs[:].rearrange("p (a c d) -> p a c d", a=3, c=DC)
        pt_hi = sb("pt_hi", [P, KC, P], F32R)
        pt_lo = sb("pt_lo", [P, KC, P], F32R)
        x1 = [sb(f"x1_{i}", [P, QT, D]) for i in range(2)]
        mx3 = sb("mx3", [P, KB])
        mx1 = sb("mx1", [P, 1])
        neg_max = sb("neg_max", [P, 1])
        sums = sb("sums", [P, 2, QT])
        rsum = sb("rsum", [P, 1])

        st = [sb(f"st{i}", [P, QT, 6]) for i in range(3)]
        mv = [sb(f"mv{i}", [P, QT, 2]) for i in range(3)]
        ve = [sb(f"ve{i}", [P, QT]) for i in range(3)]
        lnv = [sb(f"lnv{i}", [P, QT]) for i in range(3)]
        y0 = [sb(f"y0{i}", [P, QT]) for i in range(3)]
        ysq = [sb(f"ysq{i}", [P, QT]) for i in range(3)]
        rstd = [sb(f"rstd{i}", [P, QT]) for i in range(3)]
        shift = sb("shift", [P, QT])
        h_sb = sb("h_sb", [P, QT, D])
        ht = sb("ht", [P, DC, S])
        row_sb = sb("row_sb", [P, QT, ROW])
        aff = sb("aff", [P, QT, E])
        top = sb("top", [P, QT, 8])
        top_i = sb("top_i", [P, QT, 8], U32)
        top_f = sb("top_f", [P, QT])
        ea = sb("ea", [P, QT])
        ea1 = sb("ea1", [P, QT])
        hot = sb("hot", [P, QT, E], BF16)
        hot_sum = sb("hot_sum", [P, E])
        acc = sb("acc", [P, E], BF16)
        rank_e = sb("rank_e", [P, QT, E])
        rank_f = sb("rank_f", [P, QT])
        rank_i = sb("rank_i", [P, QT], I32)
        lohi_i = sb("lohi_i", [P, 2, QT], I32)
        lohi = sb("lohi", [P, 2, QT])
        lo_hot = sb("lo_hot", [P, QT, P], F32R)
        hi_hot = sb("hi_hot", [P, QT, RANKS], BF16)
        hot_id = sb("hot_id", [P, QT, E])
        put = sb("put", [P, QT, E, RANKS], F32R)
        table = sb("table", [P, E * RANKS])
        empty = ht[:, 0, 0:E * RANKS]
        ids = sb("ids", [P, E * RANKS], I32)
        cnt = sb("cnt", [P, E])
        over = sb("over", [P, E, MAXT])
        tl = sb("tl", [P, E])
        tl1 = sb("tl1", [P, E])
        tlu = sb("tlu", [P, E, E])
        ends = sb("ends", [P, E])
        past = sb("past", [P, META, E - 1])
        past_t = sb("past_t", [P, META, E - 1])
        start_f = sb("start_f", [P, META])
        meta_f = sb("meta_f", [P, 2, META])
        meta = sb("meta", [P, 2, META], I32)

        def in_parts(buf):
            return [buf[:, n * FC // 2:(n + 1) * FC // 2] for n in range(2)]

        w1_raw = [[k_raw[:, n] for n in range(DC)], [x1[n][:].rearrange("p t d -> p (t d)") for n in range(DC)]]
        w2_raw = [in_parts(v_raw), [h_sb[:], probs[:, 0:FC // 2 * D].rearrange("p (c d) -> p c d", d=D)]]
        w1_hi, w1_lo = k_hi, k_lo
        w2_hl = [in_parts(v_hl[0]), [v[:] for v in vn_hl]]
        w2_hi, w2_lo = [[[part[:, :, n] for part in parts] for parts in w2_hl] for n in range(2)]
        h1_hi, h1_lo = v_hi[1], v_lo[1]
        gate_sb = sb("gate_sb", [P, 2, HALVES])
        tok_out = sb("tok_out", [P, HALVES], I32)
        tok = [sb(f"tok{i}", [P, HALVES], I32) for i in range(2)]
        g = [row_sb[:, i * HALVES:(i + 1) * HALVES] for i in range(2)]
        vec = [sb(f"vec{i}", [P, 2 * DC + FC]) for i in range(2)]
        b2_all = [ht[:, 1, i * D:(i + 1) * D] for i in range(2)]
        xe, y_b = xn[:, 0:DC], xn[:, DC:DC + HALVES]
        xe_hi, xe_lo = [[xt[:, :, i * TILE:(i + 1) * TILE] for i in range(2)] for xt in (xt_hi, xt_lo)]
        y_banks = ps_pv, ps_ma
        h1 = x_both
        o_sb = vn_f

        ps_rank, ps_cnt = ps_ma[:, 0:QT * E], ps_mb[:, 0:E]
        LAST = B - 1

        def is_last(b):
            return isinstance(b, int) and b == LAST

        first_tiles, last_tile = range(QT - 1), range(QT - 1, QT)
        ps_h_last = ps_s[:, 1, 0:DC * P]

        def aff_bank(b):
            return ps_s[:, 2, 0:QT * E] if is_last(b) else ps_ma[:, 0:QT * E]

        def table_bank(b):
            return (ps_s[:, 0] if isinstance(b, int) and b == LAST - 1 else ps_ma)[:, 0:E * RANKS]

        w_in = [sem(f"w{n}_in") for n in range(3)]
        x0_in = [sem(f"x0_in{t}") for t in range(QT)]
        const_in, x_in, k_in, v_in, rows_out = map(sem, ("const_in", "x_in", "k_in", "v_in", "rows_out"))
        made, made2, w_hi_ok, w_lo_ok = map(sem, ("made", "made2", "w_hi_ok", "w_lo_ok"))
        scored, p_turned, pv_done, x_turned, projected = map(
            sem, ("scored", "p_turned", "pv_done", "x_turned", "projected"))
        h_turned, aff_ps, rank_ps, table_ps, cnt_ps = map(
            sem, ("h_turned", "aff_ps", "rank_ps", "table_ps", "cnt_ps"))
        exp_done, pt_hi_ok, xt_hi_ok, proj_hi_ok, ctx_hi_ok, ht_ok, gate_exp = map(
            sem, ("exp_done", "pt_hi_ok", "xt_hi_ok", "proj_hi_ok", "ctx_hi_ok", "ht_ok", "gate_exp"))
        ln_act = [sem(f"ln_act{i}") for i in range(3)]
        max_ok, pt_lo_ok, x1_ok, xt_lo_ok, proj_lo_ok, v_sum_ok = map(
            sem, ("max_ok", "pt_lo_ok", "x1_ok", "xt_lo_ok", "proj_lo_ok", "v_sum_ok"))
        var_ok = [sem(f"var_ok{i}") for i in range(3)]
        max_step = Steps(sem("max_step"), QT)
        stat_ok = [sem(f"stat_ok{i}") for i in range(3)]
        aggr_ok = [sem(f"aggr_ok{i}") for i in range(3)]
        rstd_step = [Steps(sem(f"rstd_step{i}"), 4) for i in range(3)]
        top_step = Steps(sem("top_step"), 5)
        rank_step = Steps(sem("rank_step"), 6)
        gate_ok, id_ok, lo_hot_ok, table_ok, sum_step, rsum_ok = map(
            sem, ("gate_ok", "id_ok", "lo_hot_ok", "table_ok", "sum_step", "rsum_ok"))
        meta_ok, ids_ok, meta_step, max_a, gate_step, settled = map(
            sem, ("meta_ok", "ids_ok", "meta_step", "max_a", "gate_step", "settled"))
        norm_ok, tok_out_ok, shift_ok = sem("norm_ok"), sem("tok_out_ok"), sem("shift_ok")
        x1_half, o_half = sem("x1_half"), sem("o_half")
        ctx_lo_ok, xn_ok, h_ok, row_ok, put_ok = map(sem, ("ctx_lo_ok", "xn_ok", "h_ok", "row_ok", "put_ok"))
        tok_ok, mm1_ok, mm2_ok, xe_turned = map(sem, ("tok_ok", "mm1_ok", "mm2_ok", "xe_turned"))
        w1_in, w2_in = [[sem(f"{n}_in{i}") for i in range(2)] for n in ("w1", "w2")]
        gathered = [[sem(f"gathered{i}{k}") for k in range(HALVES)] for i in range(2)]
        vec_in = [sem(f"vec_in{i}") for i in range(2)]
        stored = [sem(f"stored{k}_") for k in range(HALVES)]
        xe_ok, xe_hi_ok, xe_lo_ok, h1_ok, h1_hi_ok, h1_lo_ok = map(
            sem, ("xe_ok", "xe_hi_ok", "xe_lo_ok", "h1_ok", "h1_hi_ok", "h1_lo_ok"))
        w1_hi_ok, w2_hi_ok, w1_lo_v, w2_lo_v, w1_lo_p, w2_lo_p, resid_ok, o_ok = map(
            sem, ("w1_hi_ok", "w2_hi_ok", "w1_lo_v", "w2_lo_v", "w1_lo_p", "w2_lo_p", "resid_ok", "o_ok"))

        def no_more_than_b(n):
            return min(n, B) if isinstance(n, int) else n

        def batches(eng, body):
            body(0, 0)
            with eng.Fori(0, (B - 2) // 2) as i:
                body(2 * i + 1, 1)
                body(2 * i + 2, 0)
            body(LAST, LAST % 2)

        def tiles(eng, body):
            body(0, 0)
            with eng.Fori(0, (TILES - 1) // 2) as i:
                body(2 * i + 1, 1)
                body(2 * i + 2, 0)

        proj_bank = ps_mb, ps_ma, ps_a, ps_b, ps_mb, ps_ma

        def h_bank(n):
            return ps_s[:, n] if n < KB else ps_a[:]

        def vec_value(j, par):
            return (j - par) * 16 + 32

        def w_value(j, par):
            return (j + par) * 16

        block = ctx.enter_context(nc.Block())

        @block.sync
        def _(sp):
            def load_k(n):
                if some(NPIECE * n - 2):
                    sp.wait_ge(ctx_hi_ok, NPIECE * n - 2)
                if some(NPIECE * n - 2):
                    sp.wait_ge(ctx_lo_ok, NPIECE * n - 2)
                sp.dma_start(k_raw[:], keys_src[bass.ds(n, 1)].rearrange("o (c p) k -> p (o c) k", p=P)).then_inc(k_in, 16)

            def load_v(n):
                if some(NPIECE * n):
                    sp.wait_ge(ctx_hi_ok, NPIECE * n)
                if some(NPIECE * n):
                    sp.wait_ge(ctx_lo_ok, NPIECE * n)
                sp.dma_start(v_raw[:], vals_src[bass.ds(n, 1)].rearrange("o (p c) d -> p (o c) d", p=P)).then_inc(v_in, 16)

            def load_x(n, par):
                if some(QT * (n - 1)):
                    sp.wait_ge(x1_ok, QT * (n - 1))
                if some(n - 1):
                    sp.wait_ge(var_ok[0], n - 1)
                sp.dma_start(x_sb[par], x[bass.ds(n, 1)].rearrange("o (p t) d -> p (o t) d", p=P)).then_inc(x_in, 16)

            for t in range(QT):
                sp.dma_start(x_sb[0][:, t], x[0].rearrange("(p t) d -> p t d", p=P)[:, t]).then_inc(x0_in[t], 16)
            for n in W_ORDER:
                w = (wq, wk, wv)[n]
                sp.dma_start(w_raw[:, n], w.rearrange("(c p) d -> p c d", p=P)).then_inc(w_in[n], 16)
            sp.dma_start(bqk[:], b_cols).then_inc(const_in, 16)
            sp.dma_start(bv_all[:], bv.rearrange("(o d) -> o d", o=1).broadcast_to([P, D])).then_inc(const_in, 16)
            sp.dma_start(cent_sb[:], cent.rearrange("(c p) e -> p c e", p=P)).then_inc(const_in, 16)
            load_k(0)
            load_v(0)
            load_k(1)
            load_v(1)

            def store_rows(b):
                sp.wait_ge(row_ok, b + 1)
                sp.wait_ge(norm_ok, QT * (b + 1))
                sp.wait_ge(gate_ok, b + 1)
                sp.dma_start(rows[bass.ds(b * S, S)].rearrange("(p t) w -> p t w", p=P), row_sb[:]).then_inc(rows_out, 16)

            def body(b, par):
                if not is_last(b):
                    load_x(b + 1, 1 - par)
                if not is_last(b):
                    load_k(b + 2)
                    load_v(b + 2)
                if not isinstance(b, int) or b > 0:
                    store_rows(b - 1)

            batches(sp, body)
            last_rows = rows[LAST * S:].rearrange("(p t) w -> p t w", p=P)
            sp.wait_ge(row_ok, B)
            sp.dma_start(last_rows[:, :, REST:], row_sb[:, :, REST:]).then_inc(rows_out, 16)
            sp.wait_ge(norm_ok, QT * B)
            sp.wait_ge(gate_ok, B)
            sp.dma_start(last_rows[:, :, 0:REST], row_sb[:, :, 0:REST]).then_inc(rows_out, 16)

            def expert(j):
                settle(sp, settled)
                return sp.value_load(meta[0:1, 0, bass.ds(j, 1)], min_val=0, max_val=E - 1)

            def load_w(j, par):
                e = expert(j) + B
                for n in range(2):
                    if some(2 * (j - 2)):
                        sp.wait_ge(w1_hi_ok, 2 * (j - 2))
                    if some(j - 2):
                        sp.wait_ge(w1_lo_v, j - 2)
                    if some(j - 2):
                        sp.wait_ge(w1_lo_p, j - 2)
                    sp.dma_start(w1_raw[par][n], keys_src[bass.ds(e, 1), n * P:(n + 1) * P].rearrange("o p k -> p (o k)")
                                 ).then_inc(w1_in[par], 16)
                for n in range(2):
                    if some(2 * (j - 2)):
                        sp.wait_ge(w2_hi_ok, 2 * (j - 2))
                    if some(j - 2):
                        sp.wait_ge(w2_lo_v, j - 2)
                    if some(j - 2):
                        sp.wait_ge(w2_lo_p, j - 2)
                    c = slice(n * FC // 2, (n + 1) * FC // 2)
                    sp.dma_start(w2_raw[par][n], vals_src[bass.ds(e, 1)].rearrange("o (p c) d -> p (o c) d", p=P)[:, c]
                                 ).then_inc(w2_in[par], 16)

            def load_vec(j, par):
                if some(2 * (j - 1)):
                    sp.wait_ge(resid_ok, 2 * (j - 1))
                    settle(sp, settled)
                if some(FC * (j - 1)):
                    sp.wait_ge(h1_ok, FC * (j - 1))
                e = expert(j) if not isinstance(j, int) or j > 0 else 0
                sp.dma_start(vec[par][:], vecs[bass.ds(e, 1)].rearrange("o p n -> (o p) n")).then_inc(vec_in[par], 16)
                sp.dma_start(b2_all[par], b2[bass.ds(e, 1)].broadcast_to([P, D])).then_inc(vec_in[par], 16)

            sp.wait_ge(aff_ps, B)
            load_vec(0, 0)
            for k in range(HALVES):
                sp.wait_ge(gathered[0][k], 16)
            sp.wait_ge(meta_ok, 1)
            load_vec(1, 1)
            sp.wait_ge(row_ok, B)
            sp.wait_ge(norm_ok, QT * B)
            load_w(1, 1)
            sp.wait_ge(ctx_hi_ok, NPIECE * (B + 1))
            sp.wait_ge(ctx_lo_ok, NPIECE * (B + 1))
            load_w(2, 0)

            def tile_body(j, par):
                if not isinstance(j, int) or j > 0:
                    load_vec(j + 1, 1 - par)
                    load_w(j + 2, par)

            tiles(sp, tile_body)
            sp.wait_ge(rows_out, 16 * (B + 1))
            for k in range(HALVES):
                sp.wait_ge(stored[k], 16 * TILES)
            for loaded in (w1_in, w2_in):
                for par in range(2):
                    last = TILES + 1 - (TILES + 1 - par) % 2
                    sp.wait_ge(loaded[par], w_value(last, par))

        @block.gpsimd
        def _(pool):
            pool.memset(ident_in[:], 0.0).then_inc(made, 1)
            pool.memset(upto_in[:], 1.0).then_inc(made, 1)
            pool.memset(ones[:], 1.0).then_inc(made, 1)
            pool.memset(acc[:], 0.0).then_inc(made, 1)
            pool.memset(table[:], 0.0).then_inc(made, 1)
            pool.memset(row_sb[:], 0.0).then_inc(made, 1)
            kw = dict(allow_small_or_imprecise_dtypes=True)
            pool.iota(iota_f[:], pattern=[[1, P]], base=0, channel_multiplier=0, **kw).then_inc(made, 1)
            pool.iota(iota_e[:], pattern=[[0, QT], [1, E]], base=0, channel_multiplier=0, **kw).then_inc(made, 1)
            pool.iota(iota_r[:], pattern=[[0, QT], [1, RANKS]], base=0, channel_multiplier=0, **kw).then_inc(made, 1)
            pool.iota(tok_no[:], pattern=[[1, QT]], base=1, channel_multiplier=QT, **kw).then_inc(made, 1)
            pool.iota(thr[:], pattern=[[0, E], [TILE, MAXT]], base=0, channel_multiplier=0, **kw).then_inc(made, 1)
            pool.iota(tile_j[:], pattern=[[1, META], [0, E - 1]], base=0, channel_multiplier=0, **kw).then_inc(made, 1)
            pool.wait_ge(made, 12)
            pool.affine_select(out=ident[:], in_=ident_in[:], compare_op=ALU.not_equal, fill=1.0,
                               base=0, pattern=[[-1, P]], channel_multiplier=1).then_inc(made2, 1)
            pool.affine_select(out=tri[:], in_=ones[:], compare_op=ALU.is_gt, fill=0.0,
                               base=0, pattern=[[1, P]], channel_multiplier=-1).then_inc(made2, 1)
            pool.affine_select(out=upto[:], in_=upto_in[:], compare_op=ALU.is_ge, fill=0.0,
                               base=0, pattern=[[1, E], [-1, E]], channel_multiplier=0).then_inc(made2, 1)

            def ctx_lo(n, par, piece):
                pool.wait_ge(ctx_hi_ok, NPIECE * n + piece + 1)
                if piece < 2:
                    args = k_lo[par][:, piece], k_raw[:, piece], k_hi[par][:, piece].bitcast(F32)
                else:
                    c = slice((piece - 2) * 4, (piece - 2) * 4 + 4)
                    args = v_lo[par][:, c], v_raw[:, c], v_hi[par][:, c].bitcast(F32)
                pool.tensor_tensor(*args, ALU.subtract).then_inc(ctx_lo_ok, 1)

            for piece in range(NPIECE):
                ctx_lo(0, 0, piece)

            def body(b, par):
                later = not isinstance(b, int) or b > 0
                ctx_lo(b + 1, 1 - par, 0)
                if later:
                    residual(b - 1, 1 - par)
                ctx_lo(b + 1, 1 - par, 1)
                ctx_lo(b + 1, 1 - par, 2)
                if later:
                    put_ids(b - 1)
                ctx_lo(b + 1, 1 - par, 3)

            def residual(b, par):
                pool.wait_ge(h_ok, QT * (b + 1))
                pool.wait_ge(rows_out, 16 * b)
                pool.tensor_tensor(row_sb[:, :, REST:], x1[par][:], h_sb[:], ALU.add).then_inc(row_ok, 1)

            def put_ids(b):
                pool.wait_ge(id_ok, b + 1)
                pool.wait_ge(table_ps, b)
                for t in range(QT):
                    pool.tensor_tensor(
                        put[:, t], hot_id[:, t, :, None].broadcast_to([P, E, RANKS]),
                        hi_hot[:, t, None, :].broadcast_to([P, E, RANKS]), ALU.mult).then_inc(put_ok, 1)

            batches(pool, body)
            residual(LAST, LAST % 2)

            pool.wait_ge(ids_ok, 1)
            pool.wait_ge(rows_out, 16 * (B + 1))

            def gather_value(j, par):
                return 8 * (j - par) + 16

            def first_ids(j, par):
                if isinstance(j, int) and j == 0:
                    col = 0
                else:
                    col = pool.value_load(meta[0:1, 1, bass.ds(j, 1)], min_val=0, max_val=E * RANKS - HALVES)
                settle(pool, settled)
                if not isinstance(j, int) or j > 1:
                    for k in range(HALVES):
                        pool.wait_ge(gathered[par][k], gather_value(j, par) - 16)
                pool.tensor_copy(tok[par][:], ids[:, bass.ds(col, HALVES)]).then_inc(tok_ok, 1)

            def gather(j, par, k):
                if some(2 * (j - 2) + k + 1):
                    pool.wait_ge(resid_ok, 2 * (j - 2) + k + 1)
                pool.wait_ge(tok_ok, j + 1)
                settle(pool, settled)
                pool.indirect_dma_start(
                    out=g[par][:, k, :], out_offset=None, in_=rows[:, :],
                    in_offset=bass.IndirectOffsetOnAxis(ap=tok[par][:, k:k + 1], axis=0),
                    bounds_check=TOKENS - 1, oob_is_err=False).then_inc(gathered[par][k], 16)

            def out_ids(j):
                col = pool.value_load(meta[0:1, 1, bass.ds(j, 1)], min_val=0, max_val=E * RANKS - HALVES)
                for k in range(HALVES):
                    if some(16 * j):
                        pool.wait_ge(stored[k], 16 * j)
                pool.tensor_copy(tok_out[:], ids[:, bass.ds(col, HALVES)]).then_inc(tok_out_ok, 1)

            def scatter(j, k):
                pool.wait_ge(tok_out_ok, j + 1)
                pool.wait_ge(o_ok, 2 * j + k + 1)
                settle(pool, settled)
                pool.indirect_dma_start(
                    out=out[:, :], out_offset=bass.IndirectOffsetOnAxis(ap=tok_out[:, k:k + 1], axis=0),
                    in_=o_sb[:, k, :], in_offset=None,
                    bounds_check=TOKENS - 1, oob_is_err=False).then_inc(stored[k], 16)

            first_ids(0, 0)
            gather(0, 0, 0)
            gather(0, 0, 1)
            pool.wait_ge(meta_ok, 1)
            first_ids(1, 1)
            gather(1, 1, 0)
            gather(1, 1, 1)

            def tile_body(j, par):
                if not isinstance(j, int) or j > 0:
                    out_ids(j - 1)
                    scatter(j - 1, 0)
                    pool.wait_ge(w2_hi_ok, 2 * j - 1)
                    pool.tensor_tensor(w2_lo[par][1], w2_raw[par][1], w2_hi[par][1].bitcast(F32),
                                       ALU.subtract).then_inc(w2_lo_p, 1)
                    scatter(j - 1, 1)
                pool.wait_ge(w1_hi_ok, 2 * j + 1)
                pool.tensor_tensor(w1_lo[1 - par][:, 1], w1_raw[1 - par][1], w1_hi[1 - par][:, 1].bitcast(F32),
                                   ALU.subtract).then_inc(w1_lo_p, 1)
                first_ids(j + 2, par)
                gather(j + 2, par, 0)
                gather(j + 2, par, 1)

            tiles(pool, tile_body)
            out_ids(TILES - 1)
            scatter(TILES - 1, 0)
            scatter(TILES - 1, 1)
            for k in range(HALVES):
                for par in range(2):
                    last = TILES + 1 - (TILES + 1 - par) % 2
                    pool.wait_ge(gathered[par][k], gather_value(last, par))

        @block.scalar
        def _(act):
            act.preload_act_table_set("natural_log_exp_and_others")
            def ln(kind, n, tiles=range(QT)):
                u = slice(tiles[0], tiles[-1] + 1)
                act.wait_ge(var_ok[kind], n + 1)
                act.activation(lnv[kind][:, u], ve[kind][:, u], ACT.Ln).then_inc(ln_act[kind], 1)
                act.wait_ge(ln_act[kind], 2 * n + 1)
                act.activation(y0[kind][:, u], lnv[kind][:, u], ACT.Exp, scale=-0.5).then_inc(ln_act[kind], 1)

            def normalised(b):
                act.wait_ge(shift_ok, b + 1)
                if some(16 * b):
                    act.wait_ge(rows_out, 16 * b)
                for t in range(QT):
                    act.activation(row_sb[:, t, 0:D], h_sb[:, t], ACT.Identity, bias=shift[:, t:t + 1],
                                   scale=rstd[2][:, t:t + 1]).then_inc(norm_ok, 1)

            def ctx_hi(n, par, piece):
                if piece == 0:
                    act.wait_ge(k_in, 16 * (n + 1))
                    if some(KB * QT * (n - 1)):
                        act.wait_ge(scored, KB * QT * (n - 1))
                if piece == 2:
                    act.wait_ge(v_in, 16 * (n + 1))
                    if some(QT * (n - 1)):
                        act.wait_ge(pv_done, QT * (n - 1))
                if piece < 2:
                    args = k_hi[par][:, piece], k_raw[:, piece]
                else:
                    c = slice((piece - 2) * 4, (piece - 2) * 4 + 4)
                    args = v_hi[par][:, c], v_raw[:, c]
                act.activation(*args, ACT.Copy).then_inc(ctx_hi_ok, 1)

            def turned_x(n, c):
                act.wait_ge(x_turned, DC * n + c + 1)
                if some(NPROJ * n):
                    act.wait_ge(projected, NPROJ * n)
                act.activation(xt_hi[:, c], (ps_mb, ps_ma)[c][:], ACT.Copy).then_inc(xt_hi_ok, 1)

            def proj_hi(n, par, m):
                name, c = QKV_ORDER[m][0], int(QKV_ORDER[m][1])
                if name == "v":
                    act.wait_ge(v_sum_ok, 2 * n + c + 1)
                    if c == 0:
                        if some(QT * (n - 1)):
                            act.wait_ge(pv_done, QT * (n - 1))
                    act.activation(vn_hi[par][:, 2 * c:2 * c + 2], vn_f[:], ACT.Copy).then_inc(proj_hi_ok, 1)
                    return
                act.wait_ge(projected, NPROJ * n + m + 1)
                if m == 2:
                    if some(KB * QT * n):
                        act.wait_ge(scored, KB * QT * n)
                bank = proj_bank[m]
                dst, bias = (q_hi, 0) if name == "q" else (kn_hi, 1)
                act.activation(dst[:, c], bank[:], ACT.Identity, bias=bqk[:, bias, c:c + 1]).then_inc(proj_hi_ok, 1)

            def exps(b, par, t):
                act.wait_ge(max_ok, QT * b + t + 1)
                if some(KB * (QT * b + t)):
                    act.wait_ge(p_turned, KB * (QT * b + t))
                act.activation(probs[:], ps_s[:].rearrange("p a n -> p (a n)"), ACT.Exp, bias=neg_max[:, 0:1],
                               scale=SCALE, accum_out=sums[:, par, t:t + 1]).then_inc(exp_done, 1)

            def p_hi(b, t, n, bank):
                act.wait_ge(p_turned, KB * (QT * b + t) + n + 1)
                if n == 0:
                    if some(QT * b + t):
                        act.wait_ge(pv_done, QT * b + t)
                act.activation(pt_hi[:, GPB * n:GPB * n + GPB], bank[:].rearrange("p (g q) -> p g q", g=GPB),
                               ACT.Copy).then_inc(pt_hi_ok, 1)

            ln(0, 0)
            for n in W_ORDER:
                act.wait_ge(w_in[n], 16)
                act.activation(w_hi[:, n], w_raw[:, n], ACT.Copy).then_inc(w_hi_ok, 1)
            turned_x(0, 0)
            turned_x(0, 1)
            act.wait_ge(const_in, 16 * 3)
            ctx_hi(0, 0, 0)
            ctx_hi(0, 0, 1)
            for m in range(NPROJ):
                proj_hi(0, 0, m)
                if m == 1:
                    ctx_hi(0, 0, 2)
                if m == 3:
                    ctx_hi(0, 0, 3)
            exps(0, 0, 0)

            def turned_h_last(c):
                act.wait_ge(h_turned, DC * LAST + c + 1)
                if c < DC:
                    if c == 0:
                        act.wait_ge(aff_ps, LAST)
                    n = (QT - 1) * P
                    act.activation(ht[:, c, 0:n], (ps_ma, ps_mb)[c][:, 0:n], ACT.Copy).then_inc(ht_ok, 1)
                else:
                    act.activation(ht[:, :, (QT - 1) * P:], ps_h_last.rearrange("p (c q) -> p c q", c=DC),
                                   ACT.Copy).then_inc(ht_ok, 1)

            def turned_h(b, c):
                act.wait_ge(h_turned, DC * b + c + 1)
                act.wait_ge(aff_ps, b)
                act.activation(ht[:, c], (ps_ma, ps_mb)[c][:], ACT.Copy).then_inc(ht_ok, 1)

            def gate(b):
                act.wait_ge(top_step.sem, top_step.per * b + 2)
                act.activation(ea[:], top[:, :, 0], ACT.Exp, scale=-1.0).then_inc(gate_exp, 1)

            def body(b, par):
                later = not isinstance(b, int) or b > 0
                for t in range(1, QT):
                    p_hi(b, t - 1, 0, ps_a)
                    p_hi(b, t - 1, 1, ps_b)
                    if t == 2:
                        if is_last(b):
                            ln(2, b - 1)
                        else:
                            ln(0, b + 1)
                    ctx_hi(b + 1, 1 - par, t - 1)
                    if later and t == 1:
                        ln(1, b - 1)
                    if later and t == 2:
                        turned_h(b - 1, 0)
                        turned_h(b - 1, 1)
                    if later and t == 3:
                        gate(b - 1)
                    if is_last(b) and t == 3:
                        normalised(b - 1)
                    p_hi(b, t - 1, 2, ps_a)
                    exps(b, par, t)
                if not is_last(b):
                    turned_x(b + 1, 0)
                    turned_x(b + 1, 1)
                    for m in range(NPROJ):
                        proj_hi(b + 1, 1 - par, m)
                p_hi(b, 3, 0, ps_a)
                p_hi(b, 3, 1, ps_b)
                if later and not is_last(b):
                    ln(2, b - 1)
                if not is_last(b):
                    ctx_hi(b + 1, 1 - par, 3)
                p_hi(b, 3, 2, ps_mb if is_last(b) else ps_a)
                if is_last(b):
                    ln(1, LAST, first_tiles)
                if not is_last(b):
                    exps(b + 1, 1 - par, 0)
                    if later:
                        normalised(b - 1)
                else:
                    ctx_hi(b + 1, 1 - par, 3)

            batches(act, body)
            turned_h_last(0)
            turned_h_last(1)
            ln(1, LAST + 1, last_tile)
            turned_h_last(2)
            ln(2, LAST)
            gate(LAST)
            normalised(LAST)

            def expert_x(j, par):
                act.wait_ge(xe_turned, j + 1)
                act.wait_ge(vec_in[par], vec_value(j, par))
                if some(j):
                    act.wait_ge(xe_hi_ok, j)
                if some(j):
                    act.wait_ge(xe_lo_ok, j)
                for c in range(DC):
                    act.activation(xe[:, c], ps_mb[:, c * TILE:(c + 1) * TILE], ACT.Identity,
                                   bias=vec[par][:, DC + c:DC + c + 1], scale=vec[par][:, c:c + 1]).then_inc(xe_ok, 1)

            expert_x(0, 0)

            def w1_part(j, par, n):
                act.wait_ge(w1_in[par], w_value(j, par))
                if n == 1:
                    if some(FC // 2 * (j - 1)):
                        act.wait_ge(mm1_ok, FC // 2 * (j - 1))
                act.activation(w1_hi[par][:, n], w1_raw[par][n], ACT.Copy).then_inc(w1_hi_ok, 1)

            def w2_part(j, par, n):
                act.wait_ge(w2_in[par], w_value(j, par))
                if n == 1:
                    if some(HALVES * (j - 1)):
                        act.wait_ge(mm2_ok, HALVES * (j - 1))
                act.activation(w2_hi[par][n], w2_raw[par][n], ACT.Copy).then_inc(w2_hi_ok, 1)

            def hidden(j, par, n):
                act.wait_ge(mm1_ok, FC // 2 * j + n + 1)
                if some(FC // 2 * (j - 1) + n + 1):
                    act.wait_ge(h1_lo_ok, FC // 2 * (j - 1) + n + 1)
                for f in (2 * n, 2 * n + 1):
                    act.activation(h1[:, f], h_bank(n)[:, (f % 2) * TILE:(f % 2 + 1) * TILE], ACT.Relu,
                                   bias=vec[par][:, 2 * DC + f:2 * DC + f + 1]).then_inc(h1_ok, 1)

            def tile_body(j, par):
                hidden(j, par, 0)
                hidden(j, par, 1)
                w1_part(j + 1, 1 - par, 1)
                hidden(j, par, 2)
                hidden(j, par, 3)
                w1_part(j + 1, 1 - par, 0)
                expert_x(j + 1, 1 - par)
                w2_part(j + 1, 1 - par, 1)
                w2_part(j + 1, 1 - par, 0)

            tiles(act, tile_body)

        @block.vector
        def _(dve):
            def stats(kind, b, t, src):
                dve.bn_stats(st[kind][:, t], src).then_inc(stat_ok[kind], 1)

            def variance(kind, n, b, tiles=range(QT)):
                dve.wait_ge(stat_ok[kind], QT * b + tiles[-1] + 1)
                settle(dve, settled)
                for t in tiles:
                    ins = dve.bn_aggr(mv[kind][:, t], st[kind][:, t])
                ins.then_inc(aggr_ok[kind], 1)
                dve.wait_ge(aggr_ok[kind], n + 1)
                u = slice(tiles[0], tiles[-1] + 1)
                dve.tensor_scalar(ve[kind][:, u], mv[kind][:, u, 1], LN_EPS, None, ALU.add).then_inc(var_ok[kind], 1)

            def x_stats(n, par):
                if some(16 * n):
                    dve.wait_ge(x_in, 16 * n)
                for t in range(QT):
                    if isinstance(n, int) and n == 0:
                        dve.wait_ge(x0_in[t], 16)
                    stats(0, n, t, x_sb[par][:, t])
                variance(0, n, n)

            def x1_stats(b, par, t):
                dve.wait_ge(x1_ok, QT * b + t + 1)
                stats(1, b, t, x1[par][:, t])

            def h_stats(b, t):
                dve.wait_ge(h_ok, QT * b + t + 1)
                stats(2, b, t, h_sb[:, t])

            def refine(kind, n, tiles=range(QT)):
                s = rstd_step[kind]
                s.begin(n)
                dve.wait_ge(ln_act[kind], 2 * n + 2)
                u = slice(tiles[0], tiles[-1] + 1)
                y, sq = y0[kind][:, u], ysq[kind][:, u]
                s(dve, dve.tensor_tensor(sq, y, y, ALU.mult))
                s(dve, dve.tensor_tensor(sq, sq, ve[kind][:, u], ALU.mult))
                s(dve, dve.tensor_scalar(sq, sq, -0.5, 1.5, ALU.mult, ALU.add))
                s(dve, dve.tensor_tensor(rstd[kind][:, u], y, sq, ALU.mult))

            def norm(kind, src, dst, done, tiles=range(QT)):
                for t in tiles:
                    dve.tensor_scalar(dst(t), src(t), mv[kind][:, t, 0:1], rstd[kind][:, t:t + 1],
                                      ALU.subtract, ALU.mult).then_inc(done, 1)

            def ln1(n, par):
                refine(0, n)
                if some(DC * n):
                    dve.wait_ge(x_turned, DC * n)
                norm(0, lambda t: x_sb[par][:, t], lambda t: xn[:, t], xn_ok)

            def ln2(n, b, par, tiles=range(QT)):
                refine(1, n, tiles)
                if some(DC * b):
                    dve.wait_ge(h_turned, DC * b)
                if some(b):
                    dve.wait_ge(row_ok, b)
                if some(QT * b):
                    dve.wait_ge(norm_ok, QT * b)
                norm(1, lambda t: x1[par][:, t], lambda t: h_sb[:, t], h_ok, tiles)

            def ln3_scale(b):
                if some(QT * b):
                    dve.wait_ge(norm_ok, QT * b)
                refine(2, b)
                dve.scalar_tensor_tensor(out=shift[:], in0=mv[2][:, :, 0], scalar=-1.0, in1=rstd[2][:],
                                         op0=ALU.mult, op1=ALU.mult).then_inc(shift_ok, 1)

            def turned_x(n, c):
                dve.wait_ge(xt_hi_ok, DC * n + c + 1)
                dve.tensor_tensor(xt_lo[:, c], (ps_mb, ps_ma)[c][:], xt_hi[:, c].bitcast(F32), ALU.subtract).then_inc(xt_lo_ok, 1)

            def proj_sum(n, c):
                dve.wait_ge(projected, NPROJ * n + c + 1)
                if some(NPROJ * n + c):
                    dve.wait_ge(proj_lo_ok, NPROJ * n + c)
                dve.tensor_tensor(vn_f[:], proj_bank[c][:].rearrange("p (t d) -> p t d", t=2),
                                  bv_all[:, None, :].broadcast_to([P, 2, D]),
                                  ALU.add).then_inc(v_sum_ok, 1)

            def proj_lo(n, par, m):
                name, c = QKV_ORDER[m][0], int(QKV_ORDER[m][1])
                dve.wait_ge(proj_hi_ok, NPROJ * n + m + 1)
                if name == "v":
                    dve.tensor_tensor(vn_lo[par][:, 2 * c:2 * c + 2], vn_f[:],
                                      vn_hi[par][:, 2 * c:2 * c + 2].bitcast(F32), ALU.subtract).then_inc(proj_lo_ok, 1)
                    return
                bank = proj_bank[m]
                hi, lo, bias = (q_hi, q_lo, 0) if name == "q" else (kn_hi, kn_lo, 1)
                dve.scalar_tensor_tensor(out=lo[:, c], in0=bank[:], scalar=bqk[:, bias, c:c + 1],
                                         in1=hi[:, c].bitcast(F32), op0=ALU.add, op1=ALU.subtract).then_inc(proj_lo_ok, 1)

            def max_of(b, t, n):
                dve.wait_ge(scored, KB * (QT * b + t) + n + 1)
                ins = dve.tensor_reduce(mx3[:, n:n + 1], ps_s[:, n], AX.X, ALU.max)
                if n < KB - 1:
                    return
                max_steps(b, t, ins)

            def max_steps(b, t, ins):
                ins.then_inc(max_a, 1)
                dve.wait_ge(max_a, QT * b + t + 1)
                dve.tensor_reduce(mx1[:], mx3[:], AX.X, ALU.max).then_inc(max_step.sem, 1)
                dve.wait_ge(max_step.sem, QT * b + t + 1)
                if some(QT * b + t):
                    dve.wait_ge(exp_done, QT * b + t)
                dve.tensor_scalar(neg_max[:], mx1[:], -SCALE, None, ALU.mult).then_inc(max_ok, 1)

            def p_lo(b, t, n, bank):
                dve.wait_ge(pt_hi_ok, KB * (QT * b + t) + n + 1)
                c = slice(GPB * n, GPB * n + GPB)
                dve.tensor_tensor(pt_lo[:, c], bank[:].rearrange("p (g q) -> p g q", g=GPB), pt_hi[:, c].bitcast(F32),
                                  ALU.subtract).then_inc(pt_lo_ok, 1)

            def add_x(b, par, t):
                dve.wait_ge(pv_done, QT * b + t + 1)
                dve.reciprocal(rsum[:], sums[:, par, t:t + 1]).then_inc(rsum_ok, 1)
                dve.wait_ge(rsum_ok, QT * b + t + 1)
                if t == 0:
                    if some(b - 1):
                        dve.wait_ge(row_ok, b - 1)
                dve.scalar_tensor_tensor(out=x1[par][:, t], in0=ps_pv[:, D:], scalar=rsum[:, 0:1], in1=x_sb[par][:, t],
                                         op0=ALU.mult, op1=ALU.add).then_inc(x1_half, 1)
                dve.wait_ge(x1_half, QT * b + t + 1)
                dve.scalar_tensor_tensor(out=x1[par][:, t], in0=ps_pv[:, 0:D], scalar=rsum[:, 0:1], in1=x1[par][:, t],
                                         op0=ALU.mult, op1=ALU.add).then_inc(x1_ok, 1)

            def top_expert(b):
                s = top_step
                s.begin(b)
                dve.wait_ge(aff_ps, b + 1)
                s(dve, dve.tensor_copy(aff[:].rearrange("p t e -> p (t e)"), aff_bank(b)))
                settle(dve, settled)
                for t in range(QT):
                    ins = dve.max(top[:, t], aff[:, t])
                s(dve, ins)
                settle(dve, settled)
                for t in range(QT):
                    ins = dve.max_index(top_i[:, t], top[:, t], aff[:, t])
                s(dve, ins)
                s(dve, dve.tensor_copy(top_f[:], top_i[:, :, 0]))
                s(dve, dve.tensor_tensor(hot[:], iota_e[:], top_f[:, :, None].broadcast_to([P, QT, E]), ALU.is_equal))

            def gates(b):
                dve.wait_ge(gate_exp, b + 1)
                dve.tensor_scalar(ea1[:], ea[:], 1.0, None, ALU.add).then_inc(gate_step, 1)
                dve.wait_ge(gate_step, b + 1)
                dve.wait_ge(rows_out, 16 * b)
                dve.reciprocal(row_sb[:, :, GATE], ea1[:]).then_inc(gate_ok, 1)

            def read_ranks(b):
                s = rank_step
                s.begin(b)
                dve.wait_ge(rank_ps, b + 1)
                s.count(dve.tensor_tensor(rank_e[:], ps_rank.rearrange("p (t e) -> p t e", t=QT), hot[:], ALU.mult))

            def ranks(b):
                s = rank_step
                dve.wait_ge(s.sem, s.per * b + 1)
                s(dve, dve.tensor_reduce(rank_f[:], rank_e[:], AX.X, ALU.add))
                s(dve, dve.tensor_copy(rank_i[:], rank_f[:]))
                s.count(dve.tensor_scalar(lohi_i[:, 0], rank_i[:], P - 1, None, ALU.bitwise_and))
                s(dve, dve.tensor_scalar(lohi_i[:, 1], rank_i[:], 7, None, ALU.logical_shift_right))
                s(dve, dve.tensor_copy(lohi[:], lohi_i[:]))

            def low_ranks(b):
                dve.wait_ge(table_ps, b)
                for t in range(QT):
                    ins = dve.tensor_scalar(lo_hot[:, t], iota_f[:], lohi[:, 0, t:t + 1], None, ALU.is_equal)
                ins.then_inc(lo_hot_ok, 1)

            def high_ranks(b):
                dve.wait_ge(put_ok, QT * b)
                dve.tensor_tensor(hi_hot[:], iota_r[:], lohi[:, 1, :, None].broadcast_to([P, QT, RANKS]), ALU.is_equal)
                dve.tensor_tensor(hot_id[:], hot[:], tok_no[:, :, None].broadcast_to([P, QT, E]), ALU.mult).then_inc(id_ok, 1)
                if is_last(b):
                    return
                dve.tensor_reduce(hot_sum[:], hot[:].rearrange("p t e -> p e t"), AX.X, ALU.add).then_inc(sum_step, 1)
                dve.wait_ge(id_ok, b + 1)
                dve.tensor_scalar(tok_no[:], tok_no[:], float(S), None, ALU.add)
                dve.wait_ge(sum_step, 2 * b + 1)
                dve.tensor_tensor(acc[:], acc[:], hot_sum[:], ALU.add).then_inc(sum_step, 1)

            def put_ids(b):
                dve.wait_ge(id_ok, b + 1)
                dve.wait_ge(table_ps, b)
                for t in range(QT):
                    dve.tensor_tensor(
                        put[:, t], hot_id[:, t, :, None].broadcast_to([P, E, RANKS]),
                        hi_hot[:, t, None, :].broadcast_to([P, E, RANKS]), ALU.mult).then_inc(put_ok, 1)

            def add_table(b):
                dve.wait_ge(table_ps, b + 1)
                dve.wait_ge(table_ok, b)
                dve.tensor_tensor(table[:], table[:], table_bank(b), ALU.add).then_inc(table_ok, 1)

            x_stats(0, 0)
            ln1(0, 0)

            def weights_lo(i):
                n = W_ORDER[i]
                dve.wait_ge(w_hi_ok, i + 1)
                dve.tensor_tensor(w_lo[:, n], w_raw[:, n], w_hi[:, n].bitcast(F32), ALU.subtract).then_inc(w_lo_ok, 1)

            weights_lo(0)
            turned_x(0, 0)
            turned_x(0, 1)
            weights_lo(1)
            weights_lo(2)
            dve.wait_ge(const_in, 16 * 3)
            for c in range(2):
                proj_sum(0, c)
                proj_lo(0, 0, c)
            for m in range(2, NPROJ):
                proj_lo(0, 0, m)
            dve.wait_ge(made, 12)
            dve.wait_ge(made2, 3)
            for n in range(KB):
                max_of(0, 0, n)

            def body(b, par):
                later = not isinstance(b, int) or b > 0
                for t in range(1, QT):
                    if t > 1:
                        add_x(b, par, t - 2)
                    elif later:
                        add_x(b - 1, 1 - par, QT - 1)
                    p_lo(b, t - 1, 0, ps_a)
                    if t > 1:
                        x1_stats(b, par, t - 2)
                    elif later:
                        x1_stats(b - 1, 1 - par, QT - 1)
                    p_lo(b, t - 1, 1, ps_b)
                    if later and t == 1:
                        variance(1, b - 1, b - 1)
                    max_of(b, t, 0)
                    if later and t == 3:
                        read_ranks(b - 1)
                    max_of(b, t, 1)
                    p_lo(b, t - 1, 2, ps_a)
                    max_of(b, t, 2)
                    if later and t == 1:
                        ln2(b - 1, b - 1, 1 - par)
                    if t == 1:
                        if not is_last(b):
                            x_stats(b + 1, 1 - par)
                        else:
                            for u in range(QT):
                                h_stats(b - 1, u)
                            variance(2, b - 1, b - 1)
                    if later and t == 2:
                        top_expert(b - 1)
                    if t == 2:
                        if not is_last(b):
                            ln1(b + 1, 1 - par)
                        else:
                            ln3_scale(b - 1)
                if is_last(b):
                    gates(b - 1)
                    ranks(b - 1)
                    low_ranks(b - 1)
                    high_ranks(b - 1)
                    add_x(b, par, 2)
                    p_lo(b, 3, 0, ps_a)
                    p_lo(b, 3, 1, ps_b)
                    p_lo(b, 3, 2, ps_mb)
                    x1_stats(b, par, 2)
                    variance(1, LAST, LAST, first_tiles)
                    return
                if later:
                    for t in range(QT):
                        h_stats(b - 1, t)
                    variance(2, b - 1, b - 1)
                turned_x(b + 1, 0)
                turned_x(b + 1, 1)
                if later:
                    ranks(b - 1)
                add_x(b, par, 2)
                proj_sum(b + 1, 0)
                if later:
                    low_ranks(b - 1)
                proj_lo(b + 1, 1 - par, 0)
                proj_sum(b + 1, 1)
                if later:
                    high_ranks(b - 1)
                x1_stats(b, par, 2)
                proj_lo(b + 1, 1 - par, 1)
                for m in range(2, NPROJ):
                    proj_lo(b + 1, 1 - par, m)
                p_lo(b, 3, 0, ps_a)
                p_lo(b, 3, 1, ps_b)
                max_of(b + 1, 0, 0)
                max_of(b + 1, 0, 1)
                p_lo(b, 3, 2, ps_a)
                max_of(b + 1, 0, 2)
                if later:
                    ln3_scale(b - 1)
                    gates(b - 1)
                    add_table(b - 1)

            batches(dve, body)
            par = LAST % 2
            ln2(LAST, LAST, par, first_tiles)
            add_x(LAST, par, QT - 1)
            x1_stats(LAST, par, QT - 1)
            variance(1, LAST + 1, LAST, last_tile)
            h_stats(LAST, 0)
            ln2(LAST + 1, LAST, par, last_tile)
            for t in range(1, QT):
                h_stats(LAST, t)
            variance(2, LAST, LAST)
            top_expert(LAST)
            ln3_scale(LAST)
            read_ranks(LAST)
            ranks(LAST)
            gates(LAST)
            low_ranks(LAST)
            high_ranks(LAST)
            put_ids(LAST)
            add_table(LAST - 1)

            step = [0]

            def link(ins):
                step[0] += 1
                ins.then_inc(meta_step, 1)
                dve.wait_ge(meta_step, step[0])

            dve.wait_ge(cnt_ps, 1)
            link(dve.tensor_copy(cnt[:], ps_cnt))
            link(dve.tensor_tensor(over[:], cnt[:, :, None].broadcast_to([P, E, MAXT]), thr[:], ALU.is_gt))
            add_table(LAST)
            dve.wait_ge(table_ok, B)
            link(dve.tensor_scalar(empty, table[:], 0.0, float(NO_TOKEN), ALU.is_equal, ALU.mult))
            dve.scalar_tensor_tensor(out=ids[:], in0=table[:], scalar=-1.0, in1=empty,
                                     op0=ALU.add, op1=ALU.add).then_inc(ids_ok, 1)
            link(dve.tensor_reduce(tl[:], over[:], AX.X, ALU.add))
            link(dve.tensor_scalar(tl1[:], tl[:], 1.0, None, ALU.max))
            link(dve.tensor_tensor(tlu[:], upto[:], tl1[:, None, :].broadcast_to([P, E, E]), ALU.mult))
            link(dve.tensor_reduce(ends[:], tlu[:], AX.X, ALU.add))
            link(dve.tensor_tensor(past[:], tile_j[:], ends[:, None, 0:E - 1].broadcast_to([P, META, E - 1]), ALU.is_ge))
            link(dve.tensor_tensor(past_t[:], past[:], tl1[:, None, 0:E - 1].broadcast_to([P, META, E - 1]), ALU.mult))
            dve.tensor_reduce(meta_f[:, 0], past[:], AX.X, ALU.add)
            link(dve.tensor_reduce(start_f[:], past_t[:], AX.X, ALU.add))
            link(dve.tensor_tensor(start_f[:], tile_j[:, :, 0], start_f[:], ALU.subtract))
            link(dve.tensor_scalar(start_f[:], start_f[:], float(HALVES), None, ALU.mult))
            link(dve.scalar_tensor_tensor(out=meta_f[:, 1], in0=meta_f[:, 0], scalar=float(RANKS), in1=start_f[:],
                                          op0=ALU.mult, op1=ALU.add))
            link(dve.tensor_scalar(meta_f[:, 1], meta_f[:, 1], float(E * RANKS - HALVES), None, ALU.min))
            dve.tensor_copy(meta[:], meta_f[:]).then_inc(meta_ok, 1)

            def expert_x(j, par):
                dve.wait_ge(xe_ok, DC * (j + 1))
                if some(FC // 2 * (j - 1)):
                    dve.wait_ge(mm1_ok, FC // 2 * (j - 1))
                dve.tensor_copy(xe_hi[par], xe).then_inc(xe_hi_ok, 1)
                dve.wait_ge(xe_hi_ok, j + 1)
                dve.tensor_tensor(xe_lo[par], xe, xe_hi[par].bitcast(F32), ALU.subtract).then_inc(xe_lo_ok, 1)

            expert_x(0, 0)

            def residual(j, par, k):
                dve.wait_ge(vec_in[par], vec_value(j, par))
                dve.wait_ge(gathered[par][k], 8 * (j - par) + 16)
                gate = g[par][:, k, GATE:GATE + 1]
                dve.tensor_copy(gate_sb[:, par, k:k + 1], gate)
                dve.scalar_tensor_tensor(out=y_b[:, k], in0=b2_all[par], scalar=gate, in1=g[par][:, k, REST:],
                                         op0=ALU.mult, op1=ALU.add).then_inc(resid_ok, 1)

            def store_tile(j, par, k):
                dve.wait_ge(mm2_ok, HALVES * j + k + 1)
                dve.wait_ge(resid_ok, HALVES * (j + 1))
                if some(16 * j):
                    dve.wait_ge(stored[k], 16 * j)
                gate = gate_sb[:, par, k:k + 1]
                dve.scalar_tensor_tensor(out=o_sb[:, k], in0=y_banks[k][:, D:], scalar=gate, in1=y_b[:, k],
                                         op0=ALU.mult, op1=ALU.add).then_inc(o_half, 1)
                dve.wait_ge(o_half, HALVES * j + k + 1)
                dve.scalar_tensor_tensor(out=o_sb[:, k], in0=y_banks[k][:, 0:D], scalar=gate, in1=o_sb[:, k],
                                         op0=ALU.mult, op1=ALU.add).then_inc(o_ok, 1)

            def tile_body(j, par):
                if not isinstance(j, int) or j > 0:
                    store_tile(j - 1, 1 - par, 1)
                    dve.wait_ge(w2_hi_ok, 2 * j)
                    dve.tensor_tensor(w2_lo[par][0], w2_raw[par][0], w2_hi[par][0].bitcast(F32),
                                      ALU.subtract).then_inc(w2_lo_v, 1)
                residual(j, par, 0)
                for n in range(FC // 2):
                    c = slice(2 * n, 2 * n + 2)
                    dve.wait_ge(h1_ok, FC * j + 2 * n + 2)
                    if n == 0 and some(HALVES * j):
                        dve.wait_ge(mm2_ok, HALVES * j)
                    dve.tensor_copy(h1_hi[:, c], h1[:, c]).then_inc(h1_hi_ok, 1)
                    dve.wait_ge(h1_hi_ok, FC // 2 * j + n + 1)
                    dve.tensor_tensor(h1_lo[:, c], h1[:, c], h1_hi[:, c].bitcast(F32), ALU.subtract).then_inc(h1_lo_ok, 1)
                dve.wait_ge(w1_hi_ok, 2 * (j + 1))
                dve.tensor_tensor(w1_lo[1 - par][:, 0], w1_raw[1 - par][0], w1_hi[1 - par][:, 0].bitcast(F32),
                                  ALU.subtract).then_inc(w1_lo_v, 1)
                residual(j, par, 1)
                expert_x(j + 1, 1 - par)
                store_tile(j, par, 0)

            tiles(dve, tile_body)
            store_tile(TILES - 1, (TILES - 1) % 2, 1)

        @block.tensor
        def _(pe):
            pe.wait_ge(made, 3)
            with pe.Fori(0, 12):
                for _ in range(4):
                    pe.matmul(ps_b[:, 0:P], ones[:], ones[:], start=True, stop=True)
            pe.wait_ge(made2, 3)

            def three(out_ap, ahi, alo, bhi, blo, first, last):
                pe.matmul(out_ap, ahi, bhi, start=first, stop=False)
                pe.matmul(out_ap, ahi, blo, start=False, stop=False)
                return pe.matmul(out_ap, alo, bhi, start=False, stop=last)

            def three_in_two(bank, ahi, alo, b_hl, first, last):
                def wide():
                    return pe.matmul(bank[:], ahi, b_hl.rearrange("p n d -> p (n d)"), start=first, stop=last)

                if first:
                    wide()
                ins = pe.matmul(bank[:, 0:D], alo, b_hl[:, 0], start=False, stop=False)
                return ins if first else wide()

            def turn_x(n, c):
                if c == 0:
                    if some(DC * (n - 1)):
                        pe.wait_ge(ht_ok, DC * (n - 1))
                elif not isinstance(n, int) or n > 1:
                    pe.wait_ge(rank_step.sem, rank_step.per * (n - 2) + 1)
                for t in range(QT):
                    pe.wait_ge(xn_ok, QT * n + t + 1)
                    ins = pe.transpose((ps_mb, ps_ma)[c][:, t * P:(t + 1) * P], xn[:, t, c * P:(c + 1) * P], ident[:])
                ins.then_inc(x_turned, 1)

            def project(n, m):
                name, c = QKV_ORDER[m][0], int(QKV_ORDER[m][1])
                bank = proj_bank[m]
                if m == 0:
                    pe.wait_ge(xt_lo_ok, DC * (n + 1))
                if m == 2:
                    if some(KB * (QT * n - 1)):
                        pe.wait_ge(pt_lo_ok, KB * (QT * n - 1))
                if m >= 4:
                    pe.wait_ge(v_sum_ok, 2 * n + m - 3)
                if name == "v":
                    for u in range(2):
                        t = 2 * c + u
                        for k in range(DC):
                            tokens = slice(t * P, (t + 1) * P)
                            ins = three(bank[:, u * D:(u + 1) * D], xt_hi[:, k, tokens], xt_lo[:, k, tokens],
                                        w_hi[:, 2, k], w_lo[:, 2, k], k == 0, k == DC - 1)
                else:
                    w = "qk".index(name)
                    for k in range(DC):
                        e = slice(c * P, (c + 1) * P)
                        ins = three(bank[:], w_hi[:, w, k, e], w_lo[:, w, k, e], xt_hi[:, k], xt_lo[:, k], k == 0, k == DC - 1)
                ins.then_inc(projected, 1)

            def score(b, par, t, n):
                if n == 0:
                    if some(QT * b + t):
                        pe.wait_ge(exp_done, QT * b + t)
                    if t == 0:
                        pe.wait_ge(proj_lo_ok, NPROJ * b + 4)
                        pe.wait_ge(ctx_lo_ok, NPIECE * b + 2)
                if n == KB - 1 and t == 0:
                    pe.wait_ge(proj_lo_ok, NPROJ * (b + 1))
                for k in range(DC):
                    q = q_hi[:, k, t * P:(t + 1) * P], q_lo[:, k, t * P:(t + 1) * P]
                    if n < KB - 1:
                        kk = k_hi[par][:, k, n * BANK:(n + 1) * BANK], k_lo[par][:, k, n * BANK:(n + 1) * BANK]
                    else:
                        kk = kn_hi[:, k], kn_lo[:, k]
                    ins = three(ps_s[:, n], *q, *kk, k == 0, k == DC - 1)
                ins.then_inc(scored, 1)

            def turn_p(b, t, n, bank):
                if n == 0:
                    pe.wait_ge(exp_done, QT * b + t + 1)
                    if some(KB * (QT * b + t)):
                        pe.wait_ge(pt_lo_ok, KB * (QT * b + t))
                    if t == QT - 1 and not is_last(b):
                        pe.wait_ge(proj_lo_ok, NPROJ * (b + 1) + 4)
                if n == KB - 1 and bank is ps_a:
                    pe.wait_ge(pt_lo_ok, KB * (QT * b + t) + 1)
                for u in range(GPB):
                    c = GPB * n + u
                    ins = pe.transpose(bank[:, u * P:(u + 1) * P], probs[:, c * P:(c + 1) * P], ident[:])
                ins.then_inc(p_turned, 1)

            def attend(b, par, t):
                if some(QT * b + t):
                    pe.wait_ge(x1_ok, QT * b + t)
                for c in range(KC):
                    if c % GPB == 0:
                        pe.wait_ge(pt_lo_ok, KB * (QT * b + t) + c // GPB + 1)
                    if t == 0 and c == 0:
                        pe.wait_ge(ctx_lo_ok, NPIECE * (b + 1))
                        pe.wait_ge(proj_lo_ok, NPROJ * (b + 1))
                    v = v_hl[par][:, c] if c < CC else vn_hl[par][:, c - CC]
                    ins = three_in_two(ps_pv, pt_hi[:, c], pt_lo[:, c], v, c == 0, c == KC - 1)
                ins.then_inc(pv_done, 1)

            def turn_h(b, c):
                bank = (ps_ma, ps_mb)[c]
                if c == 0:
                    pe.wait_ge(proj_lo_ok, NPROJ * no_more_than_b(b + 2))
                    pe.wait_ge(table_ok, b)
                for t in range(QT):
                    pe.wait_ge(h_ok, QT * b + t + 1)
                    ins = pe.transpose(bank[:, t * P:(t + 1) * P], h_sb[:, t, c * P:(c + 1) * P], ident[:])
                ins.then_inc(h_turned, 1)

            def turn_last_h(c):
                if c < DC:
                    for t in first_tiles:
                        pe.wait_ge(h_ok, QT * LAST + t + 1)
                        ins = pe.transpose((ps_ma, ps_mb)[c][:, t * P:(t + 1) * P],
                                           h_sb[:, t, c * P:(c + 1) * P], ident[:])
                else:
                    t = QT - 1
                    pe.wait_ge(h_ok, QT * LAST + t + 1)
                    for k in range(DC):
                        ins = pe.transpose(ps_h_last[:, k * P:(k + 1) * P], h_sb[:, t, k * P:(k + 1) * P], ident[:])
                ins.then_inc(h_turned, 1)

            def affinities(b, tiles=range(QT)):
                for t in tiles:
                    for k in range(DC):
                        ins = pe.matmul(aff_bank(b)[:, t * E:(t + 1) * E], ht[:, k, t * P:(t + 1) * P], cent_sb[:, k],
                                        start=(k == 0), stop=(k == DC - 1))
                if QT - 1 in tiles:
                    ins.then_inc(aff_ps, 1)

            def rank(b):
                pe.wait_ge(top_step.sem, top_step.done(b))
                pe.wait_ge(sum_step, 2 * b)
                pe.matmul(ps_rank, tri[:], hot[:].rearrange("p t e -> p (t e)"), start=True, stop=False)
                for t in range(QT - 1):
                    n = QT - 1 - t
                    pe.matmul(ps_rank[:, (t + 1) * E:QT * E].rearrange("p (n e) -> p n e", n=n), ones[:],
                              hot[:, t, None, :].broadcast_to([P, n, E]), start=False, stop=False)
                pe.matmul(ps_rank.rearrange("p (n e) -> p n e", n=QT), ones[:],
                          acc[:, None, :].broadcast_to([P, QT, E]), start=False, stop=True).then_inc(rank_ps, 1)

            def fill_table(b):
                pe.wait_ge(proj_lo_ok, NPROJ * no_more_than_b(b + 2))
                pe.wait_ge(lo_hot_ok, b + 1)
                pe.wait_ge(id_ok, b + 1)
                for t in range(QT):
                    pe.wait_ge(put_ok, QT * b + t + 1)
                    ins = pe.matmul(table_bank(b), lo_hot[:, t], put[:, t].rearrange("p e r -> p (e r)"),
                                    start=(t == 0), stop=(t == QT - 1))
                ins.then_inc(table_ps, 1)

            turn_x(0, 0)
            turn_x(0, 1)
            for m in range(NPROJ):
                if m % 2 == 0:
                    pe.wait_ge(w_lo_ok, m // 2 + 1)
                project(0, m)
            for n in range(KB):
                score(0, 0, 0, n)

            def body(b, par):
                later = not isinstance(b, int) or b > 0
                for t in range(1, QT):
                    turn_p(b, t - 1, 0, ps_a)
                    turn_p(b, t - 1, 1, ps_b)
                    score(b, par, t, 0)
                    if later and t == 2:
                        turn_h(b - 1, 0)
                        turn_h(b - 1, 1)
                    if later and t == 3:
                        rank(b - 1)
                    score(b, par, t, 1)
                    turn_p(b, t - 1, 2, ps_a)
                    score(b, par, t, 2)
                    if later and t == 2:
                        pe.wait_ge(ht_ok, DC * b)
                        affinities(b - 1)
                    if not is_last(b) and t == 3:
                        turn_x(b + 1, 0)
                        turn_x(b + 1, 1)
                    attend(b, par, t - 1)
                if not is_last(b):
                    for m in range(NPROJ):
                        project(b + 1, m)
                turn_p(b, 3, 0, ps_a)
                turn_p(b, 3, 1, ps_b)
                if not is_last(b):
                    score(b + 1, 1 - par, 0, 0)
                    score(b + 1, 1 - par, 0, 1)
                turn_p(b, 3, 2, ps_mb if is_last(b) else ps_a)
                if not is_last(b):
                    score(b + 1, 1 - par, 0, 2)
                    if later:
                        fill_table(b - 1)
                attend(b, par, 3)

            batches(pe, body)
            turn_last_h(0)
            turn_last_h(1)
            fill_table(LAST - 1)
            pe.wait_ge(ht_ok, DC * LAST + DC)
            affinities(LAST, first_tiles)
            turn_last_h(2)
            pe.wait_ge(ht_ok, DC * LAST + DC + 1)
            affinities(LAST, last_tile)
            rank(LAST)
            for t in range(QT):
                pe.matmul(ps_cnt, ones[:], hot[:, t], start=(t == 0), stop=False)
            pe.matmul(ps_cnt, ones[:], acc[:], start=False, stop=True).then_inc(cnt_ps, 1)
            fill_table(LAST)

            def turn_rows(j, par):
                for k in range(HALVES):
                    pe.wait_ge(gathered[par][k], 8 * (j - par) + 16)
                if some(DC * j):
                    pe.wait_ge(xe_ok, DC * j)
                for c in range(DC):
                    for k in range(HALVES):
                        ins = pe.transpose(ps_mb[:, c * TILE + k * P:c * TILE + (k + 1) * P],
                                           g[par][:, k, c * P:(c + 1) * P], ident[:])
                ins.then_inc(xe_turned, 1)

            turn_rows(0, 0)

            def tile_body(j, par):
                pe.wait_ge(xe_lo_ok, j + 1)
                pe.wait_ge(xe_hi_ok, j + 1)
                if some(2 * j):
                    pe.wait_ge(w1_hi_ok, 2 * j)
                if some(j):
                    pe.wait_ge(w1_lo_v, j)
                if some(j):
                    pe.wait_ge(w1_lo_p, j)
                if isinstance(j, int) and j == 0:
                    pe.wait_ge(ctx_lo_ok, NPIECE * (B + 1))
                for f in range(FC):
                    if f % 2 == 0:
                        if some(FC * (j - 1) + f + 2):
                            pe.wait_ge(h1_ok, FC * (j - 1) + f + 2)
                    fs = slice(f * P, (f + 1) * P)
                    for k in range(DC):
                        ins = three(h_bank(f // 2)[:, (f % 2) * TILE:(f % 2 + 1) * TILE], w1_hi[par][:, k, fs],
                                    w1_lo[par][:, k, fs], xe_hi[par][:, k], xe_lo[par][:, k], k == 0, k == DC - 1)
                    if f % 2:
                        ins.then_inc(mm1_ok, 1)
                turn_rows(j + 1, 1 - par)
                for k in range(HALVES):
                    ks = slice(k * P, (k + 1) * P)
                    if some(HALVES * (j - 1) + k + 1):
                        pe.wait_ge(o_ok, HALVES * (j - 1) + k + 1)
                    if k == 0:
                        if some(2 * j):
                            pe.wait_ge(w2_hi_ok, 2 * j)
                        if some(j):
                            pe.wait_ge(w2_lo_v, j)
                    for f in range(FC):
                        if k == 0 and f % 2 == 0:
                            pe.wait_ge(h1_lo_ok, FC // 2 * j + f // 2 + 1)
                            pe.wait_ge(h1_hi_ok, FC // 2 * j + f // 2 + 1)
                        if k == 0 and f == FC // 2:
                            if some(j):
                                pe.wait_ge(w2_lo_p, j)
                        part, c = divmod(f, FC // 2)
                        ins = three_in_two(y_banks[k], h1_hi[:, f, ks], h1_lo[:, f, ks], w2_hl[par][part][:, c],
                                           f == 0, f == FC - 1)
                    ins.then_inc(mm2_ok, 1)

            tiles(pe, tile_body)


def kernel(x, ctx_1024, L0_xattn_Wq, L0_xattn_bq, L0_xattn_Wk, L0_xattn_bk, L0_xattn_Wv, L0_xattn_bv,
           L0_ffn_centroids, L0_ffn_ln_g, L0_ffn_ln_b, L0_ffn_w1, L0_ffn_b1, L0_ffn_w2, L0_ffn_b2):
    import numpy as np
    import concourse.bacc as bacc
    from concourse import mybir as mb
    from concourse.bass_utils import run_bass_kernel_spmd

    def a(v):
        return np.asarray(v)

    def chunked(v):
        n, r, w = v.shape
        return v.reshape(n, r // P, P, w).transpose(0, 2, 1, 3).reshape(n, r, w)

    def columns(v):
        return a(v).reshape(E, -1, P).transpose(0, 2, 1)

    data = {
        "x": a(x),
        "keys_src": np.concatenate([a(ctx_1024).reshape(B, P, CC, D).transpose(0, 3, 2, 1).reshape(B, D, K_CTX),
                                    a(L0_ffn_w1).transpose(0, 2, 1)]),
        "vals_src": np.concatenate([a(ctx_1024), chunked(a(L0_ffn_w2).transpose(0, 2, 1))]),
        "wq": a(L0_xattn_Wq).T, "wk": a(L0_xattn_Wk).T, "wv": a(L0_xattn_Wv).T,
        "b_cols": np.stack([a(v).reshape(DC, P).T for v in (L0_xattn_bq, L0_xattn_bk)], axis=1), "bv": a(L0_xattn_bv),
        "cent": a(L0_ffn_centroids).T,
        "vecs": np.concatenate([columns(L0_ffn_ln_g), columns(L0_ffn_ln_b), columns(L0_ffn_b1)], axis=2),
        "b2": a(L0_ffn_b2),
    }
    nc = bacc.Bacc("TRN2", target_bir_lowering=False, num_devices=1)
    arrays, args = {}, []
    for name, v in data.items():
        v = np.ascontiguousarray(v)
        arrays[f"in_{name}"] = v
        args.append(nc.dram_tensor(f"in_{name}", v.shape, mb.dt.from_np(v.dtype), kind="ExternalInput").ap())
    args.append(nc.dram_tensor("out_0", (TOKENS, D), mb.dt.float32, kind="ExternalOutput").ap())
    xattn_experts(nc, *args)
    r = run_bass_kernel_spmd(nc, [arrays], core_ids=[0])
    return r.results[0]["out_0"].reshape(B, S, D)
```
